# Optimizing a Trainium2 kernel written in Bass

```python
import numpy as np
import jax
import jax.numpy as jnp

def _softmax(x, axis=-1):
    return jax.nn.softmax(x, axis=axis)

def _gelu(x):
    return jax.nn.gelu(x, approximate=True)

def _silu(x):
    return jax.nn.silu(x)

def _sigmoid(x):
    return jax.nn.sigmoid(x)

def _layernorm(x, axis=-1, eps=1e-05):
    m = jnp.mean(x, axis=axis, keepdims=True)
    v = jnp.var(x, axis=axis, keepdims=True)
    return (x - m) / jnp.sqrt(v + eps)

def _scatter_add(tgt, idx, src, axis=0):
    return tgt.at[idx].add(src)

def _segment_sum(src, seg, n):
    return jax.ops.segment_sum(src, seg, n)
kernel_name = 'mk_macaron_d4_jaxref_r8_7e680e'

def setup_inputs(seed: int=0):
    np.random.seed(seed)
    _w = jnp.asarray

    def _L0_attn_setup():
        import jax, jax.numpy as jnp
        import numpy as np
        import math
        B, S, DM, H = (4, 512, 128, 16)
        HD = DM // H
        key = jax.random.key(seed)
        ks = jax.random.split(key, 5)

        def xavier(k, shape):
            bound = math.sqrt(6.0 / (shape[0] + shape[1]))
            return jax.random.uniform(k, shape, jnp.float32, -bound, bound)
        return {'x': jax.random.normal(ks[0], (B, S, DM), jnp.float32), 'Wq': xavier(ks[1], (DM, DM)), 'Wk': xavier(ks[2], (DM, DM)), 'Wv': xavier(ks[3], (DM, DM)), 'Wfc': xavier(ks[4], (DM, DM))}
    _L0_attn_in = _L0_attn_setup()

    def _L0_ffn_setup():
        import jax, jax.numpy as jnp
        import numpy as np
        D = 128
        F = 512
        E = 8
        K = 2
        B, S = (4, 256)
        key = jax.random.key(seed)
        ks = jax.random.split(key, 6)
        scale_in = 1.0 / np.sqrt(D)
        scale_mid = 1.0 / np.sqrt(F)
        return {'x': jax.random.normal(ks[0], (B, S, D), dtype=jnp.float32), 'router_w': jax.random.normal(ks[1], (E, D), dtype=jnp.float32) * scale_in, 'w1': jax.random.normal(ks[2], (E, F, D), dtype=jnp.float32) * scale_in, 'b1': jax.random.normal(ks[3], (E, F), dtype=jnp.float32) * 0.01, 'w2': jax.random.normal(ks[4], (E, D, F), dtype=jnp.float32) * scale_mid, 'b2': jax.random.normal(ks[5], (E, D), dtype=jnp.float32) * 0.01}
    _L0_ffn_in = _L0_ffn_setup()

    def _L1_attn_setup():
        import jax, jax.numpy as jnp
        import numpy as np
        H = 16

        def rotate_half(x):
            x1 = x[..., ::2]
            x2 = x[..., 1::2]
            return jnp.concatenate((-x2, x1), axis=-1)

        def rope_cache(n, hd):
            freqs = 10000.0 ** (-jnp.arange(0, hd, 2, dtype=jnp.float32) / hd)
            angles = jnp.arange(n, dtype=jnp.float32)[:, None] * freqs
            sin = jnp.sin(angles)
            cos = jnp.cos(angles)
            sin = jnp.stack([sin, sin], axis=-1).reshape(n, hd)
            cos = jnp.stack([cos, cos], axis=-1).reshape(n, hd)
            return (sin, cos)
        key = jax.random.key(seed)
        k1, k2, k3 = jax.random.split(key, 3)
        dim, inner = (128, 128)
        x = jax.random.normal(k1, (2, 256, dim), dtype=jnp.float32)
        w_qkv = jax.random.normal(k2, (dim, 3 * inner), dtype=jnp.float32) * dim ** (-0.5)
        w_out = jax.random.normal(k3, (inner, dim), dtype=jnp.float32) * inner ** (-0.5)
        b_out = jnp.zeros((dim,), dtype=jnp.float32)
        return {'x': x, 'w_qkv': w_qkv, 'w_out': w_out, 'b_out': b_out}
    _L1_attn_in = _L1_attn_setup()

    def _L1_ffn_setup():
        import jax, jax.numpy as jnp
        import numpy as np
        DIM = 128
        HIDDEN = 384
        SCALE = 1.0 / 127.0

        def _dequant(w_int, dtype):
            return w_int.astype(dtype) * jnp.asarray(SCALE, dtype)
        key = jax.random.key(seed)
        k_x, k_g, k_u, k_d = jax.random.split(key, 4)
        x = jax.random.normal(k_x, (4, 256, DIM), dtype=jnp.float32)
        w_gate = jax.random.randint(k_g, (HIDDEN, DIM), -127, 128, dtype=jnp.int32)
        w_up = jax.random.randint(k_u, (HIDDEN, DIM), -127, 128, dtype=jnp.int32)
        w_down = jax.random.randint(k_d, (DIM, HIDDEN), -127, 128, dtype=jnp.int32)
        return {'x': x, 'w_gate': w_gate, 'w_up': w_up, 'w_down': w_down}
    _L1_ffn_in = _L1_ffn_setup()

    def _L2_attn_setup():
        import jax, jax.numpy as jnp
        import numpy as np
        EPS = 1e-06
        key = jax.random.key(seed)
        ks = jax.random.split(key, 8)
        B, S, D = (4, 256, 128)
        sc = 1.0 / np.sqrt(D)
        return {'x_seq': jax.random.normal(ks[0], (B, S, D), jnp.float32), 'Wq': jax.random.normal(ks[1], (D, D), jnp.float32) * sc, 'bq': jax.random.normal(ks[2], (D,), jnp.float32) * 0.01, 'Wk': jax.random.normal(ks[3], (D, D), jnp.float32) * sc, 'bk': jax.random.normal(ks[4], (D,), jnp.float32) * 0.01, 'Wv': jax.random.normal(ks[5], (D, D), jnp.float32) * sc, 'bv': jax.random.normal(ks[6], (D,), jnp.float32) * 0.01, 'gamma': jnp.float32(0.9)}
    _L2_attn_in = _L2_attn_setup()

    def _L2_ffn_setup():
        import jax, jax.numpy as jnp
        import numpy as np
        NEG_INF = -1e+30

        def _moe_forward(x, router_w, router_b, w1, b1, w2, b2, top_k=2):
            B, S, D = x.shape
            E = router_w.shape[1]
            logits = jnp.einsum('bsd,de->bse', x, router_w) + router_b
            top_vals, top_idx = jax.lax.top_k(logits, top_k)
            keep = jax.nn.one_hot(top_idx, E, dtype=logits.dtype).sum(-2) > 0
            sparse_logits = jnp.where(keep, logits, NEG_INF)
            gating = jax.nn.softmax(sparse_logits, axis=-1)
            xf = x.reshape(-1, D)
            gf = gating.reshape(-1, E)
            h = jax.nn.relu(jnp.einsum('td,edh->eth', xf, w1) + b1[:, None, :])
            y = jnp.einsum('eth,ehd->etd', h, w2) + b2[:, None, :]
            out = jnp.einsum('etd,te->td', y, gf)
            return out.reshape(B, S, D)
        key = jax.random.key(seed)
        ks = jax.random.split(key, 5)
        B, S, D, E, H = (2, 256, 128, 8, 512)
        scale = 0.02
        return {'x': jax.random.normal(ks[0], (B, S, D), dtype=jnp.float32), 'router_w': jax.random.normal(ks[1], (D, E), dtype=jnp.float32) * scale, 'router_b': jnp.zeros((E,), dtype=jnp.float32), 'w1': jax.random.normal(ks[2], (E, D, H), dtype=jnp.float32) * scale, 'b1': jnp.zeros((E, H), dtype=jnp.float32), 'w2': jax.random.normal(ks[3], (E, H, D), dtype=jnp.float32) * scale, 'b2': jnp.zeros((E, D), dtype=jnp.float32)}
    _L2_ffn_in = _L2_ffn_setup()

    def _L3_attn_setup():
        import jax, jax.numpy as jnp
        import numpy as np
        D_MODEL = 128
        N_HEAD = 16
        HEAD_SIZE = D_MODEL // N_HEAD
        LAYER_ID = 12
        N_LAYER = 24
        HEAD_SIZE_DIVISOR = 8
        TM_DIM = 32
        TD_DIM = 64
        B, T = (4, 128)
        EPS = 1e-05 * HEAD_SIZE_DIVISOR ** 2

        def _wkv6(r, k, v, w, u):
            Bc, Tc, H, K = r.shape
            wdec = jnp.exp(-jnp.exp(w))

            def step(S, inp):
                r_t, k_t, v_t, wd_t = inp
                kv = k_t[:, :, :, None] * v_t[:, :, None, :]
                y = jnp.einsum('bhk,bhkj->bhj', r_t, S + u[None, :, :, None] * kv)
                S = S * wd_t[:, :, :, None] + kv
                return (S, y)
            S0 = jnp.zeros((Bc, H, K, K), r.dtype)
            xs = (jnp.swapaxes(r, 0, 1), jnp.swapaxes(k, 0, 1), jnp.swapaxes(v, 0, 1), jnp.swapaxes(wdec, 0, 1))
            _, ys = jax.lax.scan(step, S0, xs)
            return jnp.swapaxes(ys, 0, 1).reshape(Bc, Tc, H * K)
        key = jax.random.key(seed)
        ks = jax.random.split(key, 12)
        C = D_MODEL
        r0 = LAYER_ID / (N_LAYER - 1)
        r1 = 1.0 - LAYER_ID / N_LAYER
        ddd = np.arange(C, dtype=np.float64) / C
        time_maa_x = (1.0 - ddd ** r1).astype(np.float32)
        time_maa_w = (1.0 - ddd ** r1).astype(np.float32)
        time_maa_k = (1.0 - ddd ** r1).astype(np.float32)
        time_maa_v = (1.0 - (ddd ** r1 + 0.3 * r0)).astype(np.float32)
        time_maa_r = (1.0 - ddd ** (0.5 * r1)).astype(np.float32)
        time_maa_g = (1.0 - ddd ** (0.5 * r1)).astype(np.float32)
        n = np.arange(C, dtype=np.float64)
        time_decay = (-6.0 + 5.0 * (n / (C - 1)) ** (0.7 + 1.3 * r0)).astype(np.float32)
        zig = ((n + 1) % 3 - 1) * 0.1
        time_faaaa = (r0 * (1 - n / (C - 1)) + zig).astype(np.float32).reshape(N_HEAD, HEAD_SIZE)
        s = 1.0 / np.sqrt(C)
        inp = {'x': jax.random.normal(ks[0], (B, T, C), jnp.float32), 'time_maa_x': jnp.asarray(time_maa_x), 'time_maa_w': jnp.asarray(time_maa_w), 'time_maa_k': jnp.asarray(time_maa_k), 'time_maa_v': jnp.asarray(time_maa_v), 'time_maa_r': jnp.asarray(time_maa_r), 'time_maa_g': jnp.asarray(time_maa_g), 'time_maa_w1': jax.random.uniform(ks[1], (C, TM_DIM * 5), jnp.float32, -0.01, 0.01), 'time_maa_w2': jax.random.uniform(ks[2], (5, TM_DIM, C), jnp.float32, -0.01, 0.01), 'time_decay': jnp.asarray(time_decay), 'time_decay_w1': jax.random.uniform(ks[3], (C, TD_DIM), jnp.float32, -0.01, 0.01), 'time_decay_w2': jax.random.uniform(ks[4], (TD_DIM, C), jnp.float32, -0.01, 0.01), 'time_faaaa': jnp.asarray(time_faaaa), 'W_r': jax.random.normal(ks[5], (C, C), jnp.float32) * s, 'W_k': jax.random.normal(ks[6], (C, C), jnp.float32) * s, 'W_v': jax.random.normal(ks[7], (C, C), jnp.float32) * s, 'W_g': jax.random.normal(ks[8], (C, C), jnp.float32) * s, 'W_o': jax.random.normal(ks[9], (C, C), jnp.float32) * s, 'ln_gamma': jnp.ones((C,), jnp.float32), 'ln_beta': jnp.zeros((C,), jnp.float32)}
        return inp
    _L3_attn_in = _L3_attn_setup()

    def _L3_ffn_setup():
        import jax, jax.numpy as jnp
        import numpy as np
        DIM = 128

        def _reference_tuple_inner(x, W_r, W_k, W_v, mu_r, mu_k):
            B, T, C = x.shape
            x_prev = jnp.concatenate([jnp.zeros((B, 1, C), x.dtype), x[:, :-1, :]], axis=1)
            xr = mu_r * x + (1.0 - mu_r) * x_prev
            xk = mu_k * x + (1.0 - mu_k) * x_prev
            r = jax.nn.sigmoid(jnp.einsum('btc,dc->btd', xr, W_r))
            k = jnp.einsum('btc,dc->btd', xk, W_k)
            k_act = jnp.square(jax.nn.relu(k))
            out = r * jnp.einsum('btc,dc->btd', k_act, W_v)
            new_state = x[:, -1, :]
            return (out, new_state)
        key = jax.random.key(seed)
        ks = jax.random.split(key, 6)
        B, T, C = (8, 256, DIM)
        x = jax.random.normal(ks[0], (B, T, C), dtype=jnp.float32)
        s = 1.0 / np.sqrt(C)
        W_r = jax.random.uniform(ks[1], (C, C), jnp.float32, -s, s)
        W_k = jax.random.uniform(ks[2], (C, C), jnp.float32, -s, s)
        W_v = jax.random.uniform(ks[3], (C, C), jnp.float32, -s, s)
        mu_r = jax.random.uniform(ks[4], (C,), jnp.float32)
        mu_k = jax.random.uniform(ks[5], (C,), jnp.float32)
        return {'x': x, 'W_r': W_r, 'W_k': W_k, 'W_v': W_v, 'mu_r': mu_r, 'mu_k': mu_k}
    _L3_ffn_in = _L3_ffn_setup()
    _d = {'L0_attn_x': _L0_attn_in['x'], 'L0_attn_Wq': _L0_attn_in['Wq'], 'L0_attn_Wk': _L0_attn_in['Wk'], 'L0_attn_Wv': _L0_attn_in['Wv'], 'L0_attn_Wfc': _L0_attn_in['Wfc'], 'L0_ffn_router_w': _L0_ffn_in['router_w'], 'L0_ffn_w1': _L0_ffn_in['w1'], 'L0_ffn_b1': _L0_ffn_in['b1'], 'L0_ffn_w2': _L0_ffn_in['w2'], 'L0_ffn_b2': _L0_ffn_in['b2'], 'L1_attn_w_qkv': _L1_attn_in['w_qkv'], 'L1_attn_w_out': _L1_attn_in['w_out'], 'L1_attn_b_out': _L1_attn_in['b_out'], 'L1_ffn_w_gate': _L1_ffn_in['w_gate'], 'L1_ffn_w_up': _L1_ffn_in['w_up'], 'L1_ffn_w_down': _L1_ffn_in['w_down'], 'L2_attn_Wq': _L2_attn_in['Wq'], 'L2_attn_bq': _L2_attn_in['bq'], 'L2_attn_Wk': _L2_attn_in['Wk'], 'L2_attn_bk': _L2_attn_in['bk'], 'L2_attn_Wv': _L2_attn_in['Wv'], 'L2_attn_bv': _L2_attn_in['bv'], 'L2_attn_gamma': _L2_attn_in['gamma'], 'L2_ffn_router_w': _L2_ffn_in['router_w'], 'L2_ffn_router_b': _L2_ffn_in['router_b'], 'L2_ffn_w1': _L2_ffn_in['w1'], 'L2_ffn_b1': _L2_ffn_in['b1'], 'L2_ffn_w2': _L2_ffn_in['w2'], 'L2_ffn_b2': _L2_ffn_in['b2'], 'L3_attn_time_maa_x': _L3_attn_in['time_maa_x'], 'L3_attn_time_maa_w': _L3_attn_in['time_maa_w'], 'L3_attn_time_maa_k': _L3_attn_in['time_maa_k'], 'L3_attn_time_maa_v': _L3_attn_in['time_maa_v'], 'L3_attn_time_maa_r': _L3_attn_in['time_maa_r'], 'L3_attn_time_maa_g': _L3_attn_in['time_maa_g'], 'L3_attn_time_maa_w1': _L3_attn_in['time_maa_w1'], 'L3_attn_time_maa_w2': _L3_attn_in['time_maa_w2'], 'L3_attn_time_decay': _L3_attn_in['time_decay'], 'L3_attn_time_decay_w1': _L3_attn_in['time_decay_w1'], 'L3_attn_time_decay_w2': _L3_attn_in['time_decay_w2'], 'L3_attn_time_faaaa': _L3_attn_in['time_faaaa'], 'L3_attn_W_r': _L3_attn_in['W_r'], 'L3_attn_W_k': _L3_attn_in['W_k'], 'L3_attn_W_v': _L3_attn_in['W_v'], 'L3_attn_W_g': _L3_attn_in['W_g'], 'L3_attn_W_o': _L3_attn_in['W_o'], 'L3_attn_ln_gamma': _L3_attn_in['ln_gamma'], 'L3_attn_ln_beta': _L3_attn_in['ln_beta'], 'L3_ffn_W_r': _L3_ffn_in['W_r'], 'L3_ffn_W_k': _L3_ffn_in['W_k'], 'L3_ffn_W_v': _L3_ffn_in['W_v'], 'L3_ffn_mu_r': _L3_ffn_in['mu_r'], 'L3_ffn_mu_k': _L3_ffn_in['mu_k']}
    _x0 = _d['L0_attn_x']
    _d['L0_attn_x'] = jax.random.normal(jax.random.fold_in(jax.random.key(seed), 1), (4, 1024, 128), dtype=_x0.dtype)
    del _x0
    return _d

def reference(L0_attn_x, L0_attn_Wq, L0_attn_Wk, L0_attn_Wv, L0_attn_Wfc, L0_ffn_router_w, L0_ffn_w1, L0_ffn_b1, L0_ffn_w2, L0_ffn_b2, L1_attn_w_qkv, L1_attn_w_out, L1_attn_b_out, L1_ffn_w_gate, L1_ffn_w_up, L1_ffn_w_down, L2_attn_Wq, L2_attn_bq, L2_attn_Wk, L2_attn_bk, L2_attn_Wv, L2_attn_bv, L2_attn_gamma, L2_ffn_router_w, L2_ffn_router_b, L2_ffn_w1, L2_ffn_b1, L2_ffn_w2, L2_ffn_b2, L3_attn_time_maa_x, L3_attn_time_maa_w, L3_attn_time_maa_k, L3_attn_time_maa_v, L3_attn_time_maa_r, L3_attn_time_maa_g, L3_attn_time_maa_w1, L3_attn_time_maa_w2, L3_attn_time_decay, L3_attn_time_decay_w1, L3_attn_time_decay_w2, L3_attn_time_faaaa, L3_attn_W_r, L3_attn_W_k, L3_attn_W_v, L3_attn_W_g, L3_attn_W_o, L3_attn_ln_gamma, L3_attn_ln_beta, L3_ffn_W_r, L3_ffn_W_k, L3_ffn_W_v, L3_ffn_mu_r, L3_ffn_mu_k):

    def _L0_attn_ref(x, Wq, Wk, Wv, Wfc):
        import jax, jax.numpy as jnp
        import numpy as np
        import math
        B, S, DM, H = (4, 512, 128, 16)
        HD = DM // H
        b, s, dm = x.shape
        h, hd = (H, dm // H)
        Q = (x @ Wq.T).reshape(b, s, h, hd)
        K = (x @ Wk.T).reshape(b, s, h, hd)
        V = (x @ Wv.T).reshape(b, s, h, hd)
        scores = jnp.einsum('bshd,bstd->bsht', Q, K) / math.sqrt(hd)
        attn = jax.nn.softmax(scores, axis=-1)
        out = jnp.einsum('bsht,bstd->bshd', attn, V).reshape(b, s, dm)
        return out @ Wfc.T

    def _L0_ffn_ref(x, router_w, w1, b1, w2, b2):
        import jax, jax.numpy as jnp
        import numpy as np
        D = 128
        F = 512
        E = 8
        K = 2
        B, S = (4, 256)
        orig_shape = x.shape
        xf = x.reshape(-1, D)
        logits = jnp.einsum('td,ed->te', xf, router_w)
        top_vals, top_idx = jax.lax.top_k(logits, K)
        probs = jax.nn.softmax(top_vals, axis=-1)
        out = jnp.zeros_like(xf)
        for e in range(E):
            w = jnp.sum(jnp.where(top_idx == e, probs, 0.0), axis=-1)
            h = jax.nn.gelu(jnp.einsum('td,fd->tf', xf, w1[e]) + b1[e], approximate=False)
            y = jnp.einsum('tf,df->td', h, w2[e]) + b2[e]
            out = out + w[:, None] * y
        return out.reshape(orig_shape)

    def _L1_attn_ref(x, w_qkv, w_out, b_out):
        import jax, jax.numpy as jnp
        import numpy as np
        H = 16

        def rotate_half(x):
            x1 = x[..., ::2]
            x2 = x[..., 1::2]
            return jnp.concatenate((-x2, x1), axis=-1)

        def rope_cache(n, hd):
            freqs = 10000.0 ** (-jnp.arange(0, hd, 2, dtype=jnp.float32) / hd)
            angles = jnp.arange(n, dtype=jnp.float32)[:, None] * freqs
            sin = jnp.sin(angles)
            cos = jnp.cos(angles)
            sin = jnp.stack([sin, sin], axis=-1).reshape(n, hd)
            cos = jnp.stack([cos, cos], axis=-1).reshape(n, hd)
            return (sin, cos)
        b, n, dim = x.shape
        qkv = x @ w_qkv
        q, k, v = jnp.split(qkv, 3, axis=-1)
        heads = lambda t: t.reshape(b, n, H, -1).transpose(0, 2, 1, 3)
        q, k, v = (heads(q), heads(k), heads(v))
        hd = q.shape[-1]
        sin, cos = rope_cache(n, hd)
        q = q * cos + rotate_half(q) * sin
        k = k * cos + rotate_half(k) * sin
        scale = hd ** (-0.5)
        dots = jnp.einsum('bhid,bhjd->bhij', q, k) * scale
        attn = jax.nn.softmax(dots, axis=-1)
        out = jnp.einsum('bhij,bhjd->bhid', attn, v)
        out = out.transpose(0, 2, 1, 3).reshape(b, n, H * hd)
        return out @ w_out + b_out

    def _L1_ffn_ref(x, w_gate, w_up, w_down):
        import jax, jax.numpy as jnp
        import numpy as np
        DIM = 128
        HIDDEN = 384
        SCALE = 1.0 / 127.0

        def _dequant(w_int, dtype):
            return w_int.astype(dtype) * jnp.asarray(SCALE, dtype)
        wg = _dequant(w_gate, x.dtype)
        wu = _dequant(w_up, x.dtype)
        wd = _dequant(w_down, x.dtype)
        gate = jnp.einsum('bsd,hd->bsh', x, wg)
        up = jnp.einsum('bsd,hd->bsh', x, wu)
        h = jax.nn.silu(gate) * up
        return jnp.einsum('bsh,dh->bsd', h, wd)

    def _L2_attn_ref(x_seq, Wq, bq, Wk, bk, Wv, bv, gamma):
        import jax, jax.numpy as jnp
        import numpy as np
        EPS = 1e-06
        B, S, D = x_seq.shape
        q = jax.nn.relu(jnp.einsum('bsd,ed->bse', x_seq, Wq) + bq)
        k = jax.nn.relu(jnp.einsum('bsd,ed->bse', x_seq, Wk) + bk)
        v = jnp.einsum('bsd,ed->bse', x_seq, Wv) + bv

        def step(carry, qkv):
            s, z = carry
            q_t, k_t, v_t = qkv
            s = gamma * s + jnp.einsum('bi,bj->bij', k_t, v_t)
            z = gamma * z + k_t
            num = jnp.einsum('bi,bij->bj', q_t, s)
            denom = jnp.sum(q_t * z, axis=-1, keepdims=True) + EPS
            return ((s, z), num / denom)
        s0 = jnp.zeros((B, D, D), x_seq.dtype)
        z0 = jnp.zeros((B, D), x_seq.dtype)
        qkv = (jnp.swapaxes(q, 0, 1), jnp.swapaxes(k, 0, 1), jnp.swapaxes(v, 0, 1))
        _, ys = jax.lax.scan(step, (s0, z0), qkv)
        return jnp.swapaxes(ys, 0, 1)

    def _L2_ffn_ref(x, router_w, router_b, w1, b1, w2, b2):
        import jax, jax.numpy as jnp
        import numpy as np
        NEG_INF = -1e+30

        def _moe_forward(x, router_w, router_b, w1, b1, w2, b2, top_k=2):
            B, S, D = x.shape
            E = router_w.shape[1]
            logits = jnp.einsum('bsd,de->bse', x, router_w) + router_b
            top_vals, top_idx = jax.lax.top_k(logits, top_k)
            keep = jax.nn.one_hot(top_idx, E, dtype=logits.dtype).sum(-2) > 0
            sparse_logits = jnp.where(keep, logits, NEG_INF)
            gating = jax.nn.softmax(sparse_logits, axis=-1)
            xf = x.reshape(-1, D)
            gf = gating.reshape(-1, E)
            h = jax.nn.relu(jnp.einsum('td,edh->eth', xf, w1) + b1[:, None, :])
            y = jnp.einsum('eth,ehd->etd', h, w2) + b2[:, None, :]
            out = jnp.einsum('etd,te->td', y, gf)
            return out.reshape(B, S, D)
        return _moe_forward(x, router_w, router_b, w1, b1, w2, b2, top_k=2)

    def _L3_attn_ref(x, time_maa_x, time_maa_w, time_maa_k, time_maa_v, time_maa_r, time_maa_g, time_maa_w1, time_maa_w2, time_decay, time_decay_w1, time_decay_w2, time_faaaa, W_r, W_k, W_v, W_g, W_o, ln_gamma, ln_beta):
        import jax, jax.numpy as jnp
        import numpy as np
        D_MODEL = 128
        N_HEAD = 16
        HEAD_SIZE = D_MODEL // N_HEAD
        LAYER_ID = 12
        N_LAYER = 24
        HEAD_SIZE_DIVISOR = 8
        TM_DIM = 32
        TD_DIM = 64
        B, T = (4, 128)
        EPS = 1e-05 * HEAD_SIZE_DIVISOR ** 2

        def _wkv6(r, k, v, w, u):
            Bc, Tc, H, K = r.shape
            wdec = jnp.exp(-jnp.exp(w))

            def step(S, inp):
                r_t, k_t, v_t, wd_t = inp
                kv = k_t[:, :, :, None] * v_t[:, :, None, :]
                y = jnp.einsum('bhk,bhkj->bhj', r_t, S + u[None, :, :, None] * kv)
                S = S * wd_t[:, :, :, None] + kv
                return (S, y)
            S0 = jnp.zeros((Bc, H, K, K), r.dtype)
            xs = (jnp.swapaxes(r, 0, 1), jnp.swapaxes(k, 0, 1), jnp.swapaxes(v, 0, 1), jnp.swapaxes(wdec, 0, 1))
            _, ys = jax.lax.scan(step, S0, xs)
            return jnp.swapaxes(ys, 0, 1).reshape(Bc, Tc, H * K)
        Bc, Tc, C = x.shape
        H, K = (N_HEAD, HEAD_SIZE)
        xs = jnp.pad(x, ((0, 0), (1, 0), (0, 0)))[:, :-1]
        xx = xs - x
        xxx = x + xx * time_maa_x
        m = jnp.tanh(xxx @ time_maa_w1).reshape(Bc, Tc, 5, TM_DIM)
        m = jnp.einsum('btfe,fec->fbtc', m, time_maa_w2)
        mw, mk, mv, mr, mg = (m[0], m[1], m[2], m[3], m[4])
        xw = x + xx * (time_maa_w + mw)
        xk = x + xx * (time_maa_k + mk)
        xv = x + xx * (time_maa_v + mv)
        xr = x + xx * (time_maa_r + mr)
        xg = x + xx * (time_maa_g + mg)
        r = xr @ W_r
        k = xk @ W_k
        v = xv @ W_v
        g = jax.nn.silu(xg @ W_g)
        w = time_decay + jnp.tanh(xw @ time_decay_w1) @ time_decay_w2
        y = _wkv6(r.reshape(Bc, Tc, H, K), k.reshape(Bc, Tc, H, K), v.reshape(Bc, Tc, H, K), w.reshape(Bc, Tc, H, K), time_faaaa)
        yg = y.reshape(Bc, Tc, H, K)
        mu = jnp.mean(yg, axis=-1, keepdims=True)
        var = jnp.mean((yg - mu) ** 2, axis=-1, keepdims=True)
        yn = ((yg - mu) / jnp.sqrt(var + EPS)).reshape(Bc, Tc, C)
        yn = yn * ln_gamma + ln_beta
        return yn * g @ W_o

    def _L3_ffn_ref(x, W_r, W_k, W_v, mu_r, mu_k):
        import jax, jax.numpy as jnp
        import numpy as np
        DIM = 128

        def _reference_tuple_inner(x, W_r, W_k, W_v, mu_r, mu_k):
            B, T, C = x.shape
            x_prev = jnp.concatenate([jnp.zeros((B, 1, C), x.dtype), x[:, :-1, :]], axis=1)
            xr = mu_r * x + (1.0 - mu_r) * x_prev
            xk = mu_k * x + (1.0 - mu_k) * x_prev
            r = jax.nn.sigmoid(jnp.einsum('btc,dc->btd', xr, W_r))
            k = jnp.einsum('btc,dc->btd', xk, W_k)
            k_act = jnp.square(jax.nn.relu(k))
            out = r * jnp.einsum('btc,dc->btd', k_act, W_v)
            new_state = x[:, -1, :]
            return (out, new_state)
        return _reference_tuple_inner(x, W_r, W_k, W_v, mu_r, mu_k)[0]
    x = L0_attn_x
    x = x + 0.5 * _L0_ffn_ref(_layernorm(x, axis=-1), L0_ffn_router_w, L0_ffn_w1, L0_ffn_b1, L0_ffn_w2, L0_ffn_b2)
    x = x + _L0_attn_ref(_layernorm(x, axis=-1), L0_attn_Wq, L0_attn_Wk, L0_attn_Wv, L0_attn_Wfc)
    x = x + 0.5 * _L0_ffn_ref(_layernorm(x, axis=-1), L0_ffn_router_w, L0_ffn_w1, L0_ffn_b1, L0_ffn_w2, L0_ffn_b2)
    x = x + 0.5 * _L1_ffn_ref(_layernorm(x, axis=-1), L1_ffn_w_gate, L1_ffn_w_up, L1_ffn_w_down)
    x = x + _L1_attn_ref(_layernorm(x, axis=-1), L1_attn_w_qkv, L1_attn_w_out, L1_attn_b_out)
    x = x + 0.5 * _L1_ffn_ref(_layernorm(x, axis=-1), L1_ffn_w_gate, L1_ffn_w_up, L1_ffn_w_down)
    x = x + 0.5 * _L2_ffn_ref(_layernorm(x, axis=-1), L2_ffn_router_w, L2_ffn_router_b, L2_ffn_w1, L2_ffn_b1, L2_ffn_w2, L2_ffn_b2)
    x = x + _L2_attn_ref(_layernorm(x, axis=-1), L2_attn_Wq, L2_attn_bq, L2_attn_Wk, L2_attn_bk, L2_attn_Wv, L2_attn_bv, L2_attn_gamma)
    x = x + 0.5 * _L2_ffn_ref(_layernorm(x, axis=-1), L2_ffn_router_w, L2_ffn_router_b, L2_ffn_w1, L2_ffn_b1, L2_ffn_w2, L2_ffn_b2)
    x = x + 0.5 * _L3_ffn_ref(_layernorm(x, axis=-1), L3_ffn_W_r, L3_ffn_W_k, L3_ffn_W_v, L3_ffn_mu_r, L3_ffn_mu_k)
    x = x + _L3_attn_ref(_layernorm(x, axis=-1), L3_attn_time_maa_x, L3_attn_time_maa_w, L3_attn_time_maa_k, L3_attn_time_maa_v, L3_attn_time_maa_r, L3_attn_time_maa_g, L3_attn_time_maa_w1, L3_attn_time_maa_w2, L3_attn_time_decay, L3_attn_time_decay_w1, L3_attn_time_decay_w2, L3_attn_time_faaaa, L3_attn_W_r, L3_attn_W_k, L3_attn_W_v, L3_attn_W_g, L3_attn_W_o, L3_attn_ln_gamma, L3_attn_ln_beta)
    x = x + 0.5 * _L3_ffn_ref(_layernorm(x, axis=-1), L3_ffn_W_r, L3_ffn_W_k, L3_ffn_W_v, L3_ffn_mu_r, L3_ffn_mu_k)
    return x

_drawn_inputs = setup_inputs


def setup_inputs(seed=0):
    import zlib

    import numpy as np

    out = dict(_drawn_inputs(seed))
    spreads = {'L1_attn_b_out': (0.0, 2.0),
     'L2_ffn_router_b': (0.0, 2.0),
     'L2_ffn_b1': (0.0, 2.0),
     'L2_ffn_b2': (0.0, 2.0),
     'L3_attn_ln_gamma': (1.0, 0.6),
     'L3_attn_ln_beta': (0.0, 0.8)}
    factors = {'L0_ffn_b1': 3.831,
     'L0_ffn_b2': 3.083,
     'L1_attn_w_qkv': 8.0,
     'L1_attn_w_out': 8.0,
     'L2_attn_Wq': 64.0,
     'L2_attn_bq': 64.0,
     'L2_attn_Wk': 64.0,
     'L2_attn_bk': 64.0,
     'L2_attn_Wv': 36.192,
     'L2_attn_bv': 64.0,
     'L2_ffn_router_w': 8.0,
     'L2_ffn_w1': 8.0,
     'L2_ffn_w2': 8.0,
     'L3_attn_time_maa_x': 8.0,
     'L3_attn_time_maa_w': 64.0,
     'L3_attn_time_maa_k': 8.0,
     'L3_attn_time_maa_v': 8.0,
     'L3_attn_time_maa_r': 8.0,
     'L3_attn_time_maa_g': 8.0,
     'L3_attn_time_maa_w1': 8.0,
     'L3_attn_time_maa_w2': 8.0,
     'L3_attn_time_decay': 64.0,
     'L3_attn_time_decay_w1': 64.0,
     'L3_attn_time_decay_w2': 64.0,
     'L3_attn_time_faaaa': 40.296,
     'L3_attn_W_r': 8.0,
     'L3_attn_W_k': 8.0,
     'L3_attn_W_v': 8.0,
     'L3_attn_W_g': 8.0,
     'L3_attn_W_o': 8.0,
     'L3_ffn_W_r': 8.0,
     'L3_ffn_W_k': 8.0,
     'L3_ffn_W_v': 8.0,
     'L3_ffn_mu_r': 8.0,
     'L3_ffn_mu_k': 8.0}
    for name, (base, spread) in spreads.items():
        noise = np.random.default_rng([zlib.crc32(name.encode()), seed]).standard_normal(out[name].shape)
        drawn = base * np.exp(spread * noise) if base else spread * noise
        out[name] = jnp.asarray(drawn.astype(out[name].dtype))
    for name, factor in factors.items():
        out[name] = (out[name] * factor).astype(out[name].dtype)
    return out
```

```python
from contextlib import ExitStack

import numpy as np
import concourse.bass as bass
import concourse.mybir as mybir

F32 = mybir.dt.float32
BF16 = mybir.dt.bfloat16
I32 = mybir.dt.int32
ALU = mybir.AluOpType
ACT = mybir.ActivationFunctionType
AX = mybir.AxisListType

P = 128
B, S, D = 4, 1024, 128
T = B * S
CH = 512
TPC = CH // P
NCH = T // CH
E = 8
FF = 512
FC = FF // P
LN_EPS = 1e-5
STAGES = 12


def need(eng, sem, count):
    if isinstance(count, int) and count <= 0:
        return
    eng.wait_ge(sem, count)


def bcast(ap, shape):
    return ap.broadcast_to(shape)


def per_token(ap, n):
    return bcast(ap[:].rearrange("p (t a) -> p t a", a=1), [P, TPC, n])


class Chain:

    def __init__(self, eng, sem, start):
        self.eng, self.sem, self.count = eng, sem, start

    def then(self, ins):
        ins.then_inc(self.sem, 1)
        self.count = self.count + 1

    def wait(self):
        need(self.eng, self.sem, self.count)


class Scope(ExitStack):

    def __init__(self, nc):
        super().__init__()
        self.nc, self.sems = nc, []
        self.callback(self.clear)

    def clear(self):
        if self.sems:
            self.nc.clear_and_free_semaphores(self.sems)
            self.nc.all_engine_barrier()

    def sem(self, name):
        self.sems.append(self.nc.alloc_semaphore(name))
        return self.sems[-1]


class Net:
    pass


def open_net(nc, st, ins):
    n = Net()
    n.ins = ins

    def sb(name, shape, dt=F32):
        return st.enter_context(nc.sbuf_tensor(name, shape, dt))

    n.x = sb("x", [P, T])
    n.xnT = [sb("xnT0", [P, T]), sb("xnT1", [P, T])]
    n.gates = sb("gates", [P, T // P * E])
    n.ident = sb("ident", [P, P])
    n.rev = sb("rev", [P, E])
    n.nhalf = sb("nhalf", [P, TPC])
    n.euler = sb("euler", [P, TPC])
    n.bank = [st.enter_context(nc.psum_tensor(f"bank{i}", [P, 512], F32)) for i in range(8)]
    n.L0_b1, n.L2_b1 = sb("L0_b1", [P, E * FC]), sb("L2_b1", [P, E * FC])
    n.L0_b2, n.L2_b2 = sb("L0_b2", [E, D]), sb("L2_b2", [E, D])
    n.L0_rw, n.L2_rw = sb("L0_rw", [P, E]), sb("L2_rw", [P, E])
    n.L2_rb = sb("L2_rb", [P, E])
    n.L0_wqkv = sb("L0_wqkv", [P, 3 * D])
    n.L1_wqk = sb("L1_wqk", [P, 4, D])
    n.L1_wv, n.L1_wout, n.L1_bout = sb("L1_wv", [P, D]), sb("L1_wout", [P, D]), sb("L1_bout", [P, D])
    n.L0_wfc = sb("L0_wfc", [P, D])
    n.L2_wq, n.L2_wkv = sb("L2_wq", [P, D]), sb("L2_wkv", [P, 2 * D])
    n.L2_bq, n.L2_bk = sb("L2_bq", [P, 1]), sb("L2_bk", [P, 1])
    n.L2_bk_row, n.L2_bv_row = sb("L2_bk_row", [P, D]), sb("L2_bv_row", [P, D])
    n.L3_fr, n.L3_fk, n.L3_fv = sb("L3_fr", [P, D]), sb("L3_fk", [P, D]), sb("L3_fv", [P, D])
    n.L3_mu_r, n.L3_mu_k = sb("L3_mu_r", [P, 1]), sb("L3_mu_k", [P, 1])
    n.L1_wg_int, n.L1_wg = sb("L1_wg_int", [P, HID], I32), sb("L1_wg", [P, HID])
    n.L1_wu_int, n.L1_wu = sb("L1_wu_int", [P, HID], I32), sb("L1_wu", [P, HID])
    n.L1_wd_int, n.L1_wd = sb("L1_wd_int", [P, HC, D], I32), sb("L1_wd", [P, HC, D])
    return n



class Norm:

    def __init__(self, nc, st, net, tag, dest, route, across=False, settled=False):
        self.across, self.settled = across, settled

        def sb(name, shape):
            return st.enter_context(nc.sbuf_tensor(f"{tag}_norm_{name}", shape, F32))

        def sem(name):
            return st.sem(f"{tag}_norm_{name}")
        self.nc, self.net, self.dest, self.route = nc, net, dest, route
        self.xc = sb("xc", [P, TPC, D])
        self.sq = sb("sq", [P, TPC, D])
        self.mean = sb("mean", [P, TPC])
        self.var = sb("var", [P, TPC])
        self.ve = sb("var_eps", [P, TPC])
        self.rstd = sb("rstd", [P, TPC])
        self.xn = sb("xn", [P, CH])
        self.xs = sb("xs", [P, CH])
        self.tbank, self.rbank = net.bank[6], net.bank[7]
        self.var_ready, self.rstd_ready, self.xn_ready = sem("var_ready"), sem("rstd_ready"), sem("xn_ready")
        self.turned, self.kept, self.x_whole = sem("turned"), sem("kept"), sem("x_whole")
        self.own = sem("dve_norm_step")
        self.steps = 5
        if route:
            self.steps += 19
            self.lg, self.eq, self.one1, self.one2, self.lg2, self.g1 = (
                sb(k, [P, TPC, E]) for k in ("logits", "equal", "one_hot1", "one_hot2", "logits2", "gates1"))
            self.m1, self.m2, self.f1, self.f2, self.gap, self.ex, self.den, self.p1, self.p2 = (
                sb(k, [P, TPC]) for k in ("top1", "top2", "rank1", "rank2", "gap", "exp", "den", "p1", "p2"))
            self.gs = sb("gs", [P, TPC, E])
            self.gT = sb("gT", [E, CH])
            (self.logits_ready, self.gap_ready, self.grown, self.gates_ready, self.gates_turned, self.gates_kept,
             self.bias_ready, self.bias_added) = (sem(k) for k in (
                 "logits_ready", "gap_ready", "grown", "gates_ready", "gates_turned", "gates_kept", "bias_ready",
                 "bias_added"))

    def view(self, t, c, width=D):
        if self.across:
            return t[:].rearrange("p (b n d) -> p b n d", b=B, d=width)[:, :, bass.ds(c, 1), :].rearrange(
                "p b n d -> p b (n d)")
        return t[:, bass.ds(c * TPC * width, TPC * width)].rearrange("p (t d) -> p t d", d=width)

    def stats(self, dve, c):
        nc = self.nc
        x = self.view(self.net.x, c)
        own = Chain(dve, self.own, c * self.steps)
        own.then(nc.vector.tensor_scalar(self.sq[:], x, 1.0 / D, None, ALU.mult))
        own.wait()
        own.then(nc.vector.tensor_reduce(self.mean[:], self.sq[:], AX.X, ALU.add))
        own.wait()
        own.then(nc.vector.tensor_tensor(self.xc[:], x, per_token(self.mean, D), ALU.subtract))
        own.wait()
        own.then(nc.vector.tensor_tensor(self.sq[:], self.xc[:], self.xc[:], ALU.mult))
        own.wait()
        own.then(nc.vector.tensor_reduce(self.var[:], self.sq[:], AX.X, ALU.add))
        own.wait()
        if not self.settled:
            need(dve, self.rstd_ready, c)
        nc.vector.tensor_scalar(self.ve[:], self.var[:], 1.0 / D, LN_EPS, ALU.mult, ALU.add).then_inc(self.var_ready, 1)

    def apply(self, dve, c):
        nc = self.nc
        dve.wait_ge(self.rstd_ready, c + 1)
        if not self.settled:
            need(dve, self.turned, c)
        nc.vector.tensor_tensor(self.xn[:].rearrange("p (t d) -> p t d", d=D), self.xc[:], per_token(self.rstd, D),
                                ALU.mult).then_inc(self.xn_ready, 1)

    def pick(self, dve, c, bias):
        nc = self.nc
        own = Chain(dve, self.own, c * self.steps + 5)
        rev = bcast(self.net.rev[:].rearrange("p (a e) -> p a e", a=1), [P, TPC, E])

        def first_of(logits, top, found, one):
            own.then(nc.vector.tensor_reduce(top[:], logits[:], AX.X, ALU.max))
            own.wait()
            own.then(nc.vector.tensor_tensor(self.eq[:], logits[:], per_token(top, E), ALU.is_equal))
            own.wait()
            own.then(nc.vector.tensor_tensor(self.eq[:], self.eq[:], rev, ALU.mult))
            own.wait()
            own.then(nc.vector.tensor_reduce(found[:], self.eq[:], AX.X, ALU.max))
            own.wait()
            own.then(nc.vector.tensor_tensor(one[:], rev, per_token(found, E), ALU.is_equal))
            own.wait()
        dve.wait_ge(self.logits_ready, c + 1)
        src = self.rbank[:, 0:TPC * E].rearrange("p (t e) -> p t e", e=E)
        if bias is None:
            own.then(nc.vector.tensor_copy(self.lg[:], src))
        else:
            b = bcast(bias[:].rearrange("p (a e) -> p a e", a=1), [P, TPC, E])
            own.then(nc.vector.tensor_tensor(self.lg[:], src, b, ALU.add))
        own.wait()
        first_of(self.lg, self.m1, self.f1, self.one1)
        own.then(nc.vector.scalar_tensor_tensor(self.lg2[:], self.one1[:], -1e30, self.lg[:], ALU.mult, ALU.add))
        own.wait()
        first_of(self.lg2, self.m2, self.f2, self.one2)
        need(dve, self.grown, c)
        nc.vector.tensor_tensor(self.gap[:], self.m2[:], self.m1[:], ALU.subtract).then_inc(self.gap_ready, 1)

    def weigh(self, dve, c):
        nc = self.nc
        own = Chain(dve, self.own, c * self.steps + 17)
        dve.wait_ge(self.grown, c + 1)
        own.then(nc.vector.tensor_scalar(self.den[:], self.ex[:], 1.0, None, ALU.add))
        own.wait()
        own.then(nc.vector.reciprocal(self.p1[:], self.den[:]))
        own.wait()
        own.then(nc.vector.tensor_tensor(self.p2[:], self.ex[:], self.p1[:], ALU.mult))
        own.then(nc.vector.tensor_tensor(self.g1[:], self.one1[:], per_token(self.p1, E), ALU.mult))
        own.wait()
        own.then(nc.vector.tensor_tensor(self.lg2[:], self.one2[:], per_token(self.p2, E), ALU.mult))
        own.wait()
        own.then(nc.vector.tensor_tensor(self.g1[:], self.g1[:], self.lg2[:], ALU.add))
        own.wait()
        need(dve, self.gates_turned, c)
        nc.vector.tensor_scalar(self.gs[:], self.g1[:], 0.5, None, ALU.mult).then_inc(self.gates_ready, 1)
        own.then(nc.vector.tensor_scalar(self.view(self.net.gates, c, E), self.g1[:], 0.5, None, ALU.mult))
        own.wait()

    def add_bias(self, dve, c):
        x = self.view(self.net.x, c)
        dve.wait_ge(self.bias_ready, c + 1)
        bias = self.rbank[:].rearrange("p (t d) -> p t d", d=D)
        self.nc.vector.tensor_tensor(x, x, bias, ALU.add).then_inc(self.bias_added, 1)

    def rstd_pow(self, pool, c):
        pool.wait_ge(self.var_ready, c + 1)
        need(pool, self.xn_ready, c)
        self.nc.gpsimd.tensor_tensor(self.rstd[:], self.ve[:], self.net.nhalf[:], ALU.pow).then_inc(self.rstd_ready, 1)

    def grow(self, pool, c):
        pool.wait_ge(self.gap_ready, c + 1)
        need(pool, self.gates_ready, c)
        self.nc.gpsimd.tensor_tensor(self.ex[:], self.net.euler[:], self.gap[:], ALU.pow).then_inc(self.grown, 1)

    def turn(self, pe, c):
        pe.wait_ge(self.xn_ready, c + 1)
        if not self.settled:
            need(pe, self.kept, c)
        for i in range(TPC):
            s = slice(i * P, (i + 1) * P)
            ins = self.nc.tensor.transpose(self.tbank[:, s], self.xn[:, s], self.net.ident[:])
        ins.then_inc(self.turned, 1)

    def logits(self, pe, c, rw):
        pe.wait_ge(self.kept, c + 1)
        need(pe, self.bias_added, c)
        for i in range(TPC):
            ins = self.nc.tensor.matmul(self.rbank[:, i * E:(i + 1) * E], self.xs[:, i * P:(i + 1) * P], rw[:],
                                        start=True, stop=True)
        ins.then_inc(self.logits_ready, 1)

    def turn_g(self, pe, c):
        pe.wait_ge(self.gates_ready, c + 1)
        for i in range(TPC):
            ins = self.nc.tensor.transpose(self.rbank[0:E, i * P:(i + 1) * P], self.gs[:, i, :], self.net.ident[:])
        ins.then_inc(self.gates_turned, 1)

    def bias(self, pe, c, b2):
        pe.wait_ge(self.gates_kept, c + 1)
        for i in range(TPC):
            s = slice(i * P, (i + 1) * P)
            ins = self.nc.tensor.matmul(self.rbank[:, s], self.gT[:, s], b2[:], start=True, stop=True)
        ins.then_inc(self.bias_ready, 1)

    def keep(self, act, c):
        act.wait_ge(self.turned, c + 1)
        if self.route:
            need(act, self.logits_ready, c)
        self.nc.scalar.activation(self.xs[:], self.tbank[:], ACT.Copy)
        self.nc.scalar.activation(self.view(self.dest, c), self.tbank[:].rearrange("p (t d) -> p t d", d=D),
                                  ACT.Copy).then_inc(self.kept, 1)

    def keep_g(self, act, c):
        act.wait_ge(self.gates_turned, c + 1)
        need(act, self.bias_ready, c)
        self.nc.scalar.activation(self.gT[:], self.rbank[0:E, :], ACT.Copy).then_inc(self.gates_kept, 1)

    def all_dve(self, dve, c, route_bias=None):
        self.stats(dve, c)
        self.apply(dve, c)
        if self.route:
            self.pick(dve, c, route_bias)
            self.weigh(dve, c)
            self.add_bias(dve, c)

    def all_pe(self, pe, c, rw=None, b2=None):
        self.turn(pe, c)
        if self.route:
            self.logits(pe, c, rw)
            self.turn_g(pe, c)
            self.bias(pe, c, b2)

    def all_act(self, act, c):
        self.keep(act, c)
        if self.route:
            self.keep_g(act, c)

    def all_pool(self, pool, c):
        self.rstd_pow(pool, c)
        if self.route:
            self.grow(pool, c)


def rounds(eng, body, tail=None, count=NCH):
    body(0)
    with eng.Fori(1, count - 1) as c:
        body(c)
    body(count - 1)
    if tail:
        tail(count - 1)


def is_last(c, count=NCH):
    return isinstance(c, int) and c == count - 1


def is_first(c):
    return isinstance(c, int) and c == 0


class Router:

    def __init__(self, rw=None, rb=None, b2=None):
        self.rw, self.rb, self.b2 = rw, rb, b2



def load_stage(nc, net, router):
    ins = net.ins
    with Scope(nc) as st:
        norm = Norm(nc, st, net, "ln0", net.xnT[0], True)
        x_loaded = st.sem("x_loaded")
        w_loaded = st.sem("weights_loaded")
        set_up = st.sem("constants_set")
        small = [(net.ident, ins["ident"]), (net.rev, ins["rev"]), (net.L0_rw, ins["L0_rw"]),
                 (net.L2_rw, ins["L2_rw"]), (net.L0_b1, ins["L0_b1"]), (net.L2_b1, ins["L2_b1"]),
                 (net.L0_b2, ins["L0_b2"]), (net.L2_b2, ins["L2_b2"]), (net.L0_wqkv, ins["L0_wqkv"]),
                 (net.L0_wfc, ins["L0_wfc"]), (net.L1_wg_int, ins["L1_wg"]), (net.L1_wu_int, ins["L1_wu"]),
                 (net.L1_wd_int, ins["L1_wd"]), (net.L1_wqk, ins["L1_wqk"]), (net.L1_wv, ins["L1_wv"]),
                 (net.L1_wout, ins["L1_wout"])]
        small += [(net.L2_wq, ins["L2_wq"]), (net.L2_wkv, ins["L2_wkv"]), (net.L2_bq, ins["L2_bq"]),
                  (net.L2_bk, ins["L2_bk"]), (net.L3_fr, ins["L3_fr"]), (net.L3_fk, ins["L3_fk"]),
                  (net.L3_fv, ins["L3_fv"]), (net.L3_mu_r, ins["L3_mu_r"]), (net.L3_mu_k, ins["L3_mu_k"])]
        rows = [(net.L2_rb, ins["L2_rb"]), (net.L1_bout, ins["L1_bout"]),
                (net.L2_bk_row, ins["L2_bk_row"]), (net.L2_bv_row, ins["L2_bv_row"])]
        big = [(net.w1, ins["L0_w1"]), (net.w2, ins["L0_w2"])]
        block = st.enter_context(nc.Block())

        @block.sync
        def _(sp):
            src = ins["x"].rearrange("(t p) d -> p t d", p=P)
            dst = net.x[:].rearrange("p (t d) -> p t d", d=D)
            for c in range(NCH):
                sp.dma_start(dst[:, c * TPC:(c + 1) * TPC], src[:, c * TPC:(c + 1) * TPC]).then_inc(x_loaded, 16)
            sp.wait_ge(x_loaded, 16 * NCH)
            sp.wait_ge(w_loaded, 16 * (len(small) + len(big) + len(rows)))

        @block.scalar
        def _(act):
            for dst, src in small:
                act.dma_start(dst[:], src).then_inc(w_loaded, 16)
            for dst, src in rows:
                act.dma_start(dst[:], src.partition_broadcast(P)).then_inc(w_loaded, 16)
            for dst, src in big:
                act.dma_start(dst[:], src).then_inc(w_loaded, 16)
            rounds(act, lambda c: norm.all_act(act, c))

        @block.gpsimd
        def _(pool):
            nc.gpsimd.memset(net.nhalf[:], -0.5)
            nc.gpsimd.memset(net.euler[:], float(np.e)).then_inc(set_up, 1)
            pool.wait_ge(set_up, 1)
            rounds(pool, lambda c: norm.all_pool(pool, c))

        @block.tensor
        def _(pe):
            pe.wait_ge(w_loaded, 16 * (len(small) + len(big) + len(rows)))
            rounds(pe, lambda c: norm.all_pe(pe, c, router.rw, router.b2))

        @block.vector
        def _(dve):
            dve.wait_ge(w_loaded, 16 * (len(small) + len(big) + len(rows)))
            dve.wait_ge(x_loaded, 16 * NCH)
            for w_int, w in ((net.L1_wg_int, net.L1_wg), (net.L1_wu_int, net.L1_wu), (net.L1_wd_int, net.L1_wd)):
                nc.vector.tensor_scalar(w[:], w_int[:], QSCALE, None, ALU.mult)
            rounds(dve, lambda c: norm.all_dve(dve, c, router.rb))



def moe_stage(nc, net, tag, layer, func, src, dest, router):
    w1, b1, w2 = net.w1, net.L0_b1 if layer == "L0" else net.L2_b1, net.w2
    with Scope(nc) as st:
        norm = Norm(nc, st, net, tag, dest, router is not None)
        router = router or Router()
        hs = st.enter_context(nc.sbuf_tensor(f"{tag}_hs", [P, 2, FC, CH], F32))
        hid_ready, hid_used, y_ready, y_added = (st.sem(f"{tag}_{k}")
                                                 for k in ("hid_ready", "hid_used", "y_ready", "y_added"))
        hbank, ybank = net.bank[0:4], net.bank[4:6]
        block = st.enter_context(nc.Block())

        def over_chunks(eng, slot, tail):
            for e in range(E):
                slot(0, e, False)
            with eng.Fori(1, NCH) as c:
                for e in range(E):
                    slot(c, e, True)
            tail(NCH - 1)

        @block.tensor
        def _(pe):
            def hidden(c, e):
                for f in range(FC):
                    need(pe, hid_used, (c * E + e - 1) * FC + f + 1)
                    nc.tensor.matmul(hbank[f][:], w1[:, e, f * P:(f + 1) * P], src[:, bass.ds(c * CH, CH)],
                                     start=True, stop=True).then_inc(hid_ready, 1)

            def down(c, e):
                pe.wait_ge(hid_used, (c * E + e + 1) * FC)
                need(pe, y_added, c * E + e - 1)
                for i in range(TPC):
                    for f in range(FC):
                        ins = nc.tensor.matmul(ybank[e % 2][:, i * P:(i + 1) * P], hs[:, e % 2, f, i * P:(i + 1) * P],
                                               w2[:, e, f, :], start=(f == 0), stop=(f == FC - 1))
                ins.then_inc(y_ready, 1)

            def slot(c, e, before):
                hidden(c, e)
                if e > 0:
                    down(c, e - 1)
                elif before:
                    down(c - 1, E - 1)
                if before and e == 2:
                    norm.turn(pe, c - 1)
                if before and norm.route:
                    if e == 3:
                        norm.logits(pe, c - 1, router.rw)
                    if e == 5:
                        norm.turn_g(pe, c - 1)
                    if e == 6:
                        norm.bias(pe, c - 1, router.b2)

            def tail(c):
                down(c, E - 1)
                norm.all_pe(pe, c, router.rw, router.b2)
            over_chunks(pe, slot, tail)

        @block.scalar
        def _(act):
            def slot(c, e, before):
                need(act, y_ready, c * E + e - 1)
                for f in range(FC):
                    act.wait_ge(hid_ready, (c * E + e) * FC + f + 1)
                    nc.scalar.activation(hs[:, e % 2, f, :], hbank[f][:], func,
                                         bias=b1[:, e * FC + f:e * FC + f + 1]).then_inc(hid_used, 1)
                if before and e == 2:
                    norm.keep(act, c - 1)
                if before and e == 5 and norm.route:
                    norm.keep_g(act, c - 1)
            over_chunks(act, slot, lambda c: norm.all_act(act, c))

        @block.gpsimd
        def _(pool):
            rounds(pool, lambda c: norm.all_pool(pool, c))

        @block.vector
        def _(dve):
            def add(c, e):
                dve.wait_ge(y_ready, c * E + e + 1)
                need(dve, y_added, c * E + e)
                for i in range(TPC):
                    xt = net.x[:, bass.ds(c * CH + i * P, P)]
                    ins = nc.vector.scalar_tensor_tensor(xt, ybank[e % 2][:, i * P:(i + 1) * P],
                                                         net.gates[:, bass.ds((c * TPC + i) * E + e, 1)], xt,
                                                         ALU.mult, ALU.add)
                ins.then_inc(y_added, 1)

            def slot(c, e, before):
                if e > 0:
                    add(c, e - 1)
                elif before:
                    add(c - 1, E - 1)
                    dve.wait_ge(y_added, c * E)
                    norm.stats(dve, c - 1)
                if before and e == 1:
                    norm.apply(dve, c - 1)
                if before and norm.route:
                    if e == 4:
                        norm.pick(dve, c - 1, router.rb)
                    if e == 5:
                        norm.weigh(dve, c - 1)
                    if e == 7:
                        norm.add_bias(dve, c - 1)

            def tail(c):
                add(c, E - 1)
                dve.wait_ge(y_added, (c + 1) * E)
                norm.all_dve(dve, c, router.rb)
            over_chunks(dve, slot, tail)



H = 16
HD = D // H


class Part:

    def __init__(self, nc, st, tag):
        self.nc, self.st, self.tag = nc, st, tag

    def sb(self, name, shape, dt=F32):
        return self.st.enter_context(self.nc.sbuf_tensor(f"{self.tag}_{name}", shape, dt))

    def sem(self, name):
        return self.st.sem(f"{self.tag}_{name}")


def head_mix_stage(nc, net, tag, src, dest, router):
    with Scope(nc) as st:
        norm = Norm(nc, st, net, tag, dest, True)
        part = Part(nc, st, tag)
        xa = part.sb("xa", [P, CH])
        qkv = part.sb("qkv", [P, TPC, 3 * D])
        prod = part.sb("prod", [P, H * H * HD])
        logit = part.sb("logit", [P, 2, H * H])
        prob = part.sb("prob", [P, 2, H * H])
        top, den, rden = part.sb("top", [P, H]), part.sb("den", [P, H]), part.sb("rden", [P, H])
        mix = part.sb("mix", [P, D])
        mixed_tiles = part.sb("mixed", [P, CH])
        mixT = part.sb("mixT", [P, CH])
        xa_ready, qkv_ready, qkv_kept, logit_ready, exp_ready, mixed, own, mix_turned, mixT_kept, y_ready, y_added = (
            part.sem(k) for k in ("xa_ready", "qkv_ready", "qkv_kept", "logit_ready", "exp_ready", "tile_mixed",
                                  "dve_step", "mix_turned", "mixT_kept", "y_ready", "y_added"))
        wqkv, wfc = net.L0_wqkv, net.L0_wfc
        block = st.enter_context(nc.Block())

        @block.tensor
        def _(pe):
            def qkv_of(c):
                pe.wait_ge(xa_ready, c + 1)
                for i in range(TPC):
                    need(pe, qkv_kept, (c - 1) * TPC + i + 1)
                    nc.tensor.matmul(net.bank[i][:, 0:3 * D], xa[:, i * P:(i + 1) * P], wqkv[:],
                                     start=True, stop=True).then_inc(qkv_ready, 1)

            def project(c):
                pe.wait_ge(mixed, (c + 1) * TPC)
                need(pe, mixT_kept, c)
                for i in range(TPC):
                    s = slice(i * P, (i + 1) * P)
                    ins = nc.tensor.transpose(net.bank[4][:, s], mixed_tiles[:, s], net.ident[:])
                ins.then_inc(mix_turned, 1)
                pe.wait_ge(mixT_kept, c + 1)
                need(pe, y_added, c)
                for i in range(TPC):
                    s = slice(i * P, (i + 1) * P)
                    ins = nc.tensor.matmul(net.bank[5][:, s], mixT[:, s], wfc[:], start=True, stop=True)
                ins.then_inc(y_ready, 1)

            def body(c):
                if is_first(c):
                    qkv_of(0)
                else:
                    project(c - 1)
                    norm.turn(pe, c - 1)
                    norm.logits(pe, c - 1, router.rw)
                if not is_last(c):
                    qkv_of(c + 1)
                if not is_first(c):
                    norm.turn_g(pe, c - 1)
                    norm.bias(pe, c - 1, router.b2)

            def tail(c):
                project(c)
                norm.all_pe(pe, c, router.rw, router.b2)
            rounds(pe, body, tail)

        @block.scalar
        def _(act):
            def keep(c, i):
                act.wait_ge(qkv_ready, c * TPC + i + 1)
                need(act, mixed, (c - 1) * TPC + i + 1)
                nc.scalar.activation(qkv[:, i, :], net.bank[i][:, 0:3 * D], ACT.Copy).then_inc(qkv_kept, 1)

            def exp(c, i):
                need(act, mixed, c * TPC + i - 1)
                act.wait_ge(logit_ready, c * TPC + i + 1)
                nc.scalar.activation(prob[:, i % 2, :], logit[:, i % 2, :], ACT.Exp,
                                     scale=HD ** -0.5).then_inc(exp_ready, 1)

            def keep_mix(c):
                need(act, y_ready, c)
                act.wait_ge(mix_turned, c + 1)
                nc.scalar.activation(mixT[:], net.bank[4][:], ACT.Copy).then_inc(mixT_kept, 1)

            def body(c):
                before, after = not is_first(c), not is_last(c)
                if not before:
                    for i in range(TPC):
                        keep(0, i)
                exp(c, 0)
                if before:
                    keep_mix(c - 1)
                exp(c, 1)
                if before:
                    norm.keep(act, c - 1)
                exp(c, 2)
                if after:
                    keep(c + 1, 0)
                exp(c, 3)
                if after:
                    keep(c + 1, 1)
                if before:
                    norm.keep_g(act, c - 1)
                if after:
                    keep(c + 1, 2)
                    keep(c + 1, 3)

            def tail(c):
                keep_mix(c)
                norm.all_act(act, c)
            rounds(act, body, tail)

        @block.gpsimd
        def _(pool):
            rounds(pool, lambda c: norm.all_pool(pool, c))

        @block.vector
        def _(dve):
            def heads(ap):
                return ap.rearrange("p (h d) -> p h d", d=HD)

            def per_head(ap, n):
                return bcast(ap[:].rearrange("p (h a) -> p h a", a=1), [P, H, n])

            def fetch(c):
                need(dve, qkv_ready, c * TPC)
                nc.vector.tensor_scalar(xa[:], src[:, bass.ds(c * CH, CH)], 1.0, None, ALU.mult).then_inc(xa_ready, 1)

            def score(chain, c, i):
                q, k = heads(qkv[:, i, 0:D]), heads(qkv[:, i, D:2 * D])
                p4 = prod[:].rearrange("p (h t d) -> p h t d", t=H, d=HD)
                lg = logit[:, i % 2, :].rearrange("p (h t) -> p h t", t=H)
                dve.wait_ge(qkv_kept, c * TPC + i + 1)
                chain.then(nc.vector.tensor_tensor(
                    p4, bcast(q.rearrange("p h (a d) -> p h a d", a=1), [P, H, H, HD]),
                    bcast(k.rearrange("p (a t) d -> p a t d", a=1), [P, H, H, HD]), ALU.mult))
                need(dve, exp_ready, c * TPC + i - 1)
                chain.wait()
                chain.then(nc.vector.tensor_reduce(lg, p4, AX.X, ALU.add))
                chain.wait()
                chain.then(nc.vector.tensor_reduce(top[:], lg, AX.X, ALU.max))
                chain.wait()
                nc.vector.tensor_tensor(lg, lg, per_head(top, H), ALU.subtract).then_inc(logit_ready, 1)

            def gather(chain, c, i):
                v = qkv[:, i, 2 * D:3 * D].rearrange("p (t d) -> p d t", d=HD)
                pr = prob[:, i % 2, :].rearrange("p (h t) -> p h t", t=H)
                p4 = prod[:].rearrange("p (h d t) -> p h d t", t=H, d=HD)
                dve.wait_ge(exp_ready, c * TPC + i + 1)
                nc.vector.tensor_reduce(den[:], pr, AX.X, ALU.add)
                chain.then(nc.vector.tensor_tensor(
                    p4, bcast(pr.rearrange("p h (a t) -> p h a t", a=1), [P, H, HD, H]),
                    bcast(v.rearrange("p (a d) t -> p a d t", a=1), [P, H, HD, H]), ALU.mult))
                chain.wait()
                nc.vector.reciprocal(rden[:], den[:])
                chain.then(nc.vector.tensor_reduce(heads(mix[:]), p4, AX.X, ALU.add))
                need(dve, mix_turned, c)
                chain.wait()
                nc.vector.tensor_tensor(heads(mixed_tiles[:, i * P:(i + 1) * P]), heads(mix[:]), per_head(rden, HD),
                                        ALU.mult).then_inc(mixed, 1)

            def add(c):
                x = net.x[:, bass.ds(c * CH, CH)]
                dve.wait_ge(y_ready, c + 1)
                nc.vector.tensor_tensor(x, x, net.bank[5][:], ALU.add).then_inc(y_added, 1)
                dve.wait_ge(y_added, c + 1)

            def body(c):
                before = not is_first(c)
                chain = Chain(dve, own, c * TPC * 5)
                if not before:
                    fetch(0)
                score(chain, c, 0)
                if not is_last(c):
                    fetch(c + 1)
                if before:
                    add(c - 1)
                    norm.stats(dve, c - 1)
                score(chain, c, 1)
                gather(chain, c, 0)
                if before:
                    norm.apply(dve, c - 1)
                score(chain, c, 2)
                gather(chain, c, 1)
                if before:
                    norm.pick(dve, c - 1, router.rb)
                    norm.weigh(dve, c - 1)
                score(chain, c, 3)
                gather(chain, c, 2)
                gather(chain, c, 3)
                if before:
                    norm.add_bias(dve, c - 1)

            def tail(c):
                add(c)
                norm.all_dve(dve, c, router.rb)
            rounds(dve, body, tail)



HID = 384
HC = HID // P
QSCALE = float(np.float32(1.0 / 127.0))


def swiglu_stage(nc, net, tag, src, dest, router):
    with Scope(nc) as st:
        norm = Norm(nc, st, net, tag, dest, router is not None)
        router = router or Router()
        part = Part(nc, st, tag)
        sg = part.sb("silu", [P, 2, CH])
        hs = part.sb("hs", [P, HC, CH])
        gu_ready, silu_ready, h_ready, y_ready, y_added = (
            part.sem(k) for k in ("gate_up_ready", "silu_ready", "h_ready", "y_ready", "y_added"))
        block = st.enter_context(nc.Block())

        @block.tensor
        def _(pe):
            def gate_up(c, j):
                for w, banks in ((net.L1_wg, (0, 1, 0)), (net.L1_wu, (2, 3, 2))):
                    need(pe, h_ready, c * HC + (1 if j == 2 else 0))
                    ins = nc.tensor.matmul(net.bank[banks[j]][:], w[:, j * P:(j + 1) * P],
                                           src[:, bass.ds(c * CH, CH)], start=True, stop=True)
                ins.then_inc(gu_ready, 1)

            def down(c):
                pe.wait_ge(h_ready, (c + 1) * HC)
                need(pe, y_added, c)
                for i in range(TPC):
                    for j in range(HC):
                        ins = nc.tensor.matmul(net.bank[4][:, i * P:(i + 1) * P], hs[:, j, i * P:(i + 1) * P],
                                               net.L1_wd[:, j, :], start=(j == 0), stop=(j == HC - 1))
                ins.then_inc(y_ready, 1)

            def body(c):
                before = not is_first(c)
                gate_up(c, 0)
                if before:
                    down(c - 1)
                gate_up(c, 1)
                if before:
                    norm.turn(pe, c - 1)
                gate_up(c, 2)
                if before and norm.route:
                    norm.logits(pe, c - 1, router.rw)
                    norm.turn_g(pe, c - 1)
                    norm.bias(pe, c - 1, router.b2)

            def tail(c):
                down(c)
                norm.all_pe(pe, c, router.rw, router.b2)
            rounds(pe, body, tail)

        @block.scalar
        def _(act):
            def silu(c, j):
                need(act, h_ready, c * HC + j - 1)
                act.wait_ge(gu_ready, c * HC + j + 1)
                nc.scalar.activation(sg[:, j % 2, :], net.bank[(0, 1, 0)[j]][:], ACT.Silu).then_inc(silu_ready, 1)

            def body(c):
                before = not is_first(c)
                silu(c, 0)
                silu(c, 1)
                if before:
                    norm.keep(act, c - 1)
                silu(c, 2)
                if before and norm.route:
                    norm.keep_g(act, c - 1)
            rounds(act, body, lambda c: norm.all_act(act, c))

        @block.gpsimd
        def _(pool):
            rounds(pool, lambda c: norm.all_pool(pool, c))

        @block.vector
        def _(dve):
            def mult(c, j):
                need(dve, y_ready, c)
                dve.wait_ge(silu_ready, c * HC + j + 1)
                nc.vector.tensor_tensor(hs[:, j, :], sg[:, j % 2, :], net.bank[(2, 3, 2)[j]][:],
                                        ALU.mult).then_inc(h_ready, 1)

            def add(c):
                x = net.x[:, bass.ds(c * CH, CH)]
                dve.wait_ge(y_ready, c + 1)
                nc.vector.scalar_tensor_tensor(x, net.bank[4][:], 0.5, x, ALU.mult, ALU.add).then_inc(y_added, 1)
                dve.wait_ge(y_added, c + 1)

            def body(c):
                before = not is_first(c)
                if before:
                    add(c - 1)
                    norm.stats(dve, c - 1)
                mult(c, 0)
                if before:
                    norm.apply(dve, c - 1)
                mult(c, 1)
                mult(c, 2)
                if before and norm.route:
                    norm.pick(dve, c - 1, router.rb)
                    norm.weigh(dve, c - 1)
                    norm.add_bias(dve, c - 1)

            def tail(c):
                add(c)
                norm.all_dve(dve, c, router.rb)
            rounds(dve, body, tail)



HPB = S // CH
TPB = S // P
SLOTS_Q = (0, 0, 1, 1, 0, 2)
SLOTS_K = (0, 1, 0, 1, 2, 0)
NS = len(SLOTS_Q)
KROWS = NS * HD
MROW0 = 96
QRING = 4
MROWS = 3
VCOL = 32


def rope_stage(nc, net, tag, src, q_parts, k_parts):
    with Scope(nc) as st:
        part = Part(nc, st, tag)
        xa = part.sb("xa", [P, CH])
        cos, sin = part.sb("cos", [P, S]), part.sb("sin", [P, S])
        rot = {w: part.sb(f"{w}_cos", [P, CH]) for w in "qk"}
        rot2 = {w: part.sb(f"{w}_sin", [P, CH]) for w in "qk"}
        full = {w: part.sb(f"{w}_full", [P, 3, CH]) for w in "qk"}
        split = {w: part.sb(f"{w}_parts", [P, 2, 3, CH], BF16) for w in "qk"}
        tables, xa_ready, qkv_ready, part_in, part_out, v_kept, own = (
            part.sem(k) for k in ("tables_loaded", "xa_ready", "qkv_ready", "part_in", "part_out",
                                  "v_kept", "dve_step"))
        stored = [part.sem(f"parts_stored{hf}") for hf in range(HPB)]
        experts = part.sem("experts_loaded")
        NST = 2 * NS
        block = st.enter_context(nc.Block())

        def batches(eng, body):
            for hf in range(HPB):
                body(hf, 0, hf)
            with eng.Fori(1, B) as b:
                for hf in range(HPB):
                    body(b * HPB + hf, b, hf)

        @block.sync
        def _(sp):
            sp.dma_start(cos[:], net.ins["cos"]).then_inc(tables, 16)
            sp.dma_start(sin[:], net.ins["sin"]).then_inc(tables, 16)

            def body(c, b, hf):
                for p in range(3):
                    for n, (w, dst, slots) in enumerate((("q", q_parts, SLOTS_Q), ("k", k_parts, SLOTS_K))):
                        sp.wait_ge(part_out, c * 6 + 2 * p + n + 1)
                        for i in range(NS):
                            if slots[i] == p:
                                sp.dma_start(dst[i, :, bass.ds(c * CH, CH)], split[w][:, hf, p, :]).then_inc(
                                    stored[hf], 16)
            batches(sp, body)
            for hf in range(HPB):
                sp.wait_ge(stored[hf], 16 * NST * B)

        @block.gpsimd
        def _(pool):
            pool.dma_start(net.w1[:], net.ins["L2_w1"]).then_inc(experts, 16)
            pool.dma_start(net.w2[:], net.ins["L2_w2"]).then_inc(experts, 16)
            pool.wait_ge(experts, 32)

        @block.tensor
        def _(pe):
            def body(c, b, hf):
                need(pe, own, 2 * c)
                xc = src[:, bass.ds(c * CH, CH)]
                for n in range(4):
                    nc.tensor.matmul(net.bank[n][:], net.L1_wqk[:, n, :], xc, start=True, stop=True).then_inc(qkv_ready, 1)
                need(pe, v_kept, c)
                pe.wait_ge(xa_ready, c + 1)
                for i in range(TPC):
                    t = slice(i * P, (i + 1) * P)
                    ins = nc.tensor.matmul(net.bank[4][:, t], xa[:, t], net.L1_wv[:], start=True, stop=True)
                ins.then_inc(qkv_ready, 1)
            batches(pe, body)

        @block.scalar
        def _(act):
            def body(c, b, hf):
                need(act, stored[hf], 16 * NST * b)
                for p in range(3):
                    for n, w in enumerate("qk"):
                        act.wait_ge(part_in, c * 6 + 2 * p + n + 1)
                        nc.scalar.activation(split[w][:, hf, p, :], full[w][:, p, :], ACT.Copy).then_inc(part_out, 1)
            batches(act, body)

        @block.vector
        def _(dve):
            nc.vector.memset(net.v1[:], 1.0)
            nc.vector.memset(net.K[:], 1.0)
            nc.vector.memset(net.Q[:], 0.0)
            dve.wait_ge(tables, 32)

            def body(c, b, hf):
                chain = Chain(dve, own, c * 2)
                need(dve, qkv_ready, 5 * c)
                nc.vector.tensor_scalar(xa[:], src[:, bass.ds(c * CH, CH)], 1.0, None, ALU.mult).then_inc(xa_ready, 1)
                pos = slice(hf * CH, (hf + 1) * CH)
                for n, w in enumerate("qk"):
                    dve.wait_ge(qkv_ready, 5 * c + 2 * n + 2)
                    nc.vector.tensor_tensor(rot[w][:], net.bank[2 * n][:], cos[:, pos], ALU.mult)
                    chain.then(nc.vector.tensor_tensor(rot2[w][:], net.bank[2 * n + 1][:], sin[:, pos], ALU.mult))
                    need(dve, part_out, 6 * c)
                    chain.wait()
                    ins = nc.vector.tensor_tensor(full[w][:, 0, :], rot[w][:], rot2[w][:], ALU.add)
                    ins.then_inc(part_in, 1)
                dve.wait_ge(qkv_ready, 5 * c + 5)
                for i in range(TPC):
                    ins = nc.vector.tensor_scalar(
                        net.v1[:].rearrange("p t (h e) -> p (t h) e", e=HD + 1)[:, bass.ds((c * TPC + i) * H, H), 0:HD],
                        net.bank[4][:, i * P:(i + 1) * P].rearrange("p (h d) -> p h d", d=HD), 1.0, None, ALU.mult)
                ins.then_inc(v_kept, 1)
                for p in range(2):
                    for n, w in enumerate("qk"):
                        dve.wait_ge(part_in, 6 * c + 2 * p + n + 1)
                        dve.wait_ge(part_out, 6 * c + 2 * p + n + 1)
                        ins = nc.vector.tensor_tensor(full[w][:, p + 1, :], full[w][:, p, :], split[w][:, hf, p, :],
                                                      ALU.subtract)
                        ins.then_inc(part_in, 1)
            batches(dve, body)


def attention_stage(nc, net, tag, dest, q_parts, k_parts, router):
    with Scope(nc) as st:
        assert router is None
        norm = Norm(nc, st, net, tag, dest, False, settled=True)
        part = Part(nc, st, tag)
        RING = 4
        PAIRS = TPB // 2
        AHEAD = H - 2
        pT = part.sb("pT", [P, RING, S])
        mx = part.sb("mx", [P, 2, TPB, HPB])
        nm = part.sb("nm", [P, 2, TPB])
        rem = part.sb("m_rem", [TPB, 3, P])
        mparts = part.sb("m_parts", [TPB, 2, 3, P], BF16)
        rd = part.sb("rden", [P, 2, TPB])
        vb = part.sb("vb", [P, H, TPB, VCOL])
        sums = part.sb("sums", [P, 2, CH])
        pv_sel = part.sb("pv_sel", [P, HPB * (HD + 1)])
        o = part.sb("o", [P, TPB, D])
        oT = part.sb("oT", [P, S])
        loaded = [part.sem(f"loaded{n}") for n in range(QRING)]
        m_rows = [part.sem(f"m_rows{n}") for n in range(2)]
        (sel_loaded, v_ready, a_ready, a_used, nm_ready, nm_turned, m_ready, s_ready, exp_ready, pv_step, sums_kept,
         gathered, o_ready, split_step, over_step, o_turned, oT_kept, y_ready, y_added) = (part.sem(k) for k in (
             "sel_loaded", "v_ready", "a_ready", "a_used", "nm_ready", "nm_turned", "m_ready", "s_ready", "exp_ready",
             "pv_step", "sums_kept", "gathered", "o_ready", "split_step", "over_step", "o_turned", "oT_kept",
             "y_ready", "y_added"))
        a_bank, s_bank, pv_bank, small_bank, y_bank = net.bank[0:2], net.bank[2:4], net.bank[4:6], net.bank[6], net.bank[7]
        norm.tbank = y_bank
        nm_rows = small_bank[0:TPB, 0:P]
        GW = TPC * HPB * (HD + 1)
        block = st.enter_context(nc.Block())

        def slot(t, h, rows):
            return t[0:rows, h % QRING, :]

        def gather_bank(h):
            return small_bank[:, P + GW * (h % 2):P + GW * (h % 2 + 1)]

        def ahead(b, h):
            if h < H:
                return b, h
            return None if is_last(b, B) else (b + 1, h - H)

        def before(b, h):
            if h > 0:
                return b, h - 1
            return None if is_first(b) else (b - 1, H - 1)

        @block.sync
        def _(sp):
            def load(b, h):
                for parts, t in ((q_parts, net.Q), (k_parts, net.K)):
                    sp.dma_start(slot(t, h, KROWS), parts[:, h * HD:(h + 1) * HD, bass.ds(b * S, S)]).then_inc(
                        loaded[h % QRING], 16)

            def rows(b, h):
                sp.wait_ge(m_ready, b * H + h + 1)
                for n in range(MROWS):
                    row = MROW0 + n
                    dst = net.Q[row:row + 1, h % QRING, :].rearrange("r (a t) -> r a t", t=P)
                    sp.dma_start(dst, mparts[:, h % 2, n, :]).then_inc(m_rows[h % 2], 16)

            def body(b):
                for h in range(H):
                    rows(b, h)
                    fetched = ahead(b, h + QRING - 1)
                    if fetched:
                        need(sp, s_ready, (b * H + h) * TPB * HPB)
                        load(*fetched)
            sp.dma_start(pv_sel[:], net.ins["pv_sel"]).then_inc(sel_loaded, 16)
            for h in range(QRING - 1):
                load(0, h)
            rounds(sp, body, count=B)
            for n in range(QRING):
                sp.wait_ge(loaded[n], 32 * B * H // QRING)
            for n in range(2):
                sp.wait_ge(m_rows[n], 16 * MROWS * B * H // 2)

        @block.tensor
        def _(pe):
            def big(b, h, qt, hf):
                if qt == 0 and hf == 0:
                    pe.wait_ge(loaded[h % QRING], (b * (H // QRING) + h // QRING + 1) * 32)
                n = ((b * H + h) * TPB + qt) * HPB + hf
                need(pe, a_used, n - 1)
                nc.tensor.matmul(a_bank[hf][:], slot(net.Q, h, MROW0)[:, qt * P:(qt + 1) * P],
                                 slot(net.K, h, MROW0)[:, hf * CH:(hf + 1) * CH], start=True, stop=True).then_inc(a_ready, 1)

            def turn(b, h):
                pe.wait_ge(nm_ready, b * H + h + 1)
                need(pe, m_ready, b * H + h)
                need(pe, o_ready, b * H + h - 2)
                nc.tensor.transpose(nm_rows, nm[:, h % 2, :], net.ident[:]).then_inc(nm_turned, 1)

            def small(b, h, kt, hf):
                if kt == 0 and hf == 0:
                    pe.wait_ge(m_rows[h % 2], (b * (H // 2) + h // 2 + 1) * 16 * MROWS)
                n = ((b * H + h) * TPB + kt) * HPB + hf
                need(pe, exp_ready, n - 1)
                nc.tensor.matmul(s_bank[hf][:], slot(net.K, h, MROW0 + MROWS)[:, kt * P:(kt + 1) * P],
                                 slot(net.Q, h, MROW0 + MROWS)[:, hf * CH:(hf + 1) * CH],
                                 start=True, stop=True).then_inc(s_ready, 1)

            def pv(b, h, pair):
                if pair == 0:
                    pe.wait_ge(v_ready, b * H + h + 1)
                    need(pe, sums_kept, b * H + h - 1)
                pe.wait_ge(exp_ready, ((b * H + h) * TPB + 2 * pair + 2) * HPB)
                for odd in range(2):
                    kt = 2 * pair + odd
                    for hf in range(HPB):
                        at = (odd * HPB + hf) * VCOL
                        ins = nc.tensor.matmul(pv_bank[h % 2][at:at + VCOL, :], vb[:, h, kt, :],
                                               pT[:, kt % RING, hf * CH:(hf + 1) * CH],
                                               start=(pair == 0), stop=(pair == PAIRS - 1),
                                               skip_group_check=True)
                ins.then_inc(pv_step, 1)

            def gather(b, h):
                if is_first(b) and h == 0:
                    pe.wait_ge(sel_loaded, 16)
                pe.wait_ge(sums_kept, b * H + h + 1)
                need(pe, o_ready, b * H + h)
                if ahead(b, h + 2):
                    pe.wait_ge(split_step, (b * H + h + 2) * 5 + 1)
                W = HPB * (HD + 1)
                for i in range(TPC):
                    ins = nc.tensor.matmul(gather_bank(h)[:, i * W:(i + 1) * W], sums[:, h % 2, i * P:(i + 1) * P],
                                           pv_sel[:], start=True, stop=True)
                ins.then_inc(gathered, 1)

            def turn_o(b, hf):
                if hf == 0:
                    pe.wait_ge(o_ready, (b + 1) * H)
                else:
                    pe.wait_ge(oT_kept, b * HPB + 1)
                for i in range(TPC):
                    ins = nc.tensor.transpose(y_bank[:, i * P:(i + 1) * P], o[:, i * HPB + hf, :], net.ident[:])
                ins.then_inc(o_turned, 1)

            def project(b, hf):
                pe.wait_ge(oT_kept, (b + 1) * HPB)
                if hf == 1:
                    pe.wait_ge(norm.kept, b * HPB + 1)
                for i in range(TPC):
                    t = slice(hf * CH + i * P, hf * CH + (i + 1) * P)
                    ins = nc.tensor.matmul(y_bank[:, i * P:(i + 1) * P], oT[:, t], net.L1_wout[:], start=True, stop=True)
                ins.then_inc(y_ready, 1)

            def end_of_sequence(b, h, kt):
                if (h, kt) in ((1, 3), (1, 6)):
                    turn_o(b, (1, 3) != (h, kt))
                if (h, kt) in ((2, 4), (6, 4)):
                    project(b, h // 6)
                if (h, kt) in ((5, 4), (9, 4)):
                    norm.turn(pe, b * HPB + h // 9)

            def body(b):
                if is_first(b):
                    for h in range(2):
                        for qt in range(TPB):
                            for hf in range(HPB):
                                big(b, h, qt, hf)
                        if h == 0:
                            turn(b, h)
                for h in range(H):
                    fetched, last, turned = ahead(b, h + 2), before(b, h), ahead(b, h + 1)
                    for kt in range(TPB):
                        for hf in range(HPB):
                            small(b, h, kt, hf)
                            if fetched:
                                big(*fetched, kt, hf)
                        if kt == 0 and last:
                            pv(*last, PAIRS - 1)
                        if kt == 1 and turned:
                            turn(*turned)
                        if kt >= 2 and kt % 2 == 0:
                            pv(b, h, kt // 2 - 1)
                        if kt == 3 and last:
                            gather(*last)
                        if not is_first(b):
                            end_of_sequence(b - 1, h, kt)
            rounds(pe, body, count=B)
            pv(B - 1, H - 1, PAIRS - 1)
            gather(B - 1, H - 1)
            for h in range(H):
                for kt in range(TPB):
                    end_of_sequence(B - 1, h, kt)

        @block.scalar
        def _(act):
            def exp(b, h, kt):
                n = (b * H + h) * TPB + kt
                need(act, pv_step, (b * H + h) * PAIRS + kt // 2 - 1)
                for hf in range(HPB):
                    act.wait_ge(s_ready, n * HPB + hf + 1)
                    nc.scalar.activation(pT[:, kt % RING, hf * CH:(hf + 1) * CH], s_bank[hf][:], ACT.Exp,
                                         scale=HD ** -0.5).then_inc(exp_ready, 1)

            def evacuate(b, h):
                act.wait_ge(pv_step, (b * H + h + 1) * PAIRS)
                need(act, gathered, b * H + h - 1)
                nc.scalar.activation(sums[:, h % 2, :], pv_bank[h % 2][:], ACT.Copy).then_inc(sums_kept, 1)

            def end_of_sequence(b, h, kt):
                if (h, kt) in ((1, 4), (1, 7)):
                    hf = kt // 7
                    act.wait_ge(o_turned, b * HPB + hf + 1)
                    nc.scalar.activation(oT[:, hf * CH:(hf + 1) * CH], y_bank[:], ACT.Copy).then_inc(oT_kept, 1)
                if (h, kt) in ((5, 6), (9, 6)):
                    norm.keep(act, b * HPB + h // 9)

            def body(b):
                for h in range(H):
                    last = before(b, h)
                    for kt in range(TPB):
                        exp(b, h, kt)
                        if kt == 1 and last:
                            evacuate(*last)
                        if not is_first(b):
                            end_of_sequence(b - 1, h, kt)
            rounds(act, body, count=B)
            evacuate(B - 1, H - 1)
            for h in range(H):
                for kt in range(TPB):
                    end_of_sequence(B - 1, h, kt)

        @block.gpsimd
        def _(pool):
            def body(c):
                norm.rstd_pow(pool, c)
            rounds(pool, body)

        @block.vector
        def _(dve):
            def largest(b, h, tiles):
                for qt in tiles:
                    for hf in range(HPB):
                        dve.wait_ge(a_ready, ((b * H + h) * TPB + qt) * HPB + hf + 1)
                        nc.vector.tensor_reduce(mx[:, h % 2, qt, hf:hf + 1], a_bank[hf][:], AX.X,
                                                ALU.max).then_inc(a_used, 1)

            def join(b, h):
                need(dve, nm_turned, b * H + h - 1)
                dve.wait_ge(a_used, (b * H + h + 1) * TPB * HPB)
                nc.vector.tensor_reduce(nm[:, h % 2, :], mx[:, h % 2], AX.X, ALU.max, negate=True).then_inc(nm_ready, 1)

            def split(b, h):
                u = b * H + h
                chain = Chain(dve, split_step, u * 5)
                dve.wait_ge(nm_turned, u + 1)
                need(dve, m_rows[h % 2], (b * (H // 2) + h // 2) * 16 * MROWS)
                m = mparts[:, h % 2]
                chain.then(nc.vector.tensor_copy(rem[:, 0, :], nm_rows))
                for n in range(3):
                    chain.wait()
                    if n < 2:
                        chain.then(nc.vector.tensor_copy(m[:, n, :], rem[:, n, :]))
                        chain.wait()
                        chain.then(nc.vector.tensor_tensor(rem[:, n + 1, :], rem[:, n, :], m[:, n, :], ALU.subtract))
                    else:
                        nc.vector.tensor_copy(m[:, n, :], rem[:, n, :]).then_inc(m_ready, 1)

            def over(b, h):
                u = b * H + h
                chain = Chain(dve, over_step, u + 1)
                dve.wait_ge(gathered, u + 1)
                if h == 0:
                    need(dve, o_turned, b * HPB)
                pv = gather_bank(h).rearrange("p (t e) -> p t e", e=HD + 1)
                chain.then(nc.vector.reciprocal(rd[:, h % 2, :], pv[:, :, HD]))
                chain.wait()
                nc.vector.tensor_tensor(o[:, :, h * HD:(h + 1) * HD], pv[:, :, 0:HD],
                                        bcast(rd[:, h % 2, :].rearrange("p (t a) -> p t a", a=1), [P, TPB, HD]),
                                        ALU.mult).then_inc(o_ready, 1)

            def copy_v(b, h):
                need(dve, pv_step, ((b - 1) * H + h + 1) * PAIRS)
                nc.vector.tensor_scalar(vb[:, h, :, 0:HD + 1],
                                        net.v1[:, bass.ds(b * TPB, TPB), h * (HD + 1):(h + 1) * (HD + 1)],
                                        1.0, None, ALU.mult).then_inc(v_ready, 1)

            def end_of_sequence(b, h):
                if h in (3, 7):
                    c = b * HPB + h // 7
                    x = net.x[:, bass.ds(c * CH, CH)]
                    dve.wait_ge(y_ready, c + 1)
                    nc.vector.tensor_tensor(x, x, y_bank[:], ALU.add).then_inc(y_added, 1)
                    dve.wait_ge(y_added, c + 1)
                    x3 = x.rearrange("p (t d) -> p t d", d=D)
                    b_out = bcast(net.L1_bout[:].rearrange("p (a d) -> p a d", a=1), [P, TPC, D])
                    nc.vector.tensor_tensor(x3, x3, b_out, ALU.add).then_inc(norm.x_whole, 1)
                    dve.wait_ge(norm.x_whole, c + 1)
                    norm.stats(dve, c)
                if h in (4, 8):
                    norm.apply(dve, b * HPB + h // 8)

            def body(b):
                if is_first(b):
                    nc.vector.memset(vb[:], 0.0).then_inc(over_step, 1)
                    dve.wait_ge(over_step, 1)
                    for h in range(AHEAD):
                        copy_v(b, h)
                    largest(b, 0, range(TPB))
                    join(b, 0)
                    split(b, 0)
                    largest(b, 1, range(TPB))
                    join(b, 1)
                for h in range(H):
                    fetched, last, turned, copied = ahead(b, h + 2), before(b, h), ahead(b, h + 1), ahead(b, h + AHEAD)
                    if fetched:
                        largest(*fetched, range(0, 2))
                    if turned:
                        split(*turned)
                    if fetched:
                        largest(*fetched, range(2, 6))
                    if last:
                        over(*last)
                    if not is_first(b):
                        end_of_sequence(b - 1, h)
                    if fetched:
                        largest(*fetched, range(6, TPB))
                        join(*fetched)
                    if copied:
                        copy_v(*copied)
            rounds(dve, body, count=B)
            over(B - 1, H - 1)
            for h in range(H):
                end_of_sequence(B - 1, h)



NEXP = 8
PW = 2 * P + 2
DEN_EPS = 1e-6


def decay_stage(nc, net, tag, src, dest, router):
    with Scope(nc) as st:
        norm = Norm(nc, st, net, tag, dest, router is not None, across=True)
        part = Part(nc, st, tag)
        W1 = D + 1
        gamma = part.sb("gamma", [P, NEXP])
        bits, nbits = part.sb("bits", [P, NEXP, PW]), part.sb("nbits", [P, NEXP, PW])
        causal = part.sb("causal", [P, P])
        factor, power = part.sb("factor", [P, PW]), part.sb("power", [P, PW])
        xa = part.sb("xa", [P, B, P])
        qT, kT, qd = part.sb("qT", [P, B, P]), part.sb("kT", [P, B, P]), part.sb("qd", [P, B, P])
        kb, kd = part.sb("kb", [P, B, D]), part.sb("kd", [P, B, D])
        v1 = part.sb("v1", [P, B, W1])
        aT = part.sb("aT", [P, B, P])
        state = part.sb("state", [P, B, W1])
        den, rden, y = part.sb("den", [P, B]), part.sb("rden", [P, B]), part.sb("y", [P, B, D])
        loads, setup, xa_ready, q_ready, k_ready, kv_ready, qk_kept, weighted, a_ready, at_ready = (
            part.sem(k) for k in ("loads", "setup", "xa_ready", "q_ready", "k_ready", "kv_ready", "qk_kept", "weighted",
                                  "a_ready", "at_ready"))
        num_ready, state_ready, divided, carried, own = (
            part.sem(k) for k in ("num_ready", "state_ready", "divided", "carried", "dve_step"))
        w_decay, q_power, k_power = power[:, 0:P], power[:, P:2 * P], power[:, 2 * P:2 * P + 1]
        s_power = power[:, 2 * P + 1:2 * P + 2]
        block = st.enter_context(nc.Block())

        def pair(t, m):
            return t[:, 2 * m:2 * m + 2]

        @block.sync
        def _(sp):
            sp.dma_start(bits[:], net.ins["bits"]).then_inc(loads, 16)
            sp.dma_start(nbits[:], net.ins["nbits"]).then_inc(loads, 16)
            sp.dma_start(causal[:], net.ins["causal"]).then_inc(loads, 16)
            sp.dma_start(gamma[:, 0:1], net.ins["gamma"].partition_broadcast(P)).then_inc(loads, 16)
            sp.wait_ge(loads, 64)

        @block.tensor
        def _(pe):
            def proj(n):
                need(pe, carried, 2 * n)
                pe.wait_ge(xa_ready, n + 1)
                xf = xa[:].rearrange("p b t -> p (b t)")
                nc.tensor.matmul(net.bank[0][:], net.L2_wq[:], xf, start=True, stop=True).then_inc(q_ready, 1)
                nc.tensor.matmul(net.bank[1][:], net.L2_wkv[:, 0:D], xf, start=True, stop=True).then_inc(k_ready, 1)
                need(pe, weighted, n)
                for b in range(B):
                    ins = nc.tensor.matmul(net.bank[2 + b // 2][:, (b % 2) * 2 * D:(b % 2 + 1) * 2 * D], xa[:, b, :],
                                           net.L2_wkv[:], start=True, stop=True)
                ins.then_inc(kv_ready, 1)

            def scores(n):
                pe.wait_ge(qk_kept, 2 * (n + 1))
                need(pe, divided, 2 * n)
                for b in range(B):
                    ins = nc.tensor.matmul(net.bank[4][:, b * P:(b + 1) * P], kT[:, b, :], qT[:, b, :],
                                           start=True, stop=True)
                ins.then_inc(a_ready, 1)

            def sums(n):
                pe.wait_ge(at_ready, n + 1)
                pe.wait_ge(weighted, n + 1)
                need(pe, carried, 2 * n)
                for b in range(B):
                    out = net.bank[4 + b // 2][:, (b % 2) * W1:(b % 2 + 1) * W1]
                    nc.tensor.matmul(out, aT[:, b, :], v1[:, b, :], start=True, stop=False)
                    ins = nc.tensor.matmul(out, qd[:, b, :], state[:, b, :], start=False, stop=True)
                ins.then_inc(num_ready, 1)

            def update(n):
                for b in range(B):
                    ins = nc.tensor.matmul(net.bank[b // 2][:, (b % 2) * W1:(b % 2 + 1) * W1], kd[:, b, :], v1[:, b, :],
                                           start=True, stop=True)
                ins.then_inc(state_ready, 1)

            def body(n):
                before = not is_first(n)
                proj(n)
                if before:
                    norm.turn(pe, n - 1)
                scores(n)
                if before and norm.route:
                    norm.logits(pe, n - 1, router.rw)
                sums(n)
                if before and norm.route:
                    norm.turn_g(pe, n - 1)
                update(n)
                if before and norm.route:
                    norm.bias(pe, n - 1, router.b2)
            rounds(pe, body, lambda n: norm.all_pe(pe, n, router.rw, router.b2))

        @block.scalar
        def _(act):
            def body(n):
                act.wait_ge(q_ready, n + 1)
                nc.scalar.activation(qT[:].rearrange("p b t -> p (b t)"), net.bank[0][:], ACT.Relu,
                                     bias=net.L2_bq[:]).then_inc(qk_kept, 1)
                act.wait_ge(k_ready, n + 1)
                nc.scalar.activation(kT[:].rearrange("p b t -> p (b t)"), net.bank[1][:], ACT.Relu,
                                     bias=net.L2_bk[:]).then_inc(qk_kept, 1)
                if not is_first(n):
                    norm.keep(act, n - 1)
                    if norm.route:
                        norm.keep_g(act, n - 1)
            rounds(act, body, lambda n: norm.all_act(act, n))

        @block.gpsimd
        def _(pool):
            rounds(pool, lambda n: norm.all_pool(pool, n))

        @block.vector
        def _(dve):
            chain = Chain(dve, setup, 0)
            dve.wait_ge(loads, 64)
            for k in range(1, NEXP):
                chain.then(nc.vector.tensor_tensor(gamma[:, k:k + 1], gamma[:, k - 1:k], gamma[:, k - 1:k], ALU.mult))
                chain.wait()
            chain.then(nc.vector.memset(power[:], 1.0))
            for k in range(NEXP):
                chain.then(nc.vector.scalar_tensor_tensor(factor[:], bits[:, k, :], gamma[:, k:k + 1], nbits[:, k, :],
                                                          ALU.mult, ALU.add))
                chain.wait()
                chain.then(nc.vector.tensor_tensor(power[:], power[:], factor[:], ALU.mult))
                chain.wait()
            chain.then(nc.vector.tensor_tensor(w_decay, w_decay, causal[:], ALU.mult))
            nc.vector.memset(v1[:], 1.0)
            chain.then(nc.vector.memset(state[:], 0.0))
            chain.wait()

            def fetch(n):
                need(dve, kv_ready, n)
                nc.vector.tensor_scalar(xa[:], norm.view(src, n), 1.0, None, ALU.mult).then_inc(xa_ready, 1)

            def weight(n):
                steps = Chain(dve, own, n * 8)
                dve.wait_ge(kv_ready, n + 1)
                for m in range(2):
                    kv = net.bank[2 + m][:].rearrange("p (b e) -> p b e", b=2)
                    nc.vector.tensor_tensor(pair(v1, m)[:, :, 0:D], kv[:, :, D:2 * D],
                                            bcast(net.L2_bv_row[:].rearrange("p (a d) -> p a d", a=1), [P, 2, D]), ALU.add)
                    steps.then(nc.vector.tensor_tensor(
                        pair(kb, m), kv[:, :, 0:D],
                        bcast(net.L2_bk_row[:].rearrange("p (a d) -> p a d", a=1), [P, 2, D]), ALU.add))
                steps.wait()
                nc.vector.tensor_scalar(kd[:], kb[:], 0.0, k_power, ALU.max, ALU.mult)
                dve.wait_ge(qk_kept, 2 * n + 1)
                nc.vector.tensor_tensor(qd[:], qT[:], bcast(q_power.rearrange("p (a t) -> p a t", a=1), [P, B, P]),
                                        ALU.mult).then_inc(weighted, 1)

            def decay(n):
                dve.wait_ge(a_ready, n + 1)
                nc.vector.tensor_tensor(aT[:], net.bank[4][:].rearrange("p (b t) -> p b t", b=B),
                                        bcast(w_decay.rearrange("p (a t) -> p a t", a=1), [P, B, P]),
                                        ALU.mult).then_inc(at_ready, 1)

            def divide(n):
                steps = Chain(dve, own, n * 8 + 2)
                x = norm.view(net.x, n)
                dve.wait_ge(num_ready, n + 1)
                for m in range(2):
                    sums = net.bank[4 + m][:, 0:2 * W1].rearrange("p (b e) -> p b e", b=2)
                    steps.then(nc.vector.tensor_scalar(den[:, 2 * m:2 * m + 2], sums[:, :, D], DEN_EPS, None, ALU.add))
                    steps.wait()
                    steps.then(nc.vector.reciprocal(rden[:, 2 * m:2 * m + 2], den[:, 2 * m:2 * m + 2]))
                    steps.wait()
                    steps.then(nc.vector.tensor_tensor(
                        pair(y, m), sums[:, :, 0:D],
                        bcast(rden[:, 2 * m:2 * m + 2].rearrange("p (b a) -> p b a", a=1), [P, 2, D]), ALU.mult))
                    steps.wait()
                    nc.vector.tensor_tensor(x[:, 2 * m:2 * m + 2], x[:, 2 * m:2 * m + 2], pair(y, m),
                                            ALU.add).then_inc(divided, 1)

            def carry(n):
                dve.wait_ge(state_ready, n + 1)
                for m in range(2):
                    nc.vector.scalar_tensor_tensor(pair(state, m), pair(state, m), s_power,
                                                   net.bank[m][:, 0:2 * W1].rearrange("p (b e) -> p b e", b=2),
                                                   ALU.mult, ALU.add).then_inc(carried, 1)

            def body(n):
                before = not is_first(n)
                if before:
                    norm.apply(dve, n - 1)
                else:
                    fetch(0)
                weight(n)
                if not is_last(n):
                    fetch(n + 1)
                decay(n)
                if before and norm.route:
                    norm.pick(dve, n - 1, router.rb)
                divide(n)
                if before and norm.route:
                    norm.weigh(dve, n - 1)
                carry(n)
                if before and norm.route:
                    norm.add_bias(dve, n - 1)
                dve.wait_ge(divided, 2 * (n + 1))
                norm.stats(dve, n)

            def tail(n):
                norm.apply(dve, n)
                if norm.route:
                    norm.pick(dve, n, router.rb)
                    norm.weigh(dve, n)
                    norm.add_bias(dve, n)
            rounds(dve, body, tail)



def chunks_of_sequences(eng, body):
    for hf in range(HPB):
        body(hf, 0, hf)
    with eng.Fori(1, B) as b:
        for hf in range(HPB):
            body(b * HPB + hf, b, hf)


def fetch_shifted(nc, xs, src, c, hf):
    if hf == 0:
        return nc.vector.tensor_scalar(xs[:, 0, 1:CH + 1], src[:, bass.ds(c * CH, CH)], 1.0, None, ALU.mult)
    return nc.vector.tensor_scalar(xs[:, 1, :], src[:, bass.ds(c * CH - 1, CH + 1)], 1.0, None, ALU.mult)


def rwkv_ffn_stage(nc, net, tag, src, dest):
    with Scope(nc) as st:
        norm = Norm(nc, st, net, tag, dest, False) if dest is not None else None
        part = Part(nc, st, tag)
        xs = part.sb("xs", [P, 2, CH + 1])
        diff = part.sb("diff", [P, CH])
        xr, xk = part.sb("xr", [P, 2, CH]), part.sb("xk", [P, 2, CH])
        kr, kk, sig, gated = (part.sb(k, [P, 2, CH]) for k in ("k_relu", "k_square", "sigmoid", "gated"))
        setup, mixed, k_ready, r_ready, acted, squared, y_ready, y_added, own, x_whole = (
            part.sem(k) for k in ("setup", "mixed", "k_ready", "r_ready", "acted", "squared", "y_ready", "y_added",
                                  "dve_step", "x_whole_here"))
        block = st.enter_context(nc.Block())

        @block.tensor
        def _(pe):
            def body(c, b, hf):
                pe.wait_ge(mixed, c + 1)
                need(pe, acted, 2 * c)
                nc.tensor.matmul(net.bank[0][:], net.L3_fk[:], xk[:, hf, :], start=True, stop=True).then_inc(k_ready, 1)
                for i in range(TPC):
                    t = slice(i * P, (i + 1) * P)
                    ins = nc.tensor.matmul(net.bank[1][:, t], xr[:, hf, t], net.L3_fr[:], start=True, stop=True)
                ins.then_inc(r_ready, 1)
                if norm and not is_first(c):
                    norm.turn(pe, c - 1)
                pe.wait_ge(squared, c + 1)
                need(pe, y_added, c)
                for i in range(TPC):
                    t = slice(i * P, (i + 1) * P)
                    ins = nc.tensor.matmul(net.bank[2][:, t], kk[:, hf, t], net.L3_fv[:], start=True, stop=True)
                ins.then_inc(y_ready, 1)
            chunks_of_sequences(pe, body)
            if norm:
                norm.all_pe(pe, NCH - 1)

        @block.scalar
        def _(act):
            def body(c, b, hf):
                need(act, squared, c - 1)
                act.wait_ge(k_ready, c + 1)
                nc.scalar.activation(kr[:, hf, :], net.bank[0][:], ACT.Relu).then_inc(acted, 1)
                need(act, y_added, c - 1)
                act.wait_ge(r_ready, c + 1)
                nc.scalar.activation(sig[:, hf, :], net.bank[1][:], ACT.Sigmoid).then_inc(acted, 1)
                if norm and not is_first(c):
                    norm.keep(act, c - 1)
            chunks_of_sequences(act, body)
            if norm:
                norm.all_act(act, NCH - 1)

        @block.gpsimd
        def _(pool):
            if norm:
                rounds(pool, lambda c: norm.all_pool(pool, c))

        @block.vector
        def _(dve):
            nc.vector.memset(xs[:, 0, 0:1], 0.0).then_inc(setup, 1)
            dve.wait_ge(setup, 1)

            def mix(c, hf):
                chain = Chain(dve, own, c * 2)
                chain.then(fetch_shifted(nc, xs, src, c, hf))
                chain.wait()
                old = xs[:, hf, 0:CH]
                chain.then(nc.vector.tensor_tensor(diff[:], xs[:, hf, 1:CH + 1], old, ALU.subtract))
                need(dve, r_ready, c - 1)
                chain.wait()
                nc.vector.scalar_tensor_tensor(xk[:, hf, :], diff[:], net.L3_mu_k[:], old, ALU.mult, ALU.add)
                nc.vector.scalar_tensor_tensor(xr[:, hf, :], diff[:], net.L3_mu_r[:], old, ALU.mult,
                                               ALU.add).then_inc(mixed, 1)

            def square(c, hf):
                dve.wait_ge(acted, 2 * c + 1)
                need(dve, y_ready, c - 1)
                nc.vector.tensor_tensor(kk[:, hf, :], kr[:, hf, :], kr[:, hf, :], ALU.mult).then_inc(squared, 1)

            def add(c, hf):
                x = net.x[:, bass.ds(c * CH, CH)]
                dve.wait_ge(acted, 2 * c + 2)
                dve.wait_ge(y_ready, c + 1)
                nc.vector.tensor_tensor(gated[:, hf, :], net.bank[2][:], sig[:, hf, :], ALU.mult).then_inc(y_added, 1)
                dve.wait_ge(y_added, c + 1)
                nc.vector.scalar_tensor_tensor(x, gated[:, hf, :], 0.5, x, ALU.mult, ALU.add).then_inc(x_whole, 1)
                dve.wait_ge(x_whole, c + 1)

            def body(c, b, hf):
                mix(c, hf)
                if not is_first(c):
                    add(c - 1, 1 - hf)
                    if norm:
                        norm.stats(dve, c - 1)
                square(c, hf)
                if norm and not is_first(c):
                    norm.apply(dve, c - 1)
            chunks_of_sequences(dve, body)
            add(NCH - 1, 1)
            if norm:
                norm.all_dve(dve, NCH - 1)



NMIX = 5
TM = 32
TD = 64
GN_EPS = 1e-5 * HD ** 2


def time_mix_stage(nc, net, tag, src, dest):
    with Scope(nc) as st:
        norm = Norm(nc, st, net, tag, dest, False)
        part = Part(nc, st, tag)
        xs = part.sb("xs", [P, 2, CH + 1])
        xx, x3 = part.sb("xx", [P, CH]), part.sb("x_first_mix", [P, CH])
        m0, m1 = part.sb("tanh_m0", [P, CH]), part.sb("tanh_m1", [TM, CH])
        corr = part.sb("corr", [P, 2, CH])
        xm = part.sb("x_mixed", [P, NMIX, CH])
        tw, e1, wd = part.sb("tanh_w", [TD, CH]), part.sb("exp_w", [P, CH]), part.sb("decay", [P, CH])
        kT, rT, vT, gT = (part.sb(k, [P, CH]) for k in ("kT", "rT", "vT", "gT"))
        kv = part.sb("kv", [P, 2, CH])
        S_t = part.sb("S", [P, HD, CH + 1])
        rs = part.sb("rS", [P, 4, CH])
        rku, bonus, y, yc, sq, ve, rstd = (part.sb(k, [P, CH]) for k in ("rku", "bonus", "y", "yc", "sq", "ve", "rstd"))
        yn, yg = part.sb("yn", [P, CH]), part.sb("yg", [P, CH])
        w2a, w2b = part.sb("w2a", [P, 4, D]), part.sb("w2b", [TM, D])
        sel = part.sb("sel", [P, HD, D])
        half = part.sb("half", [P, CH])
        W_ = {k: part.sb(f"W{k}", [P, D]) for k in ("r", "k", "v", "g", "o", "blockones", "center", "blockmean")}
        w1 = part.sb("w1", [P, NMIX * TM])
        dw1, dw2 = part.sb("dw1", [P, TD]), part.sb("dw2", [TD, D])
        Wv_rep = part.sb("Wv_rep", [P, HD, D])
        vecs = part.sb("vecs", [P, 10])
        (loads, setup, xx_ready, m_ready, m_kept, mix_ready, mix_used, mixed, lin_ready, lin_kept, w1_ready, w1_kept,
         w2_ready, wd_ready, e1_ready, rep_ready, kv_done, scanned, rs_ready, y_acc, rku_ready, bonus_ready,
         bonus_used) = (part.sem(k) for k in (
             "loads", "setup", "xx_ready", "m_ready", "m_kept", "mix_ready", "mix_used", "mixed", "lin_ready", "lin_kept",
             "w1_ready", "w1_kept", "w2_ready", "wd_ready", "e1_ready", "rep_ready", "kv_done", "scanned", "rs_ready",
             "y_acc", "rku_ready", "bonus_ready", "bonus_used"))
        (y_whole, yc_ready, yc_kept, sq_ready, var_ready, ve_ready, pow_ready, yg_ready, out_ready, out_added, own) = (
            part.sem(k) for k in ("y_whole", "yc_ready", "yc_kept", "sq_ready", "var_ready", "ve_ready", "pow_ready",
                                  "yg_ready", "out_ready", "out_added", "dve_step"))
        names = ["td_decay", "u", "ln_gamma", "ln_beta", "maa_x", "maa_w", "maa_k", "maa_v", "maa_r", "maa_g"]
        vec = {k: vecs[:, i:i + 1] for i, k in enumerate(names)}
        mats = [(W_[k], "L3_" + k) for k in W_] + [(w1, "L3_w1"), (dw1, "L3_dw1"), (dw2, "L3_dw2"), (sel, "sel"),
                                                    (vecs, "L3_vecs")]
        NLOAD = len(mats) + 4 + 1 + HD
        block = st.enter_context(nc.Block())
        MIX_BANK = [net.bank[i] for i in (2, 3, 4, 5, 0)]
        LINEAR = (("k", 1, 2), ("r", 3, 3), ("v", 2, 4), ("g", 4, 5))

        @block.sync
        def _(sp):
            for t, name in mats:
                sp.dma_start(t[:], net.ins[name]).then_inc(loads, 16)
            sp.wait_ge(setup, 1)
            for f in range(4):
                sp.dma_start(w2a[f * TM:(f + 1) * TM, f, :], net.ins["L3_w2"][f]).then_inc(loads, 16)
            sp.dma_start(w2b[:], net.ins["L3_w2"][4]).then_inc(loads, 16)
            for j in range(HD):
                sp.dma_start(Wv_rep[:, j, :], net.ins["L3_v_rep"][j]).then_inc(loads, 16)
            sp.wait_ge(loads, 16 * NLOAD)

        @block.tensor
        def _(pe):
            pe.wait_ge(loads, 16 * NLOAD)

            def body(c, b, hf):
                pe.wait_ge(xx_ready, c + 1)
                need(pe, kv_done, HD * c)
                nc.tensor.matmul(net.bank[0][:], w1[:, 0:P], x3[:], start=True, stop=True).then_inc(m_ready, 1)
                nc.tensor.matmul(net.bank[1][0:TM, :], w1[:, P:P + TM], x3[:], start=True, stop=True).then_inc(m_ready, 1)
                need(pe, out_added, c)
                for f in range(NMIX):
                    pe.wait_ge(m_kept, 2 * c + (1 if f < 4 else 2))
                    lhs, rhs = (w2a[:, f, :], m0[:]) if f < 4 else (w2b[:], m1[:])
                    nc.tensor.matmul(MIX_BANK[f][:], lhs, rhs, start=True, stop=True).then_inc(mix_ready, 1)
                if not is_first(c):
                    norm.turn(pe, c - 1)
                pe.wait_ge(mixed, NMIX * c + 1)
                nc.tensor.matmul(net.bank[1][0:TD, :], dw1[:], xm[:, 0, :], start=True, stop=True).then_inc(w1_ready, 1)
                for k, f, bank in LINEAR:
                    pe.wait_ge(mixed, NMIX * (c + 1))
                    nc.tensor.matmul(net.bank[bank][:], W_[k][:], xm[:, f, :], start=True, stop=True).then_inc(lin_ready, 1)
                pe.wait_ge(w1_kept, c + 1)
                nc.tensor.matmul(net.bank[1][:], dw2[:], tw[:], start=True, stop=True).then_inc(w2_ready, 1)

                def repeat(j):
                    if j == 1:
                        pe.wait_ge(e1_ready, c + 1)
                    if j >= 2:
                        need(pe, kv_done, HD * c + j - 1)
                    nc.tensor.matmul(net.bank[j % 2][:], Wv_rep[:, j, :], xm[:, 2, :],
                                     start=True, stop=True).then_inc(rep_ready, 1)

                repeat(0)
                repeat(1)
                pe.wait_ge(lin_kept, 4 * (c + 1))
                pe.wait_ge(rku_ready, c + 1)
                nc.tensor.matmul(net.bank[3][:], W_["blockones"][:], rku[:], start=True, stop=True).then_inc(bonus_ready, 1)
                for j in range(HD):
                    if j + 2 < HD:
                        repeat(j + 2)
                    pe.wait_ge(rs_ready, HD * c + j + 1)
                    nc.tensor.matmul(net.bank[2][:], sel[:, j, :], rs[:, j % 4, :],
                                     start=(j == 0), stop=(j == HD - 1)).then_inc(y_acc, 1)
                pe.wait_ge(y_whole, c + 1)
                nc.tensor.matmul(net.bank[4][:], W_["center"][:], y[:], start=True, stop=True).then_inc(yc_ready, 1)
                pe.wait_ge(sq_ready, c + 1)
                nc.tensor.matmul(net.bank[5][:], W_["blockmean"][:], sq[:], start=True, stop=True).then_inc(var_ready, 1)
                pe.wait_ge(yg_ready, c + 1)
                for i in range(TPC):
                    t = slice(i * P, (i + 1) * P)
                    ins = nc.tensor.matmul(net.bank[3][:, t], yg[:, t], W_["o"][:], start=True, stop=True)
                ins.then_inc(out_ready, 1)
            chunks_of_sequences(pe, body)
            norm.all_pe(pe, NCH - 1)

        @block.scalar
        def _(act):
            act.wait_ge(loads, 16 * NLOAD)

            def body(c, b, hf):
                act.wait_ge(m_ready, 2 * c + 1)
                nc.scalar.activation(m0[:], net.bank[0][:], ACT.Tanh).then_inc(m_kept, 1)
                act.wait_ge(m_ready, 2 * c + 2)
                nc.scalar.activation(m1[:], net.bank[1][0:TM, :], ACT.Tanh).then_inc(m_kept, 1)
                act.wait_ge(w1_ready, c + 1)
                nc.scalar.activation(tw[:], net.bank[1][0:TD, :], ACT.Tanh).then_inc(w1_kept, 1)
                if not is_first(c):
                    norm.keep(act, c - 1)
                for n, (dst, bank, func) in enumerate(((kT, 2, ACT.Copy), (rT, 3, ACT.Copy), (vT, 4, ACT.Copy))):
                    act.wait_ge(lin_ready, 4 * c + n + 1)
                    nc.scalar.activation(dst[:], net.bank[bank][:], func).then_inc(lin_kept, 1)
                act.wait_ge(w2_ready, c + 1)
                nc.scalar.activation(e1[:], net.bank[1][:], ACT.Exp, bias=vec["td_decay"]).then_inc(e1_ready, 1)
                act.wait_ge(e1_ready, c + 1)
                nc.scalar.activation(wd[:], e1[:], ACT.Exp, scale=-1.0).then_inc(wd_ready, 1)
                act.wait_ge(lin_ready, 4 * c + 4)
                nc.scalar.activation(gT[:], net.bank[5][:], ACT.Silu).then_inc(lin_kept, 1)
                act.wait_ge(yc_ready, c + 1)
                nc.scalar.activation(yc[:], net.bank[4][:], ACT.Copy).then_inc(yc_kept, 1)
                nc.scalar.activation(sq[:], net.bank[4][:], ACT.Square).then_inc(sq_ready, 1)
            chunks_of_sequences(act, body)
            norm.all_act(act, NCH - 1)

        @block.gpsimd
        def _(pool):
            nc.gpsimd.memset(w2a[:], 0.0).then_inc(setup, 1)
            nc.gpsimd.memset(half[:], -0.5)

            def body(c, b, hf):
                if not is_first(c):
                    norm.all_pool(pool, c - 1)
                pool.wait_ge(lin_kept, 4 * c + 2)
                for j in range(HD):
                    need(pool, y_acc, HD * c + j - 3)
                    pool.wait_ge(scanned, HD * c + j + 1)
                    nc.gpsimd.tensor_tensor(rs[:, j % 4, :], rT[:], S_t[:, j, 0:CH], ALU.mult).then_inc(rs_ready, 1)
                pool.wait_ge(ve_ready, c + 1)
                nc.gpsimd.tensor_tensor(rstd[:], ve[:], half[:], ALU.pow).then_inc(pow_ready, 1)
            chunks_of_sequences(pool, body)
            norm.all_pool(pool, NCH - 1)

        @block.vector
        def _(dve):
            dve.wait_ge(loads, 16 * NLOAD)
            start = Chain(dve, own, 0)
            start.then(nc.vector.memset(xs[:, 0, 0:1], 0.0))
            start.wait()
            STEPS = 12

            def body(c, b, hf):
                chain = Chain(dve, own, c * STEPS + 1)
                cur, old = xs[:, hf, 1:CH + 1], xs[:, hf, 0:CH]
                chain.then(fetch_shifted(nc, xs, src, c, hf))
                chain.wait()
                chain.then(nc.vector.tensor_tensor(xx[:], old, cur, ALU.subtract))
                chain.wait()
                nc.vector.scalar_tensor_tensor(x3[:], xx[:], vec["maa_x"], cur, ALU.mult, ALU.add).then_inc(xx_ready, 1)
                if not is_first(c):
                    norm.apply(dve, c - 1)
                for f in range(NMIX):
                    dve.wait_ge(mix_ready, NMIX * c + f + 1)
                    chain.then(nc.vector.scalar_tensor_tensor(corr[:, f % 2, :], MIX_BANK[f][:], vecs[:, 5 + f:6 + f], xx[:],
                                                              ALU.add, ALU.mult))
                    chain.wait()
                    nc.vector.tensor_tensor(xm[:, f, :], corr[:, f % 2, :], cur, ALU.add).then_inc(mixed, 1)
                dve.wait_ge(lin_kept, 4 * c + 2)
                chain.then(nc.vector.scalar_tensor_tensor(rku[:], rT[:], vec["u"], kT[:], ALU.mult, ALU.mult))
                chain.eng.wait_ge(own, chain.count)
                nc.vector.tensor_scalar(corr[:, 0, 0:1], corr[:, 0, 0:1], 1.0, None, ALU.mult).then_inc(rku_ready, 1)
                need(dve, rs_ready, HD * c)
                if hf == 0:
                    chain.then(nc.vector.memset(S_t[:, :, 0:1], 0.0))
                else:
                    chain.then(nc.vector.tensor_copy(S_t[:, :, 0:1], S_t[:, :, CH:CH + 1]))
                for j in range(HD):
                    dve.wait_ge(rep_ready, HD * c + j + 1)
                    nc.vector.tensor_tensor(kv[:, j % 2, :], kT[:], net.bank[j % 2][:], ALU.mult).then_inc(kv_done, 1)
                    if j == 0:
                        dve.wait_ge(wd_ready, c + 1)
                        chain.wait()
                    dve.wait_ge(kv_done, HD * c + j + 1)
                    nc.vector.tensor_tensor_scan(S_t[:, j, 1:CH + 1], wd[:], kv[:, j % 2, :], S_t[:, j, 0:1],
                                                 ALU.mult, ALU.add).then_inc(scanned, 1)
                dve.wait_ge(lin_kept, 4 * c + 3)
                dve.wait_ge(bonus_ready, c + 1)
                chain.then(nc.vector.tensor_tensor(bonus[:], vT[:], net.bank[3][:], ALU.mult))
                dve.wait_ge(y_acc, HD * (c + 1))
                chain.wait()
                nc.vector.tensor_tensor(y[:], bonus[:], net.bank[2][:], ALU.add).then_inc(y_whole, 1)
                dve.wait_ge(var_ready, c + 1)
                nc.vector.tensor_scalar(ve[:], net.bank[5][:], GN_EPS, None, ALU.add).then_inc(ve_ready, 1)
                dve.wait_ge(yc_kept, c + 1)
                dve.wait_ge(pow_ready, c + 1)
                chain.then(nc.vector.tensor_tensor(yn[:], yc[:], rstd[:], ALU.mult))
                chain.wait()
                chain.then(nc.vector.tensor_scalar(yn[:], yn[:], vec["ln_gamma"], vec["ln_beta"], ALU.mult, ALU.add))
                dve.wait_ge(lin_kept, 4 * c + 4)
                chain.wait()
                nc.vector.tensor_tensor(yg[:], yn[:], gT[:], ALU.mult).then_inc(yg_ready, 1)
                x = net.x[:, bass.ds(c * CH, CH)]
                dve.wait_ge(out_ready, c + 1)
                nc.vector.tensor_tensor(x, x, net.bank[3][:], ALU.add).then_inc(out_added, 1)
                dve.wait_ge(out_added, c + 1)
                norm.stats(dve, c)
            chunks_of_sequences(dve, body)
            norm.apply(dve, NCH - 1)



def store_stage(nc, net, out):
    with Scope(nc) as st:
        stored = st.sem("stored")
        block = st.enter_context(nc.Block())

        @block.sync
        def _(sp):
            dst = out.rearrange("(t p) d -> p t d", p=P)
            src = net.x[:].rearrange("p (t d) -> p t d", d=D)
            for c in range(NCH):
                sp.dma_start(dst[:, c * TPC:(c + 1) * TPC], src[:, c * TPC:(c + 1) * TPC]).then_inc(stored, 16)
            sp.wait_ge(stored, 16 * NCH)


def rotary_attention(nc, net, tag, src, dest, router):
    with Scope(nc) as st:
        part = Part(nc, st, tag)
        q_parts, k_parts = (nc.dram_tensor(f"{tag}_{w}_parts", [NS, P, T], BF16, kind="Internal").ap() for w in "qk")
        net.v1 = part.sb("v1", [P, T // P, H * (HD + 1)])
        net.Q, net.K = part.sb("Q", [P, QRING, S], BF16), part.sb("K", [P, QRING, S], BF16)
        rope_stage(nc, net, tag + "_rope", src, q_parts, k_parts)
        attention_stage(nc, net, tag, dest, q_parts, k_parts, router)


def build(nc, ins, out):
    with Scope(nc) as st:
        net = open_net(nc, st, ins)
        l0 = Router(net.L0_rw, None, net.L0_b2)
        l2 = Router(net.L2_rw, net.L2_rb, net.L2_b2)
        experts = ExitStack()
        net.w1 = experts.enter_context(nc.sbuf_tensor("w1", [P, E, FF], F32))
        net.w2 = experts.enter_context(nc.sbuf_tensor("w2", [P, E, FC, D], F32))
        load_stage(nc, net, l0)
        src, dest = net.xnT
        stages = [lambda s, d: moe_stage(nc, net, "ffn0a", "L0", ACT.Gelu, s, d, None),
                  lambda s, d: head_mix_stage(nc, net, "mix0", s, d, l0),
                  lambda s, d: moe_stage(nc, net, "ffn0b", "L0", ACT.Gelu, s, d, None),
                  lambda s, d: swiglu_stage(nc, net, "ffn1a", s, d, None),
                  lambda s, d: rotary_attention(nc, net, "attn1", s, d, None),
                  lambda s, d: swiglu_stage(nc, net, "ffn1b", s, d, l2),
                  lambda s, d: moe_stage(nc, net, "ffn2a", "L2", ACT.Relu, s, d, None),
                  lambda s, d: decay_stage(nc, net, "decay2", s, d, l2),
                  lambda s, d: moe_stage(nc, net, "ffn2b", "L2", ACT.Relu, s, d, None),
                  lambda s, d: rwkv_ffn_stage(nc, net, "ffn3a", s, d),
                  lambda s, d: time_mix_stage(nc, net, "mix3", s, d),
                  lambda s, d: rwkv_ffn_stage(nc, net, "ffn3b", s, None),
                  ]
        for n, stage in enumerate(stages[:STAGES]):
            if n == 9:
                experts.close()
            stage(src, dest)
            src, dest = dest, src
        experts.close()
        store_stage(nc, net, out)


def lay_out(inputs):
    g = {k: np.asarray(v) for k, v in inputs.items()}
    a = {"x": g["L0_attn_x"].reshape(T, D)}

    def rows(w):
        return np.ascontiguousarray(w)
    a["L0_w1"] = rows(g["L0_ffn_w1"].transpose(2, 0, 1))
    a["L0_b1"] = rows(g["L0_ffn_b1"].reshape(E * FC, P).T)
    a["L0_w2"] = rows(g["L0_ffn_w2"].reshape(E, D, FC, P).transpose(3, 0, 2, 1))
    a["L0_b2"] = g["L0_ffn_b2"]
    a["L0_rw"] = rows(g["L0_ffn_router_w"].T)
    a["L2_w1"] = rows(g["L2_ffn_w1"].transpose(1, 0, 2))
    a["L2_b1"] = rows(g["L2_ffn_b1"].reshape(E * FC, P).T)
    a["L2_w2"] = rows(g["L2_ffn_w2"].reshape(E, FC, P, D).transpose(2, 0, 1, 3))
    a["L2_b2"] = g["L2_ffn_b2"]
    a["L2_rw"] = g["L2_ffn_router_w"]
    a["L2_rb"] = g["L2_ffn_router_b"]
    a["L0_wqkv"] = np.concatenate([g["L0_attn_Wq"].T, g["L0_attn_Wk"].T, g["L0_attn_Wv"].T], axis=1)
    a["L0_wfc"] = g["L0_attn_Wfc"].T
    a["L1_wg"] = g["L1_ffn_w_gate"].T
    a["L1_wu"] = g["L1_ffn_w_up"].T
    a["L1_wd"] = g["L1_ffn_w_down"].T.reshape(HC, P, D).transpose(1, 0, 2)
    w = g["L1_attn_w_qkv"]
    half = np.concatenate([np.arange(1, HD, 2), np.arange(0, HD, 2)])
    turned = (np.arange(H)[:, None] * HD + half[None, :]).reshape(-1)
    wq, wk = w[:, 0:D], w[:, D:2 * D]
    a["L1_wqk"] = np.stack([wq, wq[:, turned], wk, wk[:, turned]], axis=1)
    a["L1_wv"] = w[:, 2 * D:3 * D]
    a["L1_wout"] = g["L1_attn_w_out"]
    a["L1_bout"] = g["L1_attn_b_out"]
    a["L2_wq"] = g["L2_attn_Wq"].T
    a["L2_wkv"] = np.concatenate([g["L2_attn_Wk"].T, g["L2_attn_Wv"].T], axis=1)
    a["L2_bq"], a["L2_bk"] = g["L2_attn_bq"].reshape(D, 1), g["L2_attn_bk"].reshape(D, 1)
    a["L2_bk_row"], a["L2_bv_row"] = g["L2_attn_bk"], g["L2_attn_bv"]
    a["gamma"] = g["L2_attn_gamma"].reshape(1)
    a["L3_fr"], a["L3_fk"], a["L3_fv"] = g["L3_ffn_W_r"].T, g["L3_ffn_W_k"].T, g["L3_ffn_W_v"].T
    a["L3_mu_r"], a["L3_mu_k"] = g["L3_ffn_mu_r"].reshape(D, 1), g["L3_ffn_mu_k"].reshape(D, 1)
    for k in ("r", "k", "v", "g", "o"):
        a["L3_" + k] = g["L3_attn_W_" + k]
    a["L3_v_rep"] = np.stack([np.repeat(g["L3_attn_W_v"][:, j::HD], HD, axis=1) for j in range(HD)])
    a["L3_w1"], a["L3_w2"] = g["L3_attn_time_maa_w1"], g["L3_attn_time_maa_w2"]
    a["L3_dw1"], a["L3_dw2"] = g["L3_attn_time_decay_w1"], g["L3_attn_time_decay_w2"]
    a["L3_vecs"] = np.stack([g["L3_attn_" + k].reshape(D) for k in (
        "time_decay", "time_faaaa", "ln_gamma", "ln_beta", "time_maa_x", "time_maa_w", "time_maa_k", "time_maa_v",
        "time_maa_r", "time_maa_g")], axis=1)
    t, head = np.arange(P), np.arange(D) // HD
    exponents = np.concatenate([np.maximum(t[None, :] - t[:, None], 0), np.tile(t + 1, (P, 1)),
                                (P - 1 - t)[:, None], np.full((P, 1), P)], axis=1)
    a["bits"] = np.stack([exponents >> k & 1 for k in range(NEXP)], axis=1).astype(np.float32)
    a["nbits"] = np.stack([1 - (exponents >> k & 1) for k in range(NEXP)], axis=1).astype(np.float32)
    a["causal"] = (t[None, :] >= t[:, None]).astype(np.float32)
    same = (head[:, None] == head[None, :]).astype(np.float32)
    a["L3_blockones"], a["L3_blockmean"] = same, same / np.float32(HD)
    a["L3_center"] = np.eye(D, dtype=np.float32) - same / np.float32(HD)
    a["sel"] = np.stack([same * (np.arange(D) % HD == j) for j in range(HD)], axis=1).astype(np.float32)
    freqs = np.float32(10000.0) ** (-np.arange(0, HD, 2, dtype=np.float32) / np.float32(HD))
    angles = np.arange(S, dtype=np.float32)[:, None] * freqs
    sign = np.where(np.arange(HD) < HD // 2, -1.0, 1.0).astype(np.float32)
    a["cos"] = np.tile(np.repeat(np.cos(angles), 2, axis=1).T, (H, 1))
    a["sin"] = np.tile(np.repeat(np.sin(angles), 2, axis=1).T * sign[:, None], (H, 1))
    f, e = np.divmod(np.arange(HPB * (HD + 1)), HD + 1)
    a["pv_sel"] = (np.arange(P)[:, None] % (HPB * VCOL) == (f * VCOL + e)[None, :]).astype(np.float32)
    a["ident"] = np.eye(P, dtype=np.float32)
    a["rev"] = np.tile(np.arange(E, 0, -1, dtype=np.float32), (P, 1))
    return a


def kernel(**inputs):
    import concourse.bacc as bacc
    from concourse.bass_utils import run_bass_kernel_spmd as run

    nc = bacc.Bacc("TRN2", target_bir_lowering=False, num_devices=1)
    arrays, ins = {}, {}
    for name, a in lay_out(inputs).items():
        arrays[f"in_{name}"] = np.ascontiguousarray(a)
        ins[name] = nc.dram_tensor(f"in_{name}", list(a.shape), mybir.dt.from_np(a.dtype), kind="ExternalInput").ap()
    out = nc.dram_tensor("out_x", (T, D), F32, kind="ExternalOutput").ap()
    build(nc, ins, out)
    r = run(nc, [arrays], core_ids=[0])
    return r.results[0]["out_x"].reshape(B, S, D)
```

```python
from contextlib import ExitStack

import numpy as np
import concourse.bass as bass
import concourse.mybir as mybir

F32 = mybir.dt.float32
BF16 = mybir.dt.bfloat16
I32 = mybir.dt.int32
ALU = mybir.AluOpType
ACT = mybir.ActivationFunctionType
AX = mybir.AxisListType

P = 128
B, S, D = 4, 1024, 128
T = B * S
CH = 512
TPC = CH // P
NCH = T // CH
E = 8
FF = 512
FC = FF // P
LN_EPS = 1e-5
STAGES = 12


def need(eng, sem, count):
    if isinstance(count, int) and count <= 0:
        return
    eng.wait_ge(sem, count)


def bcast(ap, shape):
    return ap.broadcast_to(shape)


def per_token(ap, n):
    return bcast(ap[:].rearrange("p (t a) -> p t a", a=1), [P, TPC, n])


class Chain:

    def __init__(self, eng, sem, start):
        self.eng, self.sem, self.count = eng, sem, start

    def then(self, ins):
        ins.then_inc(self.sem, 1)
        self.count = self.count + 1

    def wait(self):
        need(self.eng, self.sem, self.count)


class Scope(ExitStack):

    def __init__(self, nc):
        super().__init__()
        self.nc, self.sems = nc, []
        self.callback(self.clear)

    def clear(self):
        if self.sems:
            self.nc.clear_and_free_semaphores(self.sems)
            self.nc.all_engine_barrier()

    def sem(self, name):
        self.sems.append(self.nc.alloc_semaphore(name))
        return self.sems[-1]


class Net:
    pass


def open_net(nc, st, ins):
    n = Net()
    n.ins = ins

    def sb(name, shape, dt=F32):
        return st.enter_context(nc.sbuf_tensor(name, shape, dt))

    n.x = sb("x", [P, T])
    n.xnT = [sb("xnT0", [P, T]), sb("xnT1", [P, T])]
    n.gates = sb("gates", [P, T // P * E])
    n.ident = sb("ident", [P, P])
    n.rev = sb("rev", [P, E])
    n.nhalf = sb("nhalf", [P, TPC])
    n.euler = sb("euler", [P, TPC])
    n.bank = [st.enter_context(nc.psum_tensor(f"bank{i}", [P, 512], F32)) for i in range(8)]
    n.L0_b1, n.L2_b1 = sb("L0_b1", [P, E * FC]), sb("L2_b1", [P, E * FC])
    n.L0_b2, n.L2_b2 = sb("L0_b2", [E, D]), sb("L2_b2", [E, D])
    n.L0_rw, n.L2_rw = sb("L0_rw", [P, E]), sb("L2_rw", [P, E])
    n.L2_rb = sb("L2_rb", [P, E])
    n.L0_wqkv = sb("L0_wqkv", [P, 3 * D])
    n.L1_wqk = sb("L1_wqk", [P, 4, D])
    n.L1_wv, n.L1_wout, n.L1_bout = sb("L1_wv", [P, D]), sb("L1_wout", [P, D]), sb("L1_bout", [P, D])
    n.L0_wfc = sb("L0_wfc", [P, D])
    n.L2_wq, n.L2_wkv = sb("L2_wq", [P, D]), sb("L2_wkv", [P, 2 * D])
    n.L2_bq, n.L2_bk = sb("L2_bq", [P, 1]), sb("L2_bk", [P, 1])
    n.L2_bk_row, n.L2_bv_row = sb("L2_bk_row", [P, D]), sb("L2_bv_row", [P, D])
    n.L3_fr, n.L3_fk, n.L3_fv = sb("L3_fr", [P, D]), sb("L3_fk", [P, D]), sb("L3_fv", [P, D])
    n.L3_mu_r, n.L3_mu_k = sb("L3_mu_r", [P, 1]), sb("L3_mu_k", [P, 1])
    n.L1_wg_int, n.L1_wg = sb("L1_wg_int", [P, HID], I32), sb("L1_wg", [P, HID])
    n.L1_wu_int, n.L1_wu = sb("L1_wu_int", [P, HID], I32), sb("L1_wu", [P, HID])
    n.L1_wd_int, n.L1_wd = sb("L1_wd_int", [P, HC, D], I32), sb("L1_wd", [P, HC, D])
    return n



class Norm:

    def __init__(self, nc, st, net, tag, dest, route, across=False, settled=False):
        self.across, self.settled = across, settled

        def sb(name, shape):
            return st.enter_context(nc.sbuf_tensor(f"{tag}_norm_{name}", shape, F32))

        def sem(name):
            return st.sem(f"{tag}_norm_{name}")
        self.nc, self.net, self.dest, self.route = nc, net, dest, route
        self.xc = sb("xc", [P, TPC, D])
        self.sq = sb("sq", [P, TPC, D])
        self.mean = sb("mean", [P, TPC])
        self.var = sb("var", [P, TPC])
        self.ve = sb("var_eps", [P, TPC])
        self.rstd = sb("rstd", [P, TPC])
        self.xn = sb("xn", [P, CH])
        self.xs = sb("xs", [P, CH])
        self.tbank, self.rbank = net.bank[6], net.bank[7]
        self.var_ready, self.rstd_ready, self.xn_ready = sem("var_ready"), sem("rstd_ready"), sem("xn_ready")
        self.turned, self.kept, self.x_whole = sem("turned"), sem("kept"), sem("x_whole")
        self.own = sem("dve_norm_step")
        if route:
            self.own_route = sem("dve_route_step")
            self.lg, self.eq, self.one1, self.one2, self.lg2, self.g1 = (
                sb(k, [P, TPC, E]) for k in ("logits", "equal", "one_hot1", "one_hot2", "logits2", "gates1"))
            self.m1, self.m2, self.f1, self.f2, self.gap, self.ex, self.den, self.p1, self.p2 = (
                sb(k, [P, TPC]) for k in ("top1", "top2", "rank1", "rank2", "gap", "exp", "den", "p1", "p2"))
            self.gs = sb("gs", [P, TPC, E])
            self.gT = sb("gT", [E, CH])
            (self.logits_ready, self.gap_ready, self.grown, self.gates_ready, self.gates_turned, self.gates_kept,
             self.bias_ready, self.bias_added) = (sem(k) for k in (
                 "logits_ready", "gap_ready", "grown", "gates_ready", "gates_turned", "gates_kept", "bias_ready",
                 "bias_added"))

    def view(self, t, c, width=D):
        if self.across:
            return t[:].rearrange("p (b n d) -> p b n d", b=B, d=width)[:, :, bass.ds(c, 1), :].rearrange(
                "p b n d -> p b (n d)")
        return t[:, bass.ds(c * TPC * width, TPC * width)].rearrange("p (t d) -> p t d", d=width)

    def stats(self, dve, c):
        nc = self.nc
        x = self.view(self.net.x, c)
        own = Chain(dve, self.own, c * 5)
        own.then(nc.vector.tensor_scalar(self.sq[:], x, 1.0 / D, None, ALU.mult))
        own.wait()
        own.then(nc.vector.tensor_reduce(self.mean[:], self.sq[:], AX.X, ALU.add))
        own.wait()
        own.then(nc.vector.tensor_tensor(self.xc[:], x, per_token(self.mean, D), ALU.subtract))
        own.wait()
        own.then(nc.vector.tensor_tensor(self.sq[:], self.xc[:], self.xc[:], ALU.mult))
        own.wait()
        own.then(nc.vector.tensor_reduce(self.var[:], self.sq[:], AX.X, ALU.add))
        own.wait()
        if not self.settled:
            need(dve, self.rstd_ready, c)
        nc.vector.tensor_scalar(self.ve[:], self.var[:], 1.0 / D, LN_EPS, ALU.mult, ALU.add).then_inc(self.var_ready, 1)

    def apply(self, dve, c):
        nc = self.nc
        dve.wait_ge(self.rstd_ready, c + 1)
        if not self.settled:
            need(dve, self.turned, c)
        nc.vector.tensor_tensor(self.xn[:].rearrange("p (t d) -> p t d", d=D), self.xc[:], per_token(self.rstd, D),
                                ALU.mult).then_inc(self.xn_ready, 1)

    def pick(self, dve, c, bias):
        nc = self.nc
        own = Chain(dve, self.own_route, c * 19)
        rev = bcast(self.net.rev[:].rearrange("p (a e) -> p a e", a=1), [P, TPC, E])

        def first_of(logits, top, found, one):
            own.then(nc.vector.tensor_reduce(top[:], logits[:], AX.X, ALU.max))
            own.wait()
            own.then(nc.vector.tensor_tensor(self.eq[:], logits[:], per_token(top, E), ALU.is_equal))
            own.wait()
            own.then(nc.vector.tensor_tensor(self.eq[:], self.eq[:], rev, ALU.mult))
            own.wait()
            own.then(nc.vector.tensor_reduce(found[:], self.eq[:], AX.X, ALU.max))
            own.wait()
            own.then(nc.vector.tensor_tensor(one[:], rev, per_token(found, E), ALU.is_equal))
            own.wait()
        dve.wait_ge(self.logits_ready, c + 1)
        src = self.rbank[:, 0:TPC * E].rearrange("p (t e) -> p t e", e=E)
        if bias is None:
            own.then(nc.vector.tensor_copy(self.lg[:], src))
        else:
            b = bcast(bias[:].rearrange("p (a e) -> p a e", a=1), [P, TPC, E])
            own.then(nc.vector.tensor_tensor(self.lg[:], src, b, ALU.add))
        own.wait()
        first_of(self.lg, self.m1, self.f1, self.one1)
        own.then(nc.vector.scalar_tensor_tensor(self.lg2[:], self.one1[:], -1e30, self.lg[:], ALU.mult, ALU.add))
        own.wait()
        first_of(self.lg2, self.m2, self.f2, self.one2)
        need(dve, self.grown, c)
        nc.vector.tensor_tensor(self.gap[:], self.m2[:], self.m1[:], ALU.subtract).then_inc(self.gap_ready, 1)

    def weigh(self, dve, c):
        nc = self.nc
        own = Chain(dve, self.own_route, c * 19 + 12)
        dve.wait_ge(self.grown, c + 1)
        own.then(nc.vector.tensor_scalar(self.den[:], self.ex[:], 1.0, None, ALU.add))
        own.wait()
        own.then(nc.vector.reciprocal(self.p1[:], self.den[:]))
        own.wait()
        own.then(nc.vector.tensor_tensor(self.p2[:], self.ex[:], self.p1[:], ALU.mult))
        own.then(nc.vector.tensor_tensor(self.g1[:], self.one1[:], per_token(self.p1, E), ALU.mult))
        own.wait()
        own.then(nc.vector.tensor_tensor(self.lg2[:], self.one2[:], per_token(self.p2, E), ALU.mult))
        own.wait()
        own.then(nc.vector.tensor_tensor(self.g1[:], self.g1[:], self.lg2[:], ALU.add))
        own.wait()
        need(dve, self.gates_turned, c)
        nc.vector.tensor_scalar(self.gs[:], self.g1[:], 0.5, None, ALU.mult).then_inc(self.gates_ready, 1)
        own.then(nc.vector.tensor_scalar(self.view(self.net.gates, c, E), self.g1[:], 0.5, None, ALU.mult))
        own.wait()

    def add_bias(self, dve, c):
        x = self.view(self.net.x, c)
        dve.wait_ge(self.bias_ready, c + 1)
        bias = self.rbank[:].rearrange("p (t d) -> p t d", d=D)
        self.nc.vector.tensor_tensor(x, x, bias, ALU.add).then_inc(self.bias_added, 1)

    def rstd_pow(self, pool, c):
        pool.wait_ge(self.var_ready, c + 1)
        if not self.settled:
            need(pool, self.xn_ready, c)
        self.nc.gpsimd.tensor_tensor(self.rstd[:], self.ve[:], self.net.nhalf[:], ALU.pow).then_inc(self.rstd_ready, 1)

    def grow(self, pool, c):
        pool.wait_ge(self.gap_ready, c + 1)
        need(pool, self.gates_ready, c)
        self.nc.gpsimd.tensor_tensor(self.ex[:], self.net.euler[:], self.gap[:], ALU.pow).then_inc(self.grown, 1)

    def turn(self, pe, c):
        pe.wait_ge(self.xn_ready, c + 1)
        if not self.settled:
            need(pe, self.kept, c)
        for i in range(TPC):
            s = slice(i * P, (i + 1) * P)
            ins = self.nc.tensor.transpose(self.tbank[:, s], self.xn[:, s], self.net.ident[:])
        ins.then_inc(self.turned, 1)

    def logits(self, pe, c, rw):
        pe.wait_ge(self.kept, c + 1)
        need(pe, self.bias_added, c)
        for i in range(TPC):
            ins = self.nc.tensor.matmul(self.rbank[:, i * E:(i + 1) * E], self.xs[:, i * P:(i + 1) * P], rw[:],
                                        start=True, stop=True)
        ins.then_inc(self.logits_ready, 1)

    def turn_g(self, pe, c):
        pe.wait_ge(self.gates_ready, c + 1)
        for i in range(TPC):
            ins = self.nc.tensor.transpose(self.rbank[0:E, i * P:(i + 1) * P], self.gs[:, i, :], self.net.ident[:])
        ins.then_inc(self.gates_turned, 1)

    def bias(self, pe, c, b2):
        pe.wait_ge(self.gates_kept, c + 1)
        for i in range(TPC):
            s = slice(i * P, (i + 1) * P)
            ins = self.nc.tensor.matmul(self.rbank[:, s], self.gT[:, s], b2[:], start=True, stop=True)
        ins.then_inc(self.bias_ready, 1)

    def keep(self, act, c):
        act.wait_ge(self.turned, c + 1)
        if self.route:
            need(act, self.logits_ready, c)
        self.nc.scalar.activation(self.xs[:], self.tbank[:], ACT.Copy)
        self.nc.scalar.activation(self.view(self.dest, c), self.tbank[:].rearrange("p (t d) -> p t d", d=D),
                                  ACT.Copy).then_inc(self.kept, 1)

    def keep_g(self, act, c):
        act.wait_ge(self.gates_turned, c + 1)
        need(act, self.bias_ready, c)
        self.nc.scalar.activation(self.gT[:], self.rbank[0:E, :], ACT.Copy).then_inc(self.gates_kept, 1)

    def all_dve(self, dve, c, route_bias=None):
        self.stats(dve, c)
        self.apply(dve, c)
        if self.route:
            self.pick(dve, c, route_bias)
            self.weigh(dve, c)
            self.add_bias(dve, c)

    def all_pe(self, pe, c, rw=None, b2=None):
        self.turn(pe, c)
        if self.route:
            self.logits(pe, c, rw)
            self.turn_g(pe, c)
            self.bias(pe, c, b2)

    def all_act(self, act, c):
        self.keep(act, c)
        if self.route:
            self.keep_g(act, c)

    def all_pool(self, pool, c):
        self.rstd_pow(pool, c)
        if self.route:
            self.grow(pool, c)


def rounds(eng, body, tail=None, count=NCH):
    peeled = 2 if count == NCH else 1
    for c in range(peeled):
        body(c)
    with eng.Fori(peeled, count - 1) as c:
        body(c)
    body(count - 1)
    if tail:
        tail(count - 1)


def deep_rounds(eng, body, tail):
    body(0, 0)
    body(1, 1)
    body(2, 2)
    with eng.Fori(3, NCH - 1) as c:
        body(c, 2)
    body(NCH - 1, 2)
    tail(NCH - 1)


def is_last(c, count=NCH):
    return isinstance(c, int) and c == count - 1


def is_first(c):
    return isinstance(c, int) and c == 0


class Router:

    def __init__(self, rw=None, rb=None, b2=None):
        self.rw, self.rb, self.b2 = rw, rb, b2



def load_stage(nc, net, router):
    ins = net.ins
    with Scope(nc) as st:
        norm = Norm(nc, st, net, "ln0", net.xnT[0], True)
        x_first, x_loaded = st.sem("x_first_loaded"), st.sem("x_loaded")
        first_loaded = st.sem("first_weights_loaded")
        w_loaded, int_loaded = st.sem("weights_loaded"), st.sem("quantized_loaded")
        set_up = st.sem("constants_set")
        first = [(net.ident, ins["ident"]), (net.rev, ins["rev"]), (net.L0_rw, ins["L0_rw"]), (net.L0_b2, ins["L0_b2"])]
        small = [(net.L2_rw, ins["L2_rw"]), (net.L0_b1, ins["L0_b1"]), (net.L2_b1, ins["L2_b1"]),
                 (net.L2_b2, ins["L2_b2"]), (net.L0_wqkv, ins["L0_wqkv"]),
                 (net.L0_wfc, ins["L0_wfc"]), (net.L1_wqk, ins["L1_wqk"]), (net.L1_wv, ins["L1_wv"]),
                 (net.L1_wout, ins["L1_wout"])]
        small += [(net.L2_wq, ins["L2_wq"]), (net.L2_wkv, ins["L2_wkv"]), (net.L2_bq, ins["L2_bq"]),
                  (net.L2_bk, ins["L2_bk"]), (net.L3_fr, ins["L3_fr"]), (net.L3_fk, ins["L3_fk"]),
                  (net.L3_fv, ins["L3_fv"]), (net.L3_mu_r, ins["L3_mu_r"]), (net.L3_mu_k, ins["L3_mu_k"])]
        rows = [(net.L2_rb, ins["L2_rb"]), (net.L1_bout, ins["L1_bout"]),
                (net.L2_bk_row, ins["L2_bk_row"]), (net.L2_bv_row, ins["L2_bv_row"])]
        quantized = [(net.L1_wg_int, ins["L1_wg"]), (net.L1_wu_int, ins["L1_wu"]), (net.L1_wd_int, ins["L1_wd"])]
        big = [(net.w1, ins["L0_w1"]), (net.w2, ins["L0_w2"])]
        block = st.enter_context(nc.Block())

        @block.sync
        def _(sp):
            src = ins["x"].rearrange("(t p) d -> p t d", p=P)
            dst = net.x[:].rearrange("p (t d) -> p t d", d=D)
            for c in range(NCH):
                sp.dma_start(dst[:, c * TPC:(c + 1) * TPC], src[:, c * TPC:(c + 1) * TPC]).then_inc(
                    x_loaded if c else x_first, 16)
                if c == 0:
                    for t, src_w in first:
                        sp.dma_start(t[:], src_w).then_inc(first_loaded, 16)
            for t, src_w in quantized:
                sp.dma_start(t[:], src_w).then_inc(int_loaded, 16)
            for t, src_w in small:
                sp.dma_start(t[:], src_w).then_inc(w_loaded, 16)
            for t, src_w in rows:
                sp.dma_start(t[:], src_w.partition_broadcast(P)).then_inc(w_loaded, 16)
            sp.wait_ge(w_loaded, 16 * (len(small) + len(big) + len(rows)))

        def steps(eng, body, finish):
            body(0, 0)
            body(1, 1)
            with eng.Fori(2, NCH) as c:
                body(c, 2)
            finish(NCH - 1)

        @block.scalar
        def _(act):
            for dst, src in big:
                act.dma_start(dst[:], src).then_inc(w_loaded, 16)

            def body(c, depth):
                norm.keep(act, c)
                if depth > 0:
                    norm.keep_g(act, c - 1)
            steps(act, body, lambda c: norm.keep_g(act, c))

        @block.gpsimd
        def _(pool):
            nc.gpsimd.memset(net.nhalf[:], -0.5)
            nc.gpsimd.memset(net.euler[:], float(np.e)).then_inc(set_up, 1)
            pool.wait_ge(set_up, 1)

            def body(c, depth):
                norm.rstd_pow(pool, c)
                if depth > 0:
                    norm.grow(pool, c - 1)
            steps(pool, body, lambda c: norm.grow(pool, c))

        @block.tensor
        def _(pe):
            pe.wait_ge(first_loaded, 16 * len(first))

            def body(c, depth):
                if depth > 0:
                    norm.logits(pe, c - 1, router.rw)
                norm.turn(pe, c)
                if depth > 0:
                    norm.turn_g(pe, c - 1)
                    norm.bias(pe, c - 1, router.b2)

            def finish(c):
                norm.logits(pe, c, router.rw)
                norm.turn_g(pe, c)
                norm.bias(pe, c, router.b2)
            steps(pe, body, finish)

        @block.vector
        def _(dve):
            dve.wait_ge(first_loaded, 16 * len(first))
            dve.wait_ge(x_first, 16)

            def body(c, depth):
                if depth > 1:
                    norm.add_bias(dve, c - 2)
                norm.stats(dve, c)
                if depth > 0:
                    norm.pick(dve, c - 1, router.rb)
                norm.apply(dve, c)
                if depth == 0:
                    dve.wait_ge(x_loaded, 16 * (NCH - 1))
                else:
                    norm.weigh(dve, c - 1)

            def finish(c):
                norm.add_bias(dve, c - 1)
                norm.pick(dve, c, router.rb)
                norm.weigh(dve, c)
                norm.add_bias(dve, c)
                dve.wait_ge(int_loaded, 16 * len(quantized))
                for w_int, w in ((net.L1_wg_int, net.L1_wg), (net.L1_wu_int, net.L1_wu), (net.L1_wd_int, net.L1_wd)):
                    nc.vector.tensor_scalar(w[:], w_int[:], QSCALE, None, ALU.mult)
            steps(dve, body, finish)



def moe_stage(nc, net, tag, layer, func, src, dest, router):
    w1, b1, w2 = net.w1, net.L0_b1 if layer == "L0" else net.L2_b1, net.w2
    with Scope(nc) as st:
        norm = Norm(nc, st, net, tag, dest, router is not None)
        router = router or Router()
        hs = st.enter_context(nc.sbuf_tensor(f"{tag}_hs", [P, 2, FC, CH], F32))
        hid_ready, hid_used, y_ready, y_added = (st.sem(f"{tag}_{k}")
                                                 for k in ("hid_ready", "hid_used", "y_ready", "y_added"))
        hbank, ybank = net.bank[0:4], net.bank[4:6]
        block = st.enter_context(nc.Block())

        def over_chunks(eng, slot, tail):
            for c in range(2):
                for e in range(E):
                    slot(c, e, c > 0)
            with eng.Fori(2, NCH) as c:
                for e in range(E):
                    slot(c, e, True)
            tail(NCH - 1)

        @block.tensor
        def _(pe):
            def hidden(c, e):
                for f in range(FC):
                    need(pe, hid_used, (c * E + e - 1) * FC + f + 1)
                    nc.tensor.matmul(hbank[f][:], w1[:, e, f * P:(f + 1) * P], src[:, bass.ds(c * CH, CH)],
                                     start=True, stop=True).then_inc(hid_ready, 1)

            def down(c, e):
                pe.wait_ge(hid_used, (c * E + e + 1) * FC)
                need(pe, y_added, c * E + e - 1)
                for i in range(TPC):
                    for f in range(FC):
                        ins = nc.tensor.matmul(ybank[e % 2][:, i * P:(i + 1) * P], hs[:, e % 2, f, i * P:(i + 1) * P],
                                               w2[:, e, f, :], start=(f == 0), stop=(f == FC - 1))
                ins.then_inc(y_ready, 1)

            def slot(c, e, before):
                hidden(c, e)
                if e > 0:
                    down(c, e - 1)
                elif before:
                    down(c - 1, E - 1)
                if before and e == 2:
                    norm.turn(pe, c - 1)
                if before and norm.route:
                    if e == 3:
                        norm.logits(pe, c - 1, router.rw)
                    if e == 5:
                        norm.turn_g(pe, c - 1)
                    if e == 6:
                        norm.bias(pe, c - 1, router.b2)

            def tail(c):
                down(c, E - 1)
                norm.all_pe(pe, c, router.rw, router.b2)
            over_chunks(pe, slot, tail)

        @block.scalar
        def _(act):
            def slot(c, e, before):
                need(act, y_ready, c * E + e - 1)
                for f in range(FC):
                    act.wait_ge(hid_ready, (c * E + e) * FC + f + 1)
                    nc.scalar.activation(hs[:, e % 2, f, :], hbank[f][:], func,
                                         bias=b1[:, e * FC + f:e * FC + f + 1]).then_inc(hid_used, 1)
                if before and e == 2:
                    norm.keep(act, c - 1)
                if before and e == 5 and norm.route:
                    norm.keep_g(act, c - 1)
            over_chunks(act, slot, lambda c: norm.all_act(act, c))

        @block.gpsimd
        def _(pool):
            rounds(pool, lambda c: norm.all_pool(pool, c))

        @block.vector
        def _(dve):
            def add(c, e):
                dve.wait_ge(y_ready, c * E + e + 1)
                need(dve, y_added, c * E + e)
                for i in range(TPC):
                    xt = net.x[:, bass.ds(c * CH + i * P, P)]
                    ins = nc.vector.scalar_tensor_tensor(xt, ybank[e % 2][:, i * P:(i + 1) * P],
                                                         net.gates[:, bass.ds((c * TPC + i) * E + e, 1)], xt,
                                                         ALU.mult, ALU.add)
                ins.then_inc(y_added, 1)

            def slot(c, e, before):
                if e > 0:
                    add(c, e - 1)
                elif before:
                    add(c - 1, E - 1)
                    dve.wait_ge(y_added, c * E)
                    norm.stats(dve, c - 1)
                if before and e == 1:
                    norm.apply(dve, c - 1)
                if before and norm.route:
                    if e == 4:
                        norm.pick(dve, c - 1, router.rb)
                    if e == 5:
                        norm.weigh(dve, c - 1)
                    if e == 7:
                        norm.add_bias(dve, c - 1)

            def tail(c):
                add(c, E - 1)
                dve.wait_ge(y_added, (c + 1) * E)
                norm.all_dve(dve, c, router.rb)
            over_chunks(dve, slot, tail)



H = 16
HD = D // H


class Part:

    def __init__(self, nc, st, tag):
        self.nc, self.st, self.tag = nc, st, tag

    def sb(self, name, shape, dt=F32):
        return self.st.enter_context(self.nc.sbuf_tensor(f"{self.tag}_{name}", shape, dt))

    def sem(self, name):
        return self.st.sem(f"{self.tag}_{name}")


def head_mix_stage(nc, net, tag, src, dest, router):
    with Scope(nc) as st:
        norm = Norm(nc, st, net, tag, dest, True)
        part = Part(nc, st, tag)
        xa = part.sb("xa", [P, CH])
        qkv = part.sb("qkv", [P, TPC, 3 * D])
        prod = part.sb("prod", [P, H * H * HD])
        pool_qk, pool_pv = part.sb("pool_qk", [P, H * H * HD]), part.sb("pool_pv", [P, H * H * HD])
        qk_ready, pv_ready = part.sem("qk_ready"), part.sem("pv_ready")
        QK_TILES, PV_TILES = (2, 3), (0, 1, 2)
        logit = part.sb("logit", [P, 2, H * H])
        prob = part.sb("prob", [P, 2, H * H])
        top, den, rden = part.sb("top", [P, H]), part.sb("den", [P, H]), part.sb("rden", [P, H])
        mix = part.sb("mix", [P, D])
        mixed_tiles = part.sb("mixed", [P, CH])
        mixT = part.sb("mixT", [P, CH])
        xa_ready, qkv_ready, qkv_kept, logit_ready, exp_ready, mixed, own, mix_turned, mixT_kept, y_ready, y_added = (
            part.sem(k) for k in ("xa_ready", "qkv_ready", "qkv_kept", "logit_ready", "exp_ready", "tile_mixed",
                                  "dve_step", "mix_turned", "mixT_kept", "y_ready", "y_added"))
        wqkv, wfc = net.L0_wqkv, net.L0_wfc
        block = st.enter_context(nc.Block())

        @block.tensor
        def _(pe):
            def qkv_of(c):
                pe.wait_ge(xa_ready, c + 1)
                for i in range(TPC):
                    need(pe, qkv_kept, (c - 1) * TPC + i + 1)
                    nc.tensor.matmul(net.bank[i][:, 0:3 * D], xa[:, i * P:(i + 1) * P], wqkv[:],
                                     start=True, stop=True).then_inc(qkv_ready, 1)

            def project(c):
                pe.wait_ge(mixed, (c + 1) * TPC)
                need(pe, mixT_kept, c)
                for i in range(TPC):
                    s = slice(i * P, (i + 1) * P)
                    ins = nc.tensor.transpose(net.bank[4][:, s], mixed_tiles[:, s], net.ident[:])
                ins.then_inc(mix_turned, 1)
                pe.wait_ge(mixT_kept, c + 1)
                need(pe, y_added, c)
                for i in range(TPC):
                    s = slice(i * P, (i + 1) * P)
                    ins = nc.tensor.matmul(net.bank[5][:, s], mixT[:, s], wfc[:], start=True, stop=True)
                ins.then_inc(y_ready, 1)

            def body(c):
                if is_first(c):
                    qkv_of(0)
                else:
                    project(c - 1)
                    norm.turn(pe, c - 1)
                    norm.logits(pe, c - 1, router.rw)
                if not is_last(c):
                    qkv_of(c + 1)
                if not is_first(c):
                    norm.turn_g(pe, c - 1)
                    norm.bias(pe, c - 1, router.b2)

            def tail(c):
                project(c)
                norm.all_pe(pe, c, router.rw, router.b2)
            rounds(pe, body, tail)

        @block.scalar
        def _(act):
            def keep(c, i):
                act.wait_ge(qkv_ready, c * TPC + i + 1)
                need(act, mixed, (c - 1) * TPC + i + 1)
                nc.scalar.activation(qkv[:, i, :], net.bank[i][:, 0:3 * D], ACT.Copy).then_inc(qkv_kept, 1)

            def exp(c, i):
                need(act, mixed, c * TPC + i - 1)
                act.wait_ge(logit_ready, c * TPC + i + 1)
                nc.scalar.activation(prob[:, i % 2, :], logit[:, i % 2, :], ACT.Exp,
                                     scale=HD ** -0.5).then_inc(exp_ready, 1)

            def keep_mix(c):
                need(act, y_ready, c)
                act.wait_ge(mix_turned, c + 1)
                nc.scalar.activation(mixT[:], net.bank[4][:], ACT.Copy).then_inc(mixT_kept, 1)

            def body(c):
                before, after = not is_first(c), not is_last(c)
                if not before:
                    for i in range(TPC):
                        keep(0, i)
                exp(c, 0)
                if before:
                    keep_mix(c - 1)
                exp(c, 1)
                if before:
                    norm.keep(act, c - 1)
                exp(c, 2)
                if after:
                    keep(c + 1, 0)
                exp(c, 3)
                if after:
                    keep(c + 1, 1)
                if before:
                    norm.keep_g(act, c - 1)
                if after:
                    keep(c + 1, 2)
                    keep(c + 1, 3)

            def tail(c):
                keep_mix(c)
                norm.all_act(act, c)
            rounds(act, body, tail)

        def heads(ap):
            return ap.rearrange("p (h d) -> p h d", d=HD)

        def times_k(eng, to, i):
            q, k = heads(qkv[:, i, 0:D]), heads(qkv[:, i, D:2 * D])
            return eng.tensor_tensor(
                to[:].rearrange("p (h t d) -> p h t d", t=H, d=HD),
                bcast(q.rearrange("p h (a d) -> p h a d", a=1), [P, H, H, HD]),
                bcast(k.rearrange("p (a t) d -> p a t d", a=1), [P, H, H, HD]), ALU.mult)

        def times_v(eng, to, i):
            v = qkv[:, i, 2 * D:3 * D].rearrange("p (t d) -> p d t", d=HD)
            pr = prob[:, i % 2, :].rearrange("p (h t) -> p h t", t=H)
            return eng.tensor_tensor(
                to[:].rearrange("p (h d t) -> p h d t", t=H, d=HD),
                bcast(pr.rearrange("p h (a t) -> p h a t", a=1), [P, H, HD, H]),
                bcast(v.rearrange("p (a d) t -> p a d t", a=1), [P, H, HD, H]), ALU.mult)

        @block.gpsimd
        def _(pool):
            def qk(c, i):
                pool.wait_ge(qkv_kept, c * TPC + i + 1)
                need(pool, logit_ready, c * TPC + (0 if i == QK_TILES[0] else i))
                times_k(nc.gpsimd, pool_qk, i).then_inc(qk_ready, 1)

            def pv(c, i):
                pool.wait_ge(exp_ready, c * TPC + i + 1)
                need(pool, mixed, c * TPC + i if i else (c - 1) * TPC + PV_TILES[-1] + 1)
                times_v(nc.gpsimd, pool_pv, i).then_inc(pv_ready, 1)

            def body(c):
                before = not is_first(c)
                qk(c, 2)
                pv(c, 0)
                if before:
                    norm.rstd_pow(pool, c - 1)
                pv(c, 1)
                qk(c, 3)
                if before:
                    norm.grow(pool, c - 1)
                pv(c, 2)
            rounds(pool, body, lambda c: norm.all_pool(pool, c))

        @block.vector
        def _(dve):
            def per_head(ap, n):
                return bcast(ap[:].rearrange("p (h a) -> p h a", a=1), [P, H, n])

            def fetch(c):
                need(dve, qkv_ready, c * TPC)
                nc.vector.tensor_scalar(xa[:], src[:, bass.ds(c * CH, CH)], 1.0, None, ALU.mult).then_inc(xa_ready, 1)

            def score(chain, c, i):
                lg = logit[:, i % 2, :].rearrange("p (h t) -> p h t", t=H)
                if i in QK_TILES:
                    dve.wait_ge(qk_ready, c * len(QK_TILES) + QK_TILES.index(i) + 1)
                    p4 = pool_qk
                else:
                    dve.wait_ge(qkv_kept, c * TPC + i + 1)
                    chain.then(times_k(nc.vector, prod, i))
                    chain.wait()
                    p4 = prod
                need(dve, exp_ready, c * TPC + i - 1)
                chain.then(nc.vector.tensor_reduce(lg, p4[:].rearrange("p (h t d) -> p h t d", t=H, d=HD), AX.X, ALU.add))
                chain.wait()
                chain.then(nc.vector.tensor_reduce(top[:], lg, AX.X, ALU.max))
                chain.wait()
                nc.vector.tensor_tensor(lg, lg, per_head(top, H), ALU.subtract).then_inc(logit_ready, 1)

            def gather(chain, c, i):
                pr = prob[:, i % 2, :].rearrange("p (h t) -> p h t", t=H)
                dve.wait_ge(exp_ready, c * TPC + i + 1)
                chain.then(nc.vector.tensor_reduce(den[:], pr, AX.X, ALU.add))
                if i in PV_TILES:
                    dve.wait_ge(pv_ready, c * len(PV_TILES) + PV_TILES.index(i) + 1)
                    p4 = pool_pv
                else:
                    chain.then(times_v(nc.vector, prod, i))
                    p4 = prod
                chain.wait()
                nc.vector.reciprocal(rden[:], den[:])
                chain.then(nc.vector.tensor_reduce(heads(mix[:]), p4[:].rearrange("p (h d t) -> p h d t", t=H, d=HD),
                                                   AX.X, ALU.add))
                need(dve, mix_turned, c)
                chain.wait()
                nc.vector.tensor_tensor(heads(mixed_tiles[:, i * P:(i + 1) * P]), heads(mix[:]), per_head(rden, HD),
                                        ALU.mult).then_inc(mixed, 1)

            def add(c):
                x = net.x[:, bass.ds(c * CH, CH)]
                dve.wait_ge(y_ready, c + 1)
                nc.vector.tensor_tensor(x, x, net.bank[5][:], ALU.add).then_inc(y_added, 1)
                dve.wait_ge(y_added, c + 1)

            def body(c):
                before = not is_first(c)
                chain = Chain(dve, own, c * (TPC * 6 - len(QK_TILES) - len(PV_TILES)))
                if not before:
                    fetch(0)
                score(chain, c, 0)
                if not is_last(c):
                    fetch(c + 1)
                score(chain, c, 1)
                if before:
                    add(c - 1)
                    norm.stats(dve, c - 1)
                gather(chain, c, 0)
                if before:
                    norm.apply(dve, c - 1)
                score(chain, c, 2)
                gather(chain, c, 1)
                if before:
                    norm.pick(dve, c - 1, router.rb)
                score(chain, c, 3)
                if before:
                    norm.weigh(dve, c - 1)
                gather(chain, c, 2)
                gather(chain, c, 3)
                if before:
                    norm.add_bias(dve, c - 1)

            def tail(c):
                add(c)
                norm.all_dve(dve, c, router.rb)
            rounds(dve, body, tail)



HID = 384
HC = HID // P
QSCALE = float(np.float32(1.0 / 127.0))


def swiglu_stage(nc, net, tag, src, dest, router):
    with Scope(nc) as st:
        norm = Norm(nc, st, net, tag, dest, router is not None)
        router = router or Router()
        part = Part(nc, st, tag)
        sg = part.sb("silu", [P, 2, CH])
        hs = part.sb("hs", [P, HC, CH])
        gu_ready, silu_ready, h_ready, y_ready, y_added = (
            part.sem(k) for k in ("gate_up_ready", "silu_ready", "h_ready", "y_ready", "y_added"))
        block = st.enter_context(nc.Block())

        @block.tensor
        def _(pe):
            def gate_up(c, j):
                for w, banks in ((net.L1_wg, (0, 1, 0)), (net.L1_wu, (2, 3, 2))):
                    need(pe, h_ready, c * HC + (1 if j == 2 else 0))
                    ins = nc.tensor.matmul(net.bank[banks[j]][:], w[:, j * P:(j + 1) * P],
                                           src[:, bass.ds(c * CH, CH)], start=True, stop=True)
                ins.then_inc(gu_ready, 1)

            def down(c):
                pe.wait_ge(h_ready, (c + 1) * HC)
                need(pe, y_added, c)
                for i in range(TPC):
                    for j in range(HC):
                        ins = nc.tensor.matmul(net.bank[4][:, i * P:(i + 1) * P], hs[:, j, i * P:(i + 1) * P],
                                               net.L1_wd[:, j, :], start=(j == 0), stop=(j == HC - 1))
                ins.then_inc(y_ready, 1)

            def body(c, depth):
                gate_up(c, 2)
                if depth > 1 and norm.route:
                    norm.turn_g(pe, c - 2)
                if depth > 0:
                    norm.turn(pe, c - 1)
                if depth > 1 and norm.route:
                    norm.bias(pe, c - 2, router.b2)
                down(c)
                if depth > 0 and norm.route:
                    norm.logits(pe, c - 1, router.rw)
                if not is_last(c):
                    gate_up(c + 1, 0)
                    gate_up(c + 1, 1)

            def tail(c):
                if norm.route:
                    norm.turn_g(pe, c - 1)
                    norm.bias(pe, c - 1, router.b2)
                norm.all_pe(pe, c, router.rw, router.b2)
            gate_up(0, 0)
            gate_up(0, 1)
            deep_rounds(pe, body, tail)

        @block.scalar
        def _(act):
            def silu(c, j):
                need(act, h_ready, c * HC + j - 1)
                act.wait_ge(gu_ready, c * HC + j + 1)
                nc.scalar.activation(sg[:, j % 2, :], net.bank[(0, 1, 0)[j]][:], ACT.Silu).then_inc(silu_ready, 1)

            def body(c, depth):
                silu(c, 0)
                silu(c, 1)
                silu(c, 2)
                if depth > 1 and norm.route:
                    norm.keep_g(act, c - 2)
                if depth > 0:
                    norm.keep(act, c - 1)

            def tail(c):
                if norm.route:
                    norm.keep_g(act, c - 1)
                norm.all_act(act, c)
            deep_rounds(act, body, tail)

        @block.gpsimd
        def _(pool):
            rounds(pool, lambda c: norm.all_pool(pool, c))

        @block.vector
        def _(dve):
            def mult(c, j):
                need(dve, y_ready, c)
                dve.wait_ge(silu_ready, c * HC + j + 1)
                nc.vector.tensor_tensor(hs[:, j, :], sg[:, j % 2, :], net.bank[(2, 3, 2)[j]][:],
                                        ALU.mult).then_inc(h_ready, 1)

            def add(c):
                x = net.x[:, bass.ds(c * CH, CH)]
                dve.wait_ge(y_ready, c + 1)
                nc.vector.scalar_tensor_tensor(x, net.bank[4][:], 0.5, x, ALU.mult, ALU.add).then_inc(y_added, 1)
                dve.wait_ge(y_added, c + 1)

            def body(c, depth):
                before, gates = depth > 0, depth > 1 and norm.route
                mult(c, 0)
                if gates:
                    norm.weigh(dve, c - 2)
                mult(c, 1)
                if before:
                    norm.apply(dve, c - 1)
                mult(c, 2)
                if gates:
                    norm.add_bias(dve, c - 2)
                add(c)
                norm.stats(dve, c)
                if before and norm.route:
                    norm.pick(dve, c - 1, router.rb)

            def tail(c):
                if norm.route:
                    norm.weigh(dve, c - 1)
                norm.apply(dve, c)
                if norm.route:
                    norm.add_bias(dve, c - 1)
                    norm.pick(dve, c, router.rb)
                    norm.weigh(dve, c)
                    norm.add_bias(dve, c)
            deep_rounds(dve, body, tail)



HPB = S // CH
TPB = S // P
SLOTS_Q = (0, 0, 1, 1, 0, 2)
SLOTS_K = (0, 1, 0, 1, 2, 0)
NS = len(SLOTS_Q)
KROWS = NS * HD
MROW0 = 96
QRING = 4
MROWS = 3
VCOL = 32


def rope_stage(nc, net, tag, src, q_parts, k_parts):
    with Scope(nc) as st:
        part = Part(nc, st, tag)
        xa = part.sb("xa", [P, CH])
        cos, sin = part.sb("cos", [P, S]), part.sb("sin", [P, S])
        rot = {w: part.sb(f"{w}_cos", [P, CH]) for w in "qk"}
        rot2 = {w: part.sb(f"{w}_sin", [P, CH]) for w in "qk"}
        full = {w: part.sb(f"{w}_full", [P, 3, CH]) for w in "qk"}
        split = {w: part.sb(f"{w}_parts", [P, 2, 3, CH], BF16) for w in "qk"}
        tables, xa_ready, qkv_ready, part_in, part_out, v_kept, own = (
            part.sem(k) for k in ("tables_loaded", "xa_ready", "qkv_ready", "part_in", "part_out",
                                  "v_kept", "dve_step"))
        stored = [part.sem(f"parts_stored{hf}") for hf in range(HPB)]
        experts = part.sem("experts_loaded")
        NST = 2 * NS
        block = st.enter_context(nc.Block())

        def batches(eng, body):
            for hf in range(HPB):
                body(hf, 0, hf)
            with eng.Fori(1, B) as b:
                for hf in range(HPB):
                    body(b * HPB + hf, b, hf)

        @block.sync
        def _(sp):
            sp.dma_start(cos[:], net.ins["cos"]).then_inc(tables, 16)
            sp.dma_start(sin[:], net.ins["sin"]).then_inc(tables, 16)

            def body(c, b, hf):
                for p in range(3):
                    for n, (w, dst, slots) in enumerate((("q", q_parts, SLOTS_Q), ("k", k_parts, SLOTS_K))):
                        sp.wait_ge(part_out, c * 6 + 2 * p + n + 1)
                        for i in range(NS):
                            if slots[i] == p:
                                sp.dma_start(dst[i, :, bass.ds(c * CH, CH)], split[w][:, hf, p, :]).then_inc(
                                    stored[hf], 16)
            batches(sp, body)
            for hf in range(HPB):
                sp.wait_ge(stored[hf], 16 * NST * B)

        @block.gpsimd
        def _(pool):
            pool.dma_start(net.w1[:], net.ins["L2_w1"]).then_inc(experts, 16)
            pool.dma_start(net.w2[:], net.ins["L2_w2"]).then_inc(experts, 16)
            pool.wait_ge(experts, 32)

        @block.tensor
        def _(pe):
            def body(c, b, hf):
                need(pe, own, 2 * c)
                xc = src[:, bass.ds(c * CH, CH)]
                for n in range(4):
                    nc.tensor.matmul(net.bank[n][:], net.L1_wqk[:, n, :], xc, start=True, stop=True).then_inc(qkv_ready, 1)
                need(pe, v_kept, c)
                pe.wait_ge(xa_ready, c + 1)
                for i in range(TPC):
                    t = slice(i * P, (i + 1) * P)
                    ins = nc.tensor.matmul(net.bank[4][:, t], xa[:, t], net.L1_wv[:], start=True, stop=True)
                ins.then_inc(qkv_ready, 1)
            batches(pe, body)

        @block.scalar
        def _(act):
            def body(c, b, hf):
                need(act, stored[hf], 16 * NST * b)
                for p in range(3):
                    for n, w in enumerate("qk"):
                        act.wait_ge(part_in, c * 6 + 2 * p + n + 1)
                        nc.scalar.activation(split[w][:, hf, p, :], full[w][:, p, :], ACT.Copy).then_inc(part_out, 1)
            batches(act, body)

        @block.vector
        def _(dve):
            nc.vector.memset(net.v1[:], 1.0)
            nc.vector.memset(net.K[:], 1.0)
            nc.vector.memset(net.Q[:], 0.0)
            dve.wait_ge(tables, 32)

            def body(c, b, hf):
                chain = Chain(dve, own, c * 2)
                need(dve, qkv_ready, 5 * c)
                nc.vector.tensor_scalar(xa[:], src[:, bass.ds(c * CH, CH)], 1.0, None, ALU.mult).then_inc(xa_ready, 1)
                pos = slice(hf * CH, (hf + 1) * CH)
                for n, w in enumerate("qk"):
                    dve.wait_ge(qkv_ready, 5 * c + 2 * n + 2)
                    nc.vector.tensor_tensor(rot[w][:], net.bank[2 * n][:], cos[:, pos], ALU.mult)
                    chain.then(nc.vector.tensor_tensor(rot2[w][:], net.bank[2 * n + 1][:], sin[:, pos], ALU.mult))
                    need(dve, part_out, 6 * c)
                    chain.wait()
                    ins = nc.vector.tensor_tensor(full[w][:, 0, :], rot[w][:], rot2[w][:], ALU.add)
                    ins.then_inc(part_in, 1)
                dve.wait_ge(qkv_ready, 5 * c + 5)
                for i in range(TPC):
                    ins = nc.vector.tensor_scalar(
                        net.v1[:].rearrange("p t (h e) -> p (t h) e", e=HD + 1)[:, bass.ds((c * TPC + i) * H, H), 0:HD],
                        net.bank[4][:, i * P:(i + 1) * P].rearrange("p (h d) -> p h d", d=HD), 1.0, None, ALU.mult)
                ins.then_inc(v_kept, 1)
                for p in range(2):
                    for n, w in enumerate("qk"):
                        dve.wait_ge(part_in, 6 * c + 2 * p + n + 1)
                        dve.wait_ge(part_out, 6 * c + 2 * p + n + 1)
                        ins = nc.vector.tensor_tensor(full[w][:, p + 1, :], full[w][:, p, :], split[w][:, hf, p, :],
                                                      ALU.subtract)
                        ins.then_inc(part_in, 1)
            batches(dve, body)


def attention_stage(nc, net, tag, dest, q_parts, k_parts, router):
    with Scope(nc) as st:
        assert router is None
        norm = Norm(nc, st, net, tag, dest, False, settled=True)
        part = Part(nc, st, tag)
        RING = 4
        PAIRS = TPB // 2
        AHEAD = H - 2
        pT = part.sb("pT", [P, RING, S])
        mx = part.sb("mx", [P, 2, TPB, HPB])
        nm = part.sb("nm", [P, 2, TPB])
        rem = part.sb("m_rem", [TPB, 3, P])
        mparts = part.sb("m_parts", [TPB, 2, 3, P], BF16)
        rd = part.sb("rden", [P, 2, TPB])
        vb = part.sb("vb", [P, H, TPB, VCOL])
        sums = part.sb("sums", [P, 2, CH])
        pv_sel = part.sb("pv_sel", [P, HPB * (HD + 1)])
        o = part.sb("o", [P, TPB, D])
        oT = part.sb("oT", [P, S])
        loaded = [part.sem(f"loaded{n}") for n in range(QRING)]
        m_rows = [part.sem(f"m_rows{n}") for n in range(2)]
        (sel_loaded, v_ready, a_ready, a_used, nm_ready, nm_turned, m_ready, s_ready, exp_ready, pv_step, sums_kept,
         gathered, o_ready, round_step, rem_step, over_step, o_turned, oT_kept, y_ready, y_added) = (part.sem(k) for k in (
             "sel_loaded", "v_ready", "a_ready", "a_used", "nm_ready", "nm_turned", "m_ready", "s_ready", "exp_ready",
             "pv_step", "sums_kept", "gathered", "o_ready", "round_step", "rem_step", "over_step", "o_turned", "oT_kept",
             "y_ready", "y_added"))
        a_bank, s_bank, pv_bank, small_bank, y_bank = net.bank[0:2], net.bank[2:4], net.bank[4:6], net.bank[6], net.bank[7]
        norm.tbank = y_bank
        nm_rows = small_bank[0:TPB, 0:P]
        GW = TPC * HPB * (HD + 1)
        block = st.enter_context(nc.Block())

        def slot(t, h, rows):
            return t[0:rows, h % QRING, :]

        def gather_bank(h):
            return small_bank[:, P + GW * (h % 2):P + GW * (h % 2 + 1)]

        def ahead(b, h):
            if h < H:
                return b, h
            return None if is_last(b, B) else (b + 1, h - H)

        def before(b, h):
            if h > 0:
                return b, h - 1
            return None if is_first(b) else (b - 1, H - 1)

        @block.sync
        def _(sp):
            def load(b, h):
                for parts, t in ((q_parts, net.Q), (k_parts, net.K)):
                    sp.dma_start(slot(t, h, KROWS), parts[:, h * HD:(h + 1) * HD, bass.ds(b * S, S)]).then_inc(
                        loaded[h % QRING], 16)

            def rows(b, h):
                sp.wait_ge(m_ready, b * H + h + 1)
                for n in range(MROWS):
                    row = MROW0 + n
                    dst = net.Q[row:row + 1, h % QRING, :].rearrange("r (a t) -> r a t", t=P)
                    sp.dma_start(dst, mparts[:, h % 2, n, :]).then_inc(m_rows[h % 2], 16)

            def body(b):
                for h in range(H):
                    rows(b, h)
                    fetched = ahead(b, h + QRING - 1)
                    if fetched:
                        need(sp, s_ready, (b * H + h) * TPB * HPB)
                        load(*fetched)
            sp.dma_start(pv_sel[:], net.ins["pv_sel"]).then_inc(sel_loaded, 16)
            for h in range(QRING - 1):
                load(0, h)
            rounds(sp, body, count=B)
            for n in range(QRING):
                sp.wait_ge(loaded[n], 32 * B * H // QRING)
            for n in range(2):
                sp.wait_ge(m_rows[n], 16 * MROWS * B * H // 2)

        @block.tensor
        def _(pe):
            def big(b, h, qt, hf):
                if qt == 0 and hf == 0:
                    pe.wait_ge(loaded[h % QRING], (b * (H // QRING) + h // QRING + 1) * 32)
                n = ((b * H + h) * TPB + qt) * HPB + hf
                need(pe, a_used, n - 1)
                nc.tensor.matmul(a_bank[hf][:], slot(net.Q, h, MROW0)[:, qt * P:(qt + 1) * P],
                                 slot(net.K, h, MROW0)[:, hf * CH:(hf + 1) * CH], start=True, stop=True).then_inc(a_ready, 1)

            def turn(b, h):
                pe.wait_ge(nm_ready, b * H + h + 1)
                need(pe, m_ready, b * H + h)
                need(pe, o_ready, b * H + h - 2)
                nc.tensor.transpose(nm_rows, nm[:, h % 2, :], net.ident[:]).then_inc(nm_turned, 1)

            def small(b, h, kt, hf):
                if kt == 0 and hf == 0:
                    pe.wait_ge(m_rows[h % 2], (b * (H // 2) + h // 2 + 1) * 16 * MROWS)
                n = ((b * H + h) * TPB + kt) * HPB + hf
                need(pe, exp_ready, n - 1)
                nc.tensor.matmul(s_bank[hf][:], slot(net.K, h, MROW0 + MROWS)[:, kt * P:(kt + 1) * P],
                                 slot(net.Q, h, MROW0 + MROWS)[:, hf * CH:(hf + 1) * CH],
                                 start=True, stop=True).then_inc(s_ready, 1)

            def pv(b, h, pair):
                if pair == 0:
                    pe.wait_ge(v_ready, b * H + h + 1)
                    need(pe, sums_kept, b * H + h - 1)
                pe.wait_ge(exp_ready, ((b * H + h) * TPB + 2 * pair + 2) * HPB)
                for odd in range(2):
                    kt = 2 * pair + odd
                    for hf in range(HPB):
                        at = (odd * HPB + hf) * VCOL
                        ins = nc.tensor.matmul(pv_bank[h % 2][at:at + VCOL, :], vb[:, h, kt, :],
                                               pT[:, kt % RING, hf * CH:(hf + 1) * CH],
                                               start=(pair == 0), stop=(pair == PAIRS - 1),
                                               skip_group_check=True)
                ins.then_inc(pv_step, 1)

            def gather(b, h):
                if is_first(b) and h == 0:
                    pe.wait_ge(sel_loaded, 16)
                pe.wait_ge(sums_kept, b * H + h + 1)
                need(pe, o_ready, b * H + h)
                if ahead(b, h + 2):
                    pe.wait_ge(round_step, (b * H + h + 2) * 3 + 2)
                W = HPB * (HD + 1)
                for i in range(TPC):
                    ins = nc.tensor.matmul(gather_bank(h)[:, i * W:(i + 1) * W], sums[:, h % 2, i * P:(i + 1) * P],
                                           pv_sel[:], start=True, stop=True)
                ins.then_inc(gathered, 1)

            def turn_o(b, hf):
                if hf == 0:
                    pe.wait_ge(o_ready, (b + 1) * H)
                else:
                    pe.wait_ge(oT_kept, b * HPB + 1)
                for i in range(TPC):
                    ins = nc.tensor.transpose(y_bank[:, i * P:(i + 1) * P], o[:, i * HPB + hf, :], net.ident[:])
                ins.then_inc(o_turned, 1)

            def project(b, hf):
                pe.wait_ge(oT_kept, (b + 1) * HPB)
                if hf == 1:
                    pe.wait_ge(norm.kept, b * HPB + 1)
                for i in range(TPC):
                    t = slice(hf * CH + i * P, hf * CH + (i + 1) * P)
                    ins = nc.tensor.matmul(y_bank[:, i * P:(i + 1) * P], oT[:, t], net.L1_wout[:], start=True, stop=True)
                ins.then_inc(y_ready, 1)

            def end_of_sequence(b, h, kt):
                if (h, kt) in ((1, 3), (1, 6)):
                    turn_o(b, (1, 3) != (h, kt))
                if (h, kt) in ((2, 4), (6, 4)):
                    project(b, h // 6)
                if (h, kt) in ((5, 4), (9, 4)):
                    norm.turn(pe, b * HPB + h // 9)

            def body(b):
                if is_first(b):
                    for h in range(2):
                        for qt in range(TPB):
                            for hf in range(HPB):
                                big(b, h, qt, hf)
                        if h == 0:
                            turn(b, h)
                for h in range(H):
                    fetched, last, turned = ahead(b, h + 2), before(b, h), ahead(b, h + 1)
                    for kt in range(TPB):
                        for hf in range(HPB):
                            if fetched:
                                big(*fetched, kt, hf)
                            small(b, h, kt, hf)
                        if kt == 0 and last:
                            pv(*last, PAIRS - 1)
                        if kt == 1 and turned:
                            turn(*turned)
                        if kt >= 2 and kt % 2 == 0:
                            pv(b, h, kt // 2 - 1)
                        if kt == 3 and last:
                            gather(*last)
                        if not is_first(b):
                            end_of_sequence(b - 1, h, kt)
            rounds(pe, body, count=B)
            pv(B - 1, H - 1, PAIRS - 1)
            gather(B - 1, H - 1)
            for h in range(H):
                for kt in range(TPB):
                    end_of_sequence(B - 1, h, kt)

        @block.scalar
        def _(act):
            def exp(b, h, kt):
                n = (b * H + h) * TPB + kt
                need(act, pv_step, (b * H + h) * PAIRS + kt // 2 - 1)
                for hf in range(HPB):
                    act.wait_ge(s_ready, n * HPB + hf + 1)
                    nc.scalar.activation(pT[:, kt % RING, hf * CH:(hf + 1) * CH], s_bank[hf][:], ACT.Exp,
                                         scale=HD ** -0.5).then_inc(exp_ready, 1)

            def rounded(b, h, n):
                u = b * H + h
                if n == 0:
                    act.wait_ge(nm_turned, u + 1)
                    nc.scalar.activation(rem[:, 0, :], nm_rows, ACT.Copy).then_inc(round_step, 1)
                    need(act, m_rows[h % 2], (b * (H // 2) + h // 2) * 16 * MROWS)
                else:
                    act.wait_ge(rem_step, 2 * u + n)
                ins = nc.scalar.activation(mparts[:, h % 2, n, :], rem[:, n, :] if n else nm_rows, ACT.Copy)
                ins.then_inc(m_ready if n == 2 else round_step, 1)

            def evacuate(b, h):
                act.wait_ge(pv_step, (b * H + h + 1) * PAIRS)
                need(act, gathered, b * H + h - 1)
                nc.scalar.activation(sums[:, h % 2, :], pv_bank[h % 2][:], ACT.Copy).then_inc(sums_kept, 1)

            def end_of_sequence(b, h, kt):
                if (h, kt) in ((1, 4), (1, 7)):
                    hf = kt // 7
                    act.wait_ge(o_turned, b * HPB + hf + 1)
                    nc.scalar.activation(oT[:, hf * CH:(hf + 1) * CH], y_bank[:], ACT.Copy).then_inc(oT_kept, 1)
                if (h, kt) in ((5, 6), (9, 6)):
                    norm.keep(act, b * HPB + h // 9)

            def body(b):
                if is_first(b):
                    for n in range(3):
                        rounded(b, 0, n)
                for h in range(H):
                    last, turned = before(b, h), ahead(b, h + 1)
                    for kt in range(TPB):
                        exp(b, h, kt)
                        if kt == 1 and last:
                            evacuate(*last)
                        if kt in (2, 3, 4) and turned:
                            rounded(*turned, kt - 2)
                        if not is_first(b):
                            end_of_sequence(b - 1, h, kt)
            rounds(act, body, count=B)
            evacuate(B - 1, H - 1)
            for h in range(H):
                for kt in range(TPB):
                    end_of_sequence(B - 1, h, kt)

        @block.gpsimd
        def _(pool):
            def remainders(b, h):
                u = b * H + h
                for n in range(2):
                    pool.wait_ge(round_step, 3 * u + 2 + n)
                    nc.gpsimd.tensor_tensor(rem[:, n + 1, :], rem[:, n, :], mparts[:, h % 2, n, :],
                                            ALU.subtract).then_inc(rem_step, 1)

            def end_of_sequence(b, h):
                if h in (3, 7):
                    norm.rstd_pow(pool, b * HPB + h // 7)

            def body(b):
                if is_first(b):
                    remainders(b, 0)
                for h in range(H):
                    turned = ahead(b, h + 1)
                    if turned:
                        remainders(*turned)
                    if not is_first(b):
                        end_of_sequence(b - 1, h)
            rounds(pool, body, count=B)
            for h in range(H):
                end_of_sequence(B - 1, h)

        @block.vector
        def _(dve):
            def largest(b, h, tiles):
                for qt in tiles:
                    for hf in range(HPB):
                        dve.wait_ge(a_ready, ((b * H + h) * TPB + qt) * HPB + hf + 1)
                        nc.vector.tensor_reduce(mx[:, h % 2, qt, hf:hf + 1], a_bank[hf][:], AX.X,
                                                ALU.max).then_inc(a_used, 1)

            def join(b, h):
                need(dve, nm_turned, b * H + h - 1)
                dve.wait_ge(a_used, (b * H + h + 1) * TPB * HPB)
                nc.vector.tensor_reduce(nm[:, h % 2, :], mx[:, h % 2], AX.X, ALU.max, negate=True).then_inc(nm_ready, 1)

            def over(b, h):
                u = b * H + h
                chain = Chain(dve, over_step, u + 1)
                dve.wait_ge(gathered, u + 1)
                if h == 0:
                    need(dve, o_turned, b * HPB)
                pv = gather_bank(h).rearrange("p (t e) -> p t e", e=HD + 1)
                chain.then(nc.vector.reciprocal(rd[:, h % 2, :], pv[:, :, HD]))
                chain.wait()
                nc.vector.tensor_tensor(o[:, :, h * HD:(h + 1) * HD], pv[:, :, 0:HD],
                                        bcast(rd[:, h % 2, :].rearrange("p (t a) -> p t a", a=1), [P, TPB, HD]),
                                        ALU.mult).then_inc(o_ready, 1)

            def copy_v(b, h):
                need(dve, pv_step, ((b - 1) * H + h + 1) * PAIRS)
                nc.vector.tensor_scalar(vb[:, h, :, 0:HD + 1],
                                        net.v1[:, bass.ds(b * TPB, TPB), h * (HD + 1):(h + 1) * (HD + 1)],
                                        1.0, None, ALU.mult).then_inc(v_ready, 1)

            def end_of_sequence(b, h):
                if h in (3, 7):
                    c = b * HPB + h // 7
                    x = net.x[:, bass.ds(c * CH, CH)]
                    dve.wait_ge(y_ready, c + 1)
                    nc.vector.tensor_tensor(x, x, y_bank[:], ALU.add).then_inc(y_added, 1)
                    dve.wait_ge(y_added, c + 1)
                    x3 = x.rearrange("p (t d) -> p t d", d=D)
                    b_out = bcast(net.L1_bout[:].rearrange("p (a d) -> p a d", a=1), [P, TPC, D])
                    nc.vector.tensor_tensor(x3, x3, b_out, ALU.add).then_inc(norm.x_whole, 1)
                    dve.wait_ge(norm.x_whole, c + 1)
                    norm.stats(dve, c)
                if h in (4, 8):
                    norm.apply(dve, b * HPB + h // 8)

            def body(b):
                if is_first(b):
                    nc.vector.memset(vb[:], 0.0).then_inc(over_step, 1)
                    dve.wait_ge(over_step, 1)
                    for h in range(AHEAD):
                        copy_v(b, h)
                    largest(b, 0, range(TPB))
                    join(b, 0)
                    largest(b, 1, range(TPB))
                    join(b, 1)
                for h in range(H):
                    fetched, last, copied = ahead(b, h + 2), before(b, h), ahead(b, h + AHEAD)
                    if fetched:
                        largest(*fetched, range(0, 6))
                    if last:
                        over(*last)
                    if not is_first(b):
                        end_of_sequence(b - 1, h)
                    if fetched:
                        largest(*fetched, range(6, TPB))
                        join(*fetched)
                    if copied:
                        copy_v(*copied)
            rounds(dve, body, count=B)
            over(B - 1, H - 1)
            for h in range(H):
                end_of_sequence(B - 1, h)



NEXP = 8
PW = 2 * P + 2
DEN_EPS = 1e-6


def decay_stage(nc, net, tag, src, dest, router):
    with Scope(nc) as st:
        norm = Norm(nc, st, net, tag, dest, router is not None, across=True)
        part = Part(nc, st, tag)
        W1 = D + 1
        gamma = part.sb("gamma", [P, NEXP])
        bits, nbits = part.sb("bits", [P, NEXP, PW]), part.sb("nbits", [P, NEXP, PW])
        causal = part.sb("causal", [P, P])
        factor, power = part.sb("factor", [P, PW]), part.sb("power", [P, PW])
        xa = part.sb("xa", [P, B, P])
        qT, kT, qd = part.sb("qT", [P, B, P]), part.sb("kT", [P, B, P]), part.sb("qd", [P, B, P])
        kb, kd = part.sb("kb", [P, B, D]), part.sb("kd", [P, B, D])
        v1 = part.sb("v1", [P, B, W1])
        aT = part.sb("aT", [P, B, P])
        state = part.sb("state", [P, B, W1])
        den, rden, y = part.sb("den", [P, B]), part.sb("rden", [P, B]), part.sb("y", [P, B, D])
        loads, setup, xa_ready, q_ready, k_ready, kv_ready, qk_kept, weighted, a_ready, at_ready = (
            part.sem(k) for k in ("loads", "setup", "xa_ready", "q_ready", "k_ready", "kv_ready", "qk_kept", "weighted",
                                  "a_ready", "at_ready"))
        num_ready, state_ready, divided, carried, own = (
            part.sem(k) for k in ("num_ready", "state_ready", "divided", "carried", "dve_step"))
        w_decay, q_power, k_power = power[:, 0:P], power[:, P:2 * P], power[:, 2 * P:2 * P + 1]
        s_power = power[:, 2 * P + 1:2 * P + 2]
        block = st.enter_context(nc.Block())

        def pair(t, m):
            return t[:, 2 * m:2 * m + 2]

        @block.sync
        def _(sp):
            sp.dma_start(bits[:], net.ins["bits"]).then_inc(loads, 16)
            sp.dma_start(nbits[:], net.ins["nbits"]).then_inc(loads, 16)
            sp.dma_start(causal[:], net.ins["causal"]).then_inc(loads, 16)
            sp.dma_start(gamma[:, 0:1], net.ins["gamma"].partition_broadcast(P)).then_inc(loads, 16)
            sp.wait_ge(loads, 64)

        @block.tensor
        def _(pe):
            def proj(n):
                need(pe, carried, 2 * n)
                pe.wait_ge(xa_ready, n + 1)
                xf = xa[:].rearrange("p b t -> p (b t)")
                nc.tensor.matmul(net.bank[0][:], net.L2_wq[:], xf, start=True, stop=True).then_inc(q_ready, 1)
                nc.tensor.matmul(net.bank[1][:], net.L2_wkv[:, 0:D], xf, start=True, stop=True).then_inc(k_ready, 1)
                need(pe, weighted, n)
                for b in range(B):
                    ins = nc.tensor.matmul(net.bank[2 + b // 2][:, (b % 2) * 2 * D:(b % 2 + 1) * 2 * D], xa[:, b, :],
                                           net.L2_wkv[:], start=True, stop=True)
                ins.then_inc(kv_ready, 1)

            def scores(n):
                pe.wait_ge(qk_kept, 2 * (n + 1))
                need(pe, divided, 2 * n)
                for b in range(B):
                    ins = nc.tensor.matmul(net.bank[4][:, b * P:(b + 1) * P], kT[:, b, :], qT[:, b, :],
                                           start=True, stop=True)
                ins.then_inc(a_ready, 1)

            def sums(n):
                pe.wait_ge(at_ready, n + 1)
                pe.wait_ge(weighted, n + 1)
                need(pe, carried, 2 * n)
                for b in range(B):
                    out = net.bank[4 + b // 2][:, (b % 2) * W1:(b % 2 + 1) * W1]
                    nc.tensor.matmul(out, aT[:, b, :], v1[:, b, :], start=True, stop=False)
                    ins = nc.tensor.matmul(out, qd[:, b, :], state[:, b, :], start=False, stop=True)
                ins.then_inc(num_ready, 1)

            def update(n):
                for b in range(B):
                    ins = nc.tensor.matmul(net.bank[b // 2][:, (b % 2) * W1:(b % 2 + 1) * W1], kd[:, b, :], v1[:, b, :],
                                           start=True, stop=True)
                ins.then_inc(state_ready, 1)

            def body(n):
                before = not is_first(n)
                proj(n)
                if before:
                    norm.turn(pe, n - 1)
                scores(n)
                if before and norm.route:
                    norm.logits(pe, n - 1, router.rw)
                sums(n)
                if before and norm.route:
                    norm.turn_g(pe, n - 1)
                update(n)
                if before and norm.route:
                    norm.bias(pe, n - 1, router.b2)
            rounds(pe, body, lambda n: norm.all_pe(pe, n, router.rw, router.b2))

        @block.scalar
        def _(act):
            def body(n):
                act.wait_ge(q_ready, n + 1)
                nc.scalar.activation(qT[:].rearrange("p b t -> p (b t)"), net.bank[0][:], ACT.Relu,
                                     bias=net.L2_bq[:]).then_inc(qk_kept, 1)
                act.wait_ge(k_ready, n + 1)
                nc.scalar.activation(kT[:].rearrange("p b t -> p (b t)"), net.bank[1][:], ACT.Relu,
                                     bias=net.L2_bk[:]).then_inc(qk_kept, 1)
                if not is_first(n):
                    norm.keep(act, n - 1)
                    if norm.route:
                        norm.keep_g(act, n - 1)
            rounds(act, body, lambda n: norm.all_act(act, n))

        @block.gpsimd
        def _(pool):
            rounds(pool, lambda n: norm.all_pool(pool, n))

        @block.vector
        def _(dve):
            chain = Chain(dve, setup, 0)
            dve.wait_ge(loads, 64)
            for k in range(1, NEXP):
                chain.then(nc.vector.tensor_tensor(gamma[:, k:k + 1], gamma[:, k - 1:k], gamma[:, k - 1:k], ALU.mult))
                chain.wait()
            chain.then(nc.vector.memset(power[:], 1.0))
            for k in range(NEXP):
                chain.then(nc.vector.scalar_tensor_tensor(factor[:], bits[:, k, :], gamma[:, k:k + 1], nbits[:, k, :],
                                                          ALU.mult, ALU.add))
                chain.wait()
                chain.then(nc.vector.tensor_tensor(power[:], power[:], factor[:], ALU.mult))
                chain.wait()
            chain.then(nc.vector.tensor_tensor(w_decay, w_decay, causal[:], ALU.mult))
            nc.vector.memset(v1[:], 1.0)
            chain.then(nc.vector.memset(state[:], 0.0))
            chain.wait()

            def fetch(n):
                need(dve, kv_ready, n)
                nc.vector.tensor_scalar(xa[:], norm.view(src, n), 1.0, None, ALU.mult).then_inc(xa_ready, 1)

            def weight(n):
                steps = Chain(dve, own, n * 8)
                dve.wait_ge(kv_ready, n + 1)
                for m in range(2):
                    kv = net.bank[2 + m][:].rearrange("p (b e) -> p b e", b=2)
                    nc.vector.tensor_tensor(pair(v1, m)[:, :, 0:D], kv[:, :, D:2 * D],
                                            bcast(net.L2_bv_row[:].rearrange("p (a d) -> p a d", a=1), [P, 2, D]), ALU.add)
                    steps.then(nc.vector.tensor_tensor(
                        pair(kb, m), kv[:, :, 0:D],
                        bcast(net.L2_bk_row[:].rearrange("p (a d) -> p a d", a=1), [P, 2, D]), ALU.add))
                steps.wait()
                nc.vector.tensor_scalar(kd[:], kb[:], 0.0, k_power, ALU.max, ALU.mult)
                dve.wait_ge(qk_kept, 2 * n + 1)
                nc.vector.tensor_tensor(qd[:], qT[:], bcast(q_power.rearrange("p (a t) -> p a t", a=1), [P, B, P]),
                                        ALU.mult).then_inc(weighted, 1)

            def decay(n):
                dve.wait_ge(a_ready, n + 1)
                nc.vector.tensor_tensor(aT[:], net.bank[4][:].rearrange("p (b t) -> p b t", b=B),
                                        bcast(w_decay.rearrange("p (a t) -> p a t", a=1), [P, B, P]),
                                        ALU.mult).then_inc(at_ready, 1)

            def divide(n):
                steps = Chain(dve, own, n * 8 + 2)
                x = norm.view(net.x, n)
                dve.wait_ge(num_ready, n + 1)
                for m in range(2):
                    sums = net.bank[4 + m][:, 0:2 * W1].rearrange("p (b e) -> p b e", b=2)
                    steps.then(nc.vector.tensor_scalar(den[:, 2 * m:2 * m + 2], sums[:, :, D], DEN_EPS, None, ALU.add))
                    steps.wait()
                    steps.then(nc.vector.reciprocal(rden[:, 2 * m:2 * m + 2], den[:, 2 * m:2 * m + 2]))
                    steps.wait()
                    steps.then(nc.vector.tensor_tensor(
                        pair(y, m), sums[:, :, 0:D],
                        bcast(rden[:, 2 * m:2 * m + 2].rearrange("p (b a) -> p b a", a=1), [P, 2, D]), ALU.mult))
                    steps.wait()
                    nc.vector.tensor_tensor(x[:, 2 * m:2 * m + 2], x[:, 2 * m:2 * m + 2], pair(y, m),
                                            ALU.add).then_inc(divided, 1)

            def carry(n):
                dve.wait_ge(state_ready, n + 1)
                for m in range(2):
                    nc.vector.scalar_tensor_tensor(pair(state, m), pair(state, m), s_power,
                                                   net.bank[m][:, 0:2 * W1].rearrange("p (b e) -> p b e", b=2),
                                                   ALU.mult, ALU.add).then_inc(carried, 1)

            def body(n):
                before = not is_first(n)
                if before:
                    norm.apply(dve, n - 1)
                else:
                    fetch(0)
                weight(n)
                if not is_last(n):
                    fetch(n + 1)
                decay(n)
                if before and norm.route:
                    norm.pick(dve, n - 1, router.rb)
                divide(n)
                if before and norm.route:
                    norm.weigh(dve, n - 1)
                carry(n)
                if before and norm.route:
                    norm.add_bias(dve, n - 1)
                dve.wait_ge(divided, 2 * (n + 1))
                norm.stats(dve, n)

            def tail(n):
                norm.apply(dve, n)
                if norm.route:
                    norm.pick(dve, n, router.rb)
                    norm.weigh(dve, n)
                    norm.add_bias(dve, n)
            rounds(dve, body, tail)



def chunks_of_sequences(eng, body):
    for hf in range(HPB):
        body(hf, 0, hf)
    with eng.Fori(1, B) as b:
        for hf in range(HPB):
            body(b * HPB + hf, b, hf)


def fetch_shifted(nc, xs, src, c, hf):
    if hf == 0:
        return nc.vector.tensor_scalar(xs[:, 0, 1:CH + 1], src[:, bass.ds(c * CH, CH)], 1.0, None, ALU.mult)
    return nc.vector.tensor_scalar(xs[:, 1, :], src[:, bass.ds(c * CH - 1, CH + 1)], 1.0, None, ALU.mult)


def rwkv_ffn_stage(nc, net, tag, src, dest):
    with Scope(nc) as st:
        norm = Norm(nc, st, net, tag, dest, False) if dest is not None else None
        part = Part(nc, st, tag)
        xs = part.sb("xs", [P, 2, CH + 1])
        diff = part.sb("diff", [P, CH])
        xr, xk = part.sb("xr", [P, 2, CH]), part.sb("xk", [P, 2, CH])
        kr, kk, sig, gated = (part.sb(k, [P, 2, CH]) for k in ("k_relu", "k_square", "sigmoid", "gated"))
        setup, mixed, k_ready, r_ready, acted, squared, y_ready, y_added, own, x_whole = (
            part.sem(k) for k in ("setup", "mixed", "k_ready", "r_ready", "acted", "squared", "y_ready", "y_added",
                                  "dve_step", "x_whole_here"))
        block = st.enter_context(nc.Block())

        @block.tensor
        def _(pe):
            def body(c, b, hf):
                pe.wait_ge(mixed, c + 1)
                need(pe, acted, 2 * c)
                nc.tensor.matmul(net.bank[0][:], net.L3_fk[:], xk[:, hf, :], start=True, stop=True).then_inc(k_ready, 1)
                for i in range(TPC):
                    t = slice(i * P, (i + 1) * P)
                    ins = nc.tensor.matmul(net.bank[1][:, t], xr[:, hf, t], net.L3_fr[:], start=True, stop=True)
                ins.then_inc(r_ready, 1)
                if norm and not is_first(c):
                    norm.turn(pe, c - 1)
                pe.wait_ge(squared, c + 1)
                need(pe, y_added, c)
                for i in range(TPC):
                    t = slice(i * P, (i + 1) * P)
                    ins = nc.tensor.matmul(net.bank[2][:, t], kk[:, hf, t], net.L3_fv[:], start=True, stop=True)
                ins.then_inc(y_ready, 1)
            chunks_of_sequences(pe, body)
            if norm:
                norm.all_pe(pe, NCH - 1)

        @block.scalar
        def _(act):
            def body(c, b, hf):
                need(act, squared, c - 1)
                act.wait_ge(k_ready, c + 1)
                nc.scalar.activation(kr[:, hf, :], net.bank[0][:], ACT.Relu).then_inc(acted, 1)
                need(act, y_added, c - 1)
                act.wait_ge(r_ready, c + 1)
                nc.scalar.activation(sig[:, hf, :], net.bank[1][:], ACT.Sigmoid).then_inc(acted, 1)
                if norm and not is_first(c):
                    norm.keep(act, c - 1)
            chunks_of_sequences(act, body)
            if norm:
                norm.all_act(act, NCH - 1)

        @block.gpsimd
        def _(pool):
            if norm:
                rounds(pool, lambda c: norm.all_pool(pool, c))

        @block.vector
        def _(dve):
            nc.vector.memset(xs[:, 0, 0:1], 0.0).then_inc(setup, 1)
            dve.wait_ge(setup, 1)

            def mix(c, hf):
                chain = Chain(dve, own, c * 2)
                chain.then(fetch_shifted(nc, xs, src, c, hf))
                chain.wait()
                old = xs[:, hf, 0:CH]
                chain.then(nc.vector.tensor_tensor(diff[:], xs[:, hf, 1:CH + 1], old, ALU.subtract))
                need(dve, r_ready, c - 1)
                chain.wait()
                nc.vector.scalar_tensor_tensor(xk[:, hf, :], diff[:], net.L3_mu_k[:], old, ALU.mult, ALU.add)
                nc.vector.scalar_tensor_tensor(xr[:, hf, :], diff[:], net.L3_mu_r[:], old, ALU.mult,
                                               ALU.add).then_inc(mixed, 1)

            def square(c, hf):
                dve.wait_ge(acted, 2 * c + 1)
                need(dve, y_ready, c - 1)
                nc.vector.tensor_tensor(kk[:, hf, :], kr[:, hf, :], kr[:, hf, :], ALU.mult).then_inc(squared, 1)

            def add(c, hf):
                x = net.x[:, bass.ds(c * CH, CH)]
                dve.wait_ge(acted, 2 * c + 2)
                dve.wait_ge(y_ready, c + 1)
                nc.vector.tensor_tensor(gated[:, hf, :], net.bank[2][:], sig[:, hf, :], ALU.mult).then_inc(y_added, 1)
                dve.wait_ge(y_added, c + 1)
                nc.vector.scalar_tensor_tensor(x, gated[:, hf, :], 0.5, x, ALU.mult, ALU.add).then_inc(x_whole, 1)
                dve.wait_ge(x_whole, c + 1)

            def body(c, b, hf):
                mix(c, hf)
                if not is_first(c):
                    add(c - 1, 1 - hf)
                    if norm:
                        norm.stats(dve, c - 1)
                square(c, hf)
                if norm and not is_first(c):
                    norm.apply(dve, c - 1)
            chunks_of_sequences(dve, body)
            add(NCH - 1, 1)
            if norm:
                norm.all_dve(dve, NCH - 1)



NMIX = 5
TM = 32
TD = 64
GN_EPS = 1e-5 * HD ** 2


def time_mix_stage(nc, net, tag, src, dest):
    with Scope(nc) as st:
        norm = Norm(nc, st, net, tag, dest, False)
        part = Part(nc, st, tag)
        xs = part.sb("xs", [P, 2, CH + 1])
        xx, x3 = part.sb("xx", [P, CH]), part.sb("x_first_mix", [P, CH])
        m0, m1 = part.sb("tanh_m0", [P, CH]), part.sb("tanh_m1", [TM, CH])
        corr = part.sb("corr", [P, 2, CH])
        xm = part.sb("x_mixed", [P, NMIX, CH])
        tw, e1, wd = part.sb("tanh_w", [TD, CH]), part.sb("exp_w", [P, CH]), part.sb("decay", [P, CH])
        kT, rT, vT, gT = (part.sb(k, [P, CH]) for k in ("kT", "rT", "vT", "gT"))
        kv = part.sb("kv", [P, 2, CH])
        S_t = part.sb("S", [P, HD, CH + 1])
        rs = part.sb("rS", [P, 4, CH])
        rku, bonus, y, yc, sq, std, rstd = (part.sb(k, [P, CH])
                                            for k in ("rku", "bonus", "y", "yc", "sq", "std", "rstd"))
        yn, yg = part.sb("yn", [P, CH]), part.sb("yg", [P, CH])
        w2a, w2b = part.sb("w2a", [P, 4, D]), part.sb("w2b", [TM, D])
        sel = part.sb("sel", [P, HD, D])
        gn_eps = part.sb("gn_eps", [P, 1])
        W_ = {k: part.sb(f"W{k}", [P, D]) for k in ("r", "k", "v", "g", "o", "blockones", "center", "blockmean")}
        w1 = part.sb("w1", [P, NMIX * TM])
        dw1, dw2 = part.sb("dw1", [P, TD]), part.sb("dw2", [TD, D])
        Wv_rep = part.sb("Wv_rep", [P, HD, D])
        vecs = part.sb("vecs", [P, 10])
        (loads, setup, xx_ready, m_ready, m_kept, mix_ready, mix_used, mixed, lin_ready, lin_kept, w1_ready, w1_kept,
         w2_ready, wd_ready, e1_ready, rep_ready, kv_done, scanned, rs_ready, y_acc, rku_ready, bonus_ready,
         bonus_used) = (part.sem(k) for k in (
             "loads", "setup", "xx_ready", "m_ready", "m_kept", "mix_ready", "mix_used", "mixed", "lin_ready", "lin_kept",
             "w1_ready", "w1_kept", "w2_ready", "wd_ready", "e1_ready", "rep_ready", "kv_done", "scanned", "rs_ready",
             "y_acc", "rku_ready", "bonus_ready", "bonus_used"))
        (y_whole, yc_ready, yc_kept, sq_ready, var_ready, std_ready, yg_ready, out_ready, out_added, own) = (
            part.sem(k) for k in ("y_whole", "yc_ready", "yc_kept", "sq_ready", "var_ready", "std_ready",
                                  "yg_ready", "out_ready", "out_added", "dve_step"))
        gn_step = part.sem("group_norm_step")
        y_bank, var_bank = net.bank[7], net.bank[6]
        names = ["td_decay", "u", "ln_gamma", "ln_beta", "maa_x", "maa_w", "maa_k", "maa_v", "maa_r", "maa_g"]
        vec = {k: vecs[:, i:i + 1] for i, k in enumerate(names)}
        mats = [(W_[k], "L3_" + k) for k in W_] + [(w1, "L3_w1"), (dw1, "L3_dw1"), (dw2, "L3_dw2"), (sel, "sel"),
                                                    (vecs, "L3_vecs")]
        NLOAD = len(mats) + 4 + 1 + HD
        block = st.enter_context(nc.Block())
        MIX_BANK = [net.bank[i] for i in (2, 3, 4, 5, 0)]
        LINEAR = (("k", 1, 2), ("r", 3, 3), ("v", 2, 4), ("g", 4, 5))

        @block.sync
        def _(sp):
            for t, name in mats:
                sp.dma_start(t[:], net.ins[name]).then_inc(loads, 16)
            sp.wait_ge(setup, 1)
            for f in range(4):
                sp.dma_start(w2a[f * TM:(f + 1) * TM, f, :], net.ins["L3_w2"][f]).then_inc(loads, 16)
            sp.dma_start(w2b[:], net.ins["L3_w2"][4]).then_inc(loads, 16)
            for j in range(HD):
                sp.dma_start(Wv_rep[:, j, :], net.ins["L3_v_rep"][j]).then_inc(loads, 16)
            sp.wait_ge(loads, 16 * NLOAD)

        @block.tensor
        def _(pe):
            pe.wait_ge(loads, 16 * NLOAD)

            def center(c):
                pe.wait_ge(y_whole, c + 1)
                nc.tensor.matmul(y_bank[:], W_["center"][:], y[:], start=True, stop=True).then_inc(yc_ready, 1)

            def variance(c):
                pe.wait_ge(sq_ready, c + 1)
                need(pe, norm.kept, c)
                nc.tensor.matmul(var_bank[:], W_["blockmean"][:], sq[:], start=True, stop=True).then_inc(var_ready, 1)

            def project(c):
                pe.wait_ge(yg_ready, c + 1)
                for i in range(TPC):
                    t = slice(i * P, (i + 1) * P)
                    ins = nc.tensor.matmul(y_bank[:, t], yg[:, t], W_["o"][:], start=True, stop=True)
                ins.then_inc(out_ready, 1)

            def body(c, b, hf):
                if not is_first(c):
                    center(c - 1)
                pe.wait_ge(xx_ready, c + 1)
                need(pe, kv_done, HD * c)
                nc.tensor.matmul(net.bank[0][:], w1[:, 0:P], x3[:], start=True, stop=True).then_inc(m_ready, 1)
                nc.tensor.matmul(net.bank[1][0:TM, :], w1[:, P:P + TM], x3[:], start=True, stop=True).then_inc(m_ready, 1)
                if not is_first(c):
                    variance(c - 1)
                need(pe, lin_kept, 4 * c)
                need(pe, y_whole, c)
                for f in range(NMIX):
                    pe.wait_ge(m_kept, 2 * c + (1 if f < 4 else 2))
                    lhs, rhs = (w2a[:, f, :], m0[:]) if f < 4 else (w2b[:], m1[:])
                    nc.tensor.matmul(MIX_BANK[f][:], lhs, rhs, start=True, stop=True).then_inc(mix_ready, 1)
                pe.wait_ge(mixed, NMIX * c + 1)
                nc.tensor.matmul(net.bank[1][0:TD, :], dw1[:], xm[:, 0, :], start=True, stop=True).then_inc(w1_ready, 1)
                for k, f, bank in LINEAR:
                    if k == "g" and not is_first(c):
                        project(c - 1)
                    pe.wait_ge(mixed, NMIX * (c + 1))
                    nc.tensor.matmul(net.bank[bank][:], W_[k][:], xm[:, f, :], start=True, stop=True).then_inc(lin_ready, 1)
                pe.wait_ge(w1_kept, c + 1)
                nc.tensor.matmul(net.bank[1][:], dw2[:], tw[:], start=True, stop=True).then_inc(w2_ready, 1)

                def repeat(j):
                    if j == 1:
                        pe.wait_ge(e1_ready, c + 1)
                    if j >= 2:
                        need(pe, kv_done, HD * c + j - 1)
                    nc.tensor.matmul(net.bank[j % 2][:], Wv_rep[:, j, :], xm[:, 2, :],
                                     start=True, stop=True).then_inc(rep_ready, 1)

                repeat(0)
                repeat(1)
                pe.wait_ge(lin_kept, 4 * (c + 1))
                pe.wait_ge(rku_ready, c + 1)
                nc.tensor.matmul(net.bank[3][:], W_["blockones"][:], rku[:], start=True, stop=True).then_inc(bonus_ready, 1)
                for j in range(HD):
                    if j + 2 < HD:
                        repeat(j + 2)
                    if j == 0:
                        need(pe, out_added, c)
                    pe.wait_ge(rs_ready, HD * c + j + 1)
                    nc.tensor.matmul(y_bank[:], sel[:, j, :], rs[:, j % 4, :],
                                     start=(j == 0), stop=(j == HD - 1)).then_inc(y_acc, 1)
                if not is_first(c):
                    norm.turn(pe, c - 1)
            chunks_of_sequences(pe, body)
            center(NCH - 1)
            variance(NCH - 1)
            project(NCH - 1)
            norm.all_pe(pe, NCH - 1)

        @block.scalar
        def _(act):
            act.wait_ge(loads, 16 * NLOAD)
            act.wait_ge(setup, 2)

            def squares(c):
                act.wait_ge(yc_ready, c + 1)
                nc.scalar.activation(yc[:], y_bank[:], ACT.Copy).then_inc(yc_kept, 1)
                nc.scalar.activation(sq[:], y_bank[:], ACT.Square).then_inc(sq_ready, 1)

            def deviation(c):
                act.wait_ge(var_ready, c + 1)
                nc.scalar.activation(std[:], var_bank[:], ACT.Sqrt, bias=gn_eps[:]).then_inc(std_ready, 1)

            def body(c, b, hf):
                if not is_first(c):
                    squares(c - 1)
                act.wait_ge(m_ready, 2 * c + 1)
                nc.scalar.activation(m0[:], net.bank[0][:], ACT.Tanh).then_inc(m_kept, 1)
                act.wait_ge(m_ready, 2 * c + 2)
                nc.scalar.activation(m1[:], net.bank[1][0:TM, :], ACT.Tanh).then_inc(m_kept, 1)
                act.wait_ge(w1_ready, c + 1)
                nc.scalar.activation(tw[:], net.bank[1][0:TD, :], ACT.Tanh).then_inc(w1_kept, 1)
                if not is_first(c):
                    deviation(c - 1)
                for n, (dst, bank, func) in enumerate(((kT, 2, ACT.Copy), (rT, 3, ACT.Copy), (vT, 4, ACT.Copy))):
                    act.wait_ge(lin_ready, 4 * c + n + 1)
                    nc.scalar.activation(dst[:], net.bank[bank][:], func).then_inc(lin_kept, 1)
                act.wait_ge(w2_ready, c + 1)
                nc.scalar.activation(e1[:], net.bank[1][:], ACT.Exp, bias=vec["td_decay"]).then_inc(e1_ready, 1)
                act.wait_ge(e1_ready, c + 1)
                nc.scalar.activation(wd[:], e1[:], ACT.Exp, scale=-1.0).then_inc(wd_ready, 1)
                act.wait_ge(lin_ready, 4 * c + 4)
                need(act, yg_ready, c)
                nc.scalar.activation(gT[:], net.bank[5][:], ACT.Silu).then_inc(lin_kept, 1)
                if not is_first(c):
                    norm.keep(act, c - 1)
            chunks_of_sequences(act, body)
            squares(NCH - 1)
            deviation(NCH - 1)
            norm.all_act(act, NCH - 1)

        @block.gpsimd
        def _(pool):
            nc.gpsimd.memset(w2a[:], 0.0).then_inc(setup, 1)
            nc.gpsimd.memset(gn_eps[:], GN_EPS).then_inc(setup, 1)

            def body(c, b, hf):
                pool.wait_ge(lin_kept, 4 * c + 2)
                for j in range(HD):
                    if j == 4 and not is_first(c):
                        norm.rstd_pow(pool, c - 1)
                    need(pool, y_acc, HD * c + j - 3)
                    pool.wait_ge(scanned, HD * c + j + 1)
                    nc.gpsimd.tensor_tensor(rs[:, j % 4, :], rT[:], S_t[:, j, 0:CH], ALU.mult).then_inc(rs_ready, 1)
            chunks_of_sequences(pool, body)
            norm.all_pool(pool, NCH - 1)

        @block.vector
        def _(dve):
            dve.wait_ge(loads, 16 * NLOAD)
            start = Chain(dve, own, 0)
            start.then(nc.vector.memset(xs[:, 0, 0:1], 0.0))
            start.wait()
            STEPS = 10

            def group(c):
                steps = Chain(dve, gn_step, c * 3)
                dve.wait_ge(yc_kept, c + 1)
                dve.wait_ge(std_ready, c + 1)
                steps.then(nc.vector.reciprocal(rstd[:], std[:]))
                steps.wait()
                steps.then(nc.vector.tensor_tensor(yn[:], yc[:], rstd[:], ALU.mult))
                steps.wait()
                steps.then(nc.vector.tensor_scalar(yn[:], yn[:], vec["ln_gamma"], vec["ln_beta"], ALU.mult, ALU.add))
                dve.wait_ge(lin_kept, 4 * c + 4)
                steps.wait()
                nc.vector.tensor_tensor(yg[:], yn[:], gT[:], ALU.mult).then_inc(yg_ready, 1)

            def add(c):
                x = net.x[:, bass.ds(c * CH, CH)]
                dve.wait_ge(out_ready, c + 1)
                nc.vector.tensor_tensor(x, x, y_bank[:], ALU.add).then_inc(out_added, 1)

            def body(c, b, hf):
                chain = Chain(dve, own, c * STEPS + 1)
                cur, old = xs[:, hf, 1:CH + 1], xs[:, hf, 0:CH]
                chain.then(fetch_shifted(nc, xs, src, c, hf))
                chain.wait()
                chain.then(nc.vector.tensor_tensor(xx[:], old, cur, ALU.subtract))
                chain.wait()
                nc.vector.scalar_tensor_tensor(x3[:], xx[:], vec["maa_x"], cur, ALU.mult, ALU.add).then_inc(xx_ready, 1)
                for f in range(NMIX):
                    dve.wait_ge(mix_ready, NMIX * c + f + 1)
                    chain.then(nc.vector.scalar_tensor_tensor(corr[:, f % 2, :], MIX_BANK[f][:], vecs[:, 5 + f:6 + f], xx[:],
                                                              ALU.add, ALU.mult))
                    chain.wait()
                    nc.vector.tensor_tensor(xm[:, f, :], corr[:, f % 2, :], cur, ALU.add).then_inc(mixed, 1)
                if not is_first(c):
                    group(c - 1)
                    add(c - 1)
                dve.wait_ge(lin_kept, 4 * c + 2)
                chain.then(nc.vector.scalar_tensor_tensor(rku[:], rT[:], vec["u"], kT[:], ALU.mult, ALU.mult))
                chain.eng.wait_ge(own, chain.count)
                nc.vector.tensor_scalar(corr[:, 0, 0:1], corr[:, 0, 0:1], 1.0, None, ALU.mult).then_inc(rku_ready, 1)
                need(dve, rs_ready, HD * c)
                if hf == 0:
                    chain.then(nc.vector.memset(S_t[:, :, 0:1], 0.0))
                else:
                    chain.then(nc.vector.tensor_copy(S_t[:, :, 0:1], S_t[:, :, CH:CH + 1]))
                for j in range(HD):
                    if j == 2 and not is_first(c):
                        dve.wait_ge(out_added, c)
                        norm.stats(dve, c - 1)
                    if j == 6 and not is_first(c):
                        norm.apply(dve, c - 1)
                    dve.wait_ge(rep_ready, HD * c + j + 1)
                    nc.vector.tensor_tensor(kv[:, j % 2, :], kT[:], net.bank[j % 2][:], ALU.mult).then_inc(kv_done, 1)
                    if j == 0:
                        dve.wait_ge(wd_ready, c + 1)
                        chain.wait()
                    dve.wait_ge(kv_done, HD * c + j + 1)
                    nc.vector.tensor_tensor_scan(S_t[:, j, 1:CH + 1], wd[:], kv[:, j % 2, :], S_t[:, j, 0:1],
                                                 ALU.mult, ALU.add).then_inc(scanned, 1)
                dve.wait_ge(lin_kept, 4 * c + 3)
                dve.wait_ge(bonus_ready, c + 1)
                chain.then(nc.vector.tensor_tensor(bonus[:], vT[:], net.bank[3][:], ALU.mult))
                dve.wait_ge(y_acc, HD * (c + 1))
                chain.wait()
                nc.vector.tensor_tensor(y[:], bonus[:], y_bank[:], ALU.add).then_inc(y_whole, 1)
            chunks_of_sequences(dve, body)
            group(NCH - 1)
            add(NCH - 1)
            dve.wait_ge(out_added, NCH)
            norm.all_dve(dve, NCH - 1)



def store_stage(nc, net, out):
    with Scope(nc) as st:
        stored = st.sem("stored")
        block = st.enter_context(nc.Block())

        @block.sync
        def _(sp):
            dst = out.rearrange("(t p) d -> p t d", p=P)
            src = net.x[:].rearrange("p (t d) -> p t d", d=D)
            for c in range(NCH):
                sp.dma_start(dst[:, c * TPC:(c + 1) * TPC], src[:, c * TPC:(c + 1) * TPC]).then_inc(stored, 16)
            sp.wait_ge(stored, 16 * NCH)


def rotary_attention(nc, net, tag, src, dest, router):
    with Scope(nc) as st:
        part = Part(nc, st, tag)
        q_parts, k_parts = (nc.dram_tensor(f"{tag}_{w}_parts", [NS, P, T], BF16, kind="Internal").ap() for w in "qk")
        net.v1 = part.sb("v1", [P, T // P, H * (HD + 1)])
        net.Q, net.K = part.sb("Q", [P, QRING, S], BF16), part.sb("K", [P, QRING, S], BF16)
        rope_stage(nc, net, tag + "_rope", src, q_parts, k_parts)
        attention_stage(nc, net, tag, dest, q_parts, k_parts, router)


def build(nc, ins, out):
    with Scope(nc) as st:
        net = open_net(nc, st, ins)
        l0 = Router(net.L0_rw, None, net.L0_b2)
        l2 = Router(net.L2_rw, net.L2_rb, net.L2_b2)
        experts = ExitStack()
        net.w1 = experts.enter_context(nc.sbuf_tensor("w1", [P, E, FF], F32))
        net.w2 = experts.enter_context(nc.sbuf_tensor("w2", [P, E, FC, D], F32))
        load_stage(nc, net, l0)
        src, dest = net.xnT
        stages = [lambda s, d: moe_stage(nc, net, "ffn0a", "L0", ACT.Gelu, s, d, None),
                  lambda s, d: head_mix_stage(nc, net, "mix0", s, d, l0),
                  lambda s, d: moe_stage(nc, net, "ffn0b", "L0", ACT.Gelu, s, d, None),
                  lambda s, d: swiglu_stage(nc, net, "ffn1a", s, d, None),
                  lambda s, d: rotary_attention(nc, net, "attn1", s, d, None),
                  lambda s, d: swiglu_stage(nc, net, "ffn1b", s, d, l2),
                  lambda s, d: moe_stage(nc, net, "ffn2a", "L2", ACT.Relu, s, d, None),
                  lambda s, d: decay_stage(nc, net, "decay2", s, d, l2),
                  lambda s, d: moe_stage(nc, net, "ffn2b", "L2", ACT.Relu, s, d, None),
                  lambda s, d: rwkv_ffn_stage(nc, net, "ffn3a", s, d),
                  lambda s, d: time_mix_stage(nc, net, "mix3", s, d),
                  lambda s, d: rwkv_ffn_stage(nc, net, "ffn3b", s, None),
                  ]
        for n, stage in enumerate(stages[:STAGES]):
            if n == 9:
                experts.close()
            stage(src, dest)
            src, dest = dest, src
        experts.close()
        store_stage(nc, net, out)


def lay_out(inputs):
    g = {k: np.asarray(v) for k, v in inputs.items()}
    a = {"x": g["L0_attn_x"].reshape(T, D)}

    def rows(w):
        return np.ascontiguousarray(w)
    a["L0_w1"] = rows(g["L0_ffn_w1"].transpose(2, 0, 1))
    a["L0_b1"] = rows(g["L0_ffn_b1"].reshape(E * FC, P).T)
    a["L0_w2"] = rows(g["L0_ffn_w2"].reshape(E, D, FC, P).transpose(3, 0, 2, 1))
    a["L0_b2"] = g["L0_ffn_b2"]
    a["L0_rw"] = rows(g["L0_ffn_router_w"].T)
    a["L2_w1"] = rows(g["L2_ffn_w1"].transpose(1, 0, 2))
    a["L2_b1"] = rows(g["L2_ffn_b1"].reshape(E * FC, P).T)
    a["L2_w2"] = rows(g["L2_ffn_w2"].reshape(E, FC, P, D).transpose(2, 0, 1, 3))
    a["L2_b2"] = g["L2_ffn_b2"]
    a["L2_rw"] = g["L2_ffn_router_w"]
    a["L2_rb"] = g["L2_ffn_router_b"]
    a["L0_wqkv"] = np.concatenate([g["L0_attn_Wq"].T, g["L0_attn_Wk"].T, g["L0_attn_Wv"].T], axis=1)
    a["L0_wfc"] = g["L0_attn_Wfc"].T
    a["L1_wg"] = g["L1_ffn_w_gate"].T
    a["L1_wu"] = g["L1_ffn_w_up"].T
    a["L1_wd"] = g["L1_ffn_w_down"].T.reshape(HC, P, D).transpose(1, 0, 2)
    w = g["L1_attn_w_qkv"]
    half = np.concatenate([np.arange(1, HD, 2), np.arange(0, HD, 2)])
    turned = (np.arange(H)[:, None] * HD + half[None, :]).reshape(-1)
    wq, wk = w[:, 0:D], w[:, D:2 * D]
    a["L1_wqk"] = np.stack([wq, wq[:, turned], wk, wk[:, turned]], axis=1)
    a["L1_wv"] = w[:, 2 * D:3 * D]
    a["L1_wout"] = g["L1_attn_w_out"]
    a["L1_bout"] = g["L1_attn_b_out"]
    a["L2_wq"] = g["L2_attn_Wq"].T
    a["L2_wkv"] = np.concatenate([g["L2_attn_Wk"].T, g["L2_attn_Wv"].T], axis=1)
    a["L2_bq"], a["L2_bk"] = g["L2_attn_bq"].reshape(D, 1), g["L2_attn_bk"].reshape(D, 1)
    a["L2_bk_row"], a["L2_bv_row"] = g["L2_attn_bk"], g["L2_attn_bv"]
    a["gamma"] = g["L2_attn_gamma"].reshape(1)
    a["L3_fr"], a["L3_fk"], a["L3_fv"] = g["L3_ffn_W_r"].T, g["L3_ffn_W_k"].T, g["L3_ffn_W_v"].T
    a["L3_mu_r"], a["L3_mu_k"] = g["L3_ffn_mu_r"].reshape(D, 1), g["L3_ffn_mu_k"].reshape(D, 1)
    for k in ("r", "k", "v", "g", "o"):
        a["L3_" + k] = g["L3_attn_W_" + k]
    a["L3_v_rep"] = np.stack([np.repeat(g["L3_attn_W_v"][:, j::HD], HD, axis=1) for j in range(HD)])
    a["L3_w1"], a["L3_w2"] = g["L3_attn_time_maa_w1"], g["L3_attn_time_maa_w2"]
    a["L3_dw1"], a["L3_dw2"] = g["L3_attn_time_decay_w1"], g["L3_attn_time_decay_w2"]
    a["L3_vecs"] = np.stack([g["L3_attn_" + k].reshape(D) for k in (
        "time_decay", "time_faaaa", "ln_gamma", "ln_beta", "time_maa_x", "time_maa_w", "time_maa_k", "time_maa_v",
        "time_maa_r", "time_maa_g")], axis=1)
    t, head = np.arange(P), np.arange(D) // HD
    exponents = np.concatenate([np.maximum(t[None, :] - t[:, None], 0), np.tile(t + 1, (P, 1)),
                                (P - 1 - t)[:, None], np.full((P, 1), P)], axis=1)
    a["bits"] = np.stack([exponents >> k & 1 for k in range(NEXP)], axis=1).astype(np.float32)
    a["nbits"] = np.stack([1 - (exponents >> k & 1) for k in range(NEXP)], axis=1).astype(np.float32)
    a["causal"] = (t[None, :] >= t[:, None]).astype(np.float32)
    same = (head[:, None] == head[None, :]).astype(np.float32)
    a["L3_blockones"], a["L3_blockmean"] = same, same / np.float32(HD)
    a["L3_center"] = np.eye(D, dtype=np.float32) - same / np.float32(HD)
    a["sel"] = np.stack([same * (np.arange(D) % HD == j) for j in range(HD)], axis=1).astype(np.float32)
    freqs = np.float32(10000.0) ** (-np.arange(0, HD, 2, dtype=np.float32) / np.float32(HD))
    angles = np.arange(S, dtype=np.float32)[:, None] * freqs
    sign = np.where(np.arange(HD) < HD // 2, -1.0, 1.0).astype(np.float32)
    a["cos"] = np.tile(np.repeat(np.cos(angles), 2, axis=1).T, (H, 1))
    a["sin"] = np.tile(np.repeat(np.sin(angles), 2, axis=1).T * sign[:, None], (H, 1))
    f, e = np.divmod(np.arange(HPB * (HD + 1)), HD + 1)
    a["pv_sel"] = (np.arange(P)[:, None] % (HPB * VCOL) == (f * VCOL + e)[None, :]).astype(np.float32)
    a["ident"] = np.eye(P, dtype=np.float32)
    a["rev"] = np.tile(np.arange(E, 0, -1, dtype=np.float32), (P, 1))
    return a


def kernel(**inputs):
    import concourse.bacc as bacc
    from concourse.bass_utils import run_bass_kernel_spmd as run

    nc = bacc.Bacc("TRN2", target_bir_lowering=False, num_devices=1)
    arrays, ins = {}, {}
    for name, a in lay_out(inputs).items():
        arrays[f"in_{name}"] = np.ascontiguousarray(a)
        ins[name] = nc.dram_tensor(f"in_{name}", list(a.shape), mybir.dt.from_np(a.dtype), kind="ExternalInput").ap()
    out = nc.dram_tensor("out_x", (T, D), F32, kind="ExternalOutput").ap()
    build(nc, ins, out)
    r = run(nc, [arrays], core_ids=[0])
    return r.results[0]["out_x"].reshape(B, S, D)
```
